# Optimizing a Trainium2 kernel written in Bass

```python
import numpy as np
import jax
import jax.numpy as jnp

def _softmax(x, axis=-1):
    return jax.nn.softmax(x, axis=axis)

def _gelu(x):
    return jax.nn.gelu(x, approximate=True)

def _silu(x):
    return jax.nn.silu(x)

def _sigmoid(x):
    return jax.nn.sigmoid(x)

def _layernorm(x, axis=-1, eps=1e-05):
    m = jnp.mean(x, axis=axis, keepdims=True)
    v = jnp.var(x, axis=axis, keepdims=True)
    return (x - m) / jnp.sqrt(v + eps)

def _scatter_add(tgt, idx, src, axis=0):
    return tgt.at[idx].add(src)

def _segment_sum(src, seg, n):
    return jax.ops.segment_sum(src, seg, n)
kernel_name = 'mk_decoder_postln_d2_seqx_r8_45901f'

def setup_inputs(seed: int=0):
    np.random.seed(seed)
    _w = jnp.asarray

    def _rec_inputs():
        import jax
        import jax.numpy as jnp
        _rk = jax.random.key(seed)
        x = -0.0002928 + 1 * jax.random.normal(jax.random.fold_in(_rk, 1), (64, 128, 128), jnp.float32)
        _lenS = 128 - jax.random.randint(jax.random.fold_in(_rk, 7), (64,), 0, max(1, 128 // 4) + 1, jnp.int32)
        _lenS2 = 77 - jax.random.randint(jax.random.fold_in(_rk, 8), (64,), 0, max(1, 77 // 4) + 1, jnp.int32)
        _ctx_1024P = jax.random.normal(jax.random.fold_in(_rk, 11), (64, 16, 128), jnp.float32)
        _ctx_1024c = jax.random.dirichlet(jax.random.fold_in(_rk, 511), 0.3 * jnp.ones((16,), jnp.float32), (64, 77))
        _ctx_1024t = jnp.einsum('bsk,bkd->bsd', _ctx_1024c, _ctx_1024P)
        _ctx_1024t = _ctx_1024t * jax.lax.rsqrt(jnp.mean(jnp.square(_ctx_1024t)) + 1e-12) * 0.953939
        ctx_1024 = -1.39393e-06 + 0.999914 * (_ctx_1024t + 0.3 * jax.random.normal(jax.random.fold_in(_rk, 611), (64, 77, 128), jnp.float32))
        fside_BxSxS2_0 = -4.48278e-06 + 1.00019 * jax.random.normal(jax.random.fold_in(_rk, 12), (64, 128, 77), jnp.float32)
        _validS = jnp.arange(128)[None, :] < _lenS[:, None]
        _validS2 = jnp.arange(77)[None, :] < _lenS2[:, None]
        _causal = jnp.tril(jnp.ones((128, 128), dtype=bool))
        mask_BxSxS2_ff0 = jnp.where(jnp.ones((64, 128, 77), dtype=bool), 0.0, -1000000000.0).astype(jnp.float32)
        return (x, ctx_1024, fside_BxSxS2_0, mask_BxSxS2_ff0)
    x, ctx_1024, fside_BxSxS2_0, mask_BxSxS2_ff0 = _rec_inputs()

    def _L0_attn_setup():
        import jax, jax.numpy as jnp
        import numpy as np
        FP32_EPS = 1.1920929e-07

        def rms_norm(x):
            return x * jax.lax.rsqrt(jnp.mean(x * x, axis=-1, keepdims=True) + FP32_EPS)
        key = jax.random.key(seed)
        k1, k2, k3, k4 = jax.random.split(key, 4)
        n_embd, n_qkv = (128, 128)
        B, T = (4, 1024)

        def casted_init(k, out_f, in_f):
            s = 3.0 ** 0.5 * in_f ** (-0.5)
            return jax.random.uniform(k, (out_f, in_f), jnp.float32, -s, s)
        return {'x': jax.random.normal(k1, (B, T, n_embd), jnp.float32), 'w_qkv': casted_init(k2, 3 * n_qkv, n_embd), 'w_swiglu': casted_init(k3, 2 * n_embd, n_qkv), 'w_out': casted_init(k4, n_embd, n_embd)}
    _L0_attn_all = _L0_attn_setup()
    _L0_attn_in = {k: v for k, v in _L0_attn_all.items() if k in ('w_qkv', 'w_swiglu', 'w_out')}
    del _L0_attn_all

    def _L0_xattn_setup():
        import jax, jax.numpy as jnp
        import numpy as np
        HIDDEN = 128
        HEADS = 16
        DK = HIDDEN // HEADS
        B, N = (2, 256)
        key = jax.random.key(seed)
        ks = jax.random.split(key, 12)
        s = 0.02
        return {'q': jax.random.normal(ks[0], (B, N, HIDDEN), jnp.float32), 'k': jax.random.normal(ks[1], (B, N, HIDDEN), jnp.float32), 'v': jax.random.normal(ks[2], (B, N, HIDDEN), jnp.float32), 'attn_bias': jax.random.normal(ks[3], (B, N, N), jnp.float32), 'attention_mask': jnp.zeros((B, N, N), jnp.float32), 'Wq': jax.random.normal(ks[4], (HIDDEN, HIDDEN), jnp.float32) * s, 'bq': jnp.zeros((HIDDEN,), jnp.float32), 'Wk': jax.random.normal(ks[5], (HIDDEN, HIDDEN), jnp.float32) * s, 'bk': jnp.zeros((HIDDEN,), jnp.float32), 'Wv': jax.random.normal(ks[6], (HIDDEN, HIDDEN), jnp.float32) * s, 'bv': jnp.zeros((HIDDEN,), jnp.float32), 'Wo': jax.random.normal(ks[7], (HIDDEN, HIDDEN), jnp.float32) * s, 'bo': jnp.zeros((HIDDEN,), jnp.float32)}
    _L0_xattn_all = _L0_xattn_setup()
    _L0_xattn_in = {k: v for k, v in _L0_xattn_all.items() if k in ('Wq', 'bq', 'Wk', 'bk', 'Wv', 'bv', 'Wo', 'bo')}
    del _L0_xattn_all

    def _L0_ffn_setup():
        import jax, jax.numpy as jnp
        import numpy as np
        B, S, DIM = (2, 256, 128)
        HID = 256
        E, NSH, TOPK = (8, 2, 2)

        def _ffn(x, w1, w2, w3):
            return jax.nn.silu(x @ w1.T) * (x @ w3.T) @ w2.T
        key = jax.random.key(seed)
        ks = jax.random.split(key, 8)
        sc = 0.02
        return {'x': jax.random.normal(ks[0], (B, S, DIM), jnp.float32), 'router_w': jax.random.normal(ks[1], (E, DIM), jnp.float32) * sc, 'expert_bias': jnp.zeros((E,), jnp.float32), 'w1': jax.random.normal(ks[2], (E, HID, DIM), jnp.float32) * sc, 'w3': jax.random.normal(ks[3], (E, HID, DIM), jnp.float32) * sc, 'w2': jax.random.normal(ks[4], (E, DIM, HID), jnp.float32) * sc, 'sw1': jax.random.normal(ks[5], (NSH, HID, DIM), jnp.float32) * sc, 'sw3': jax.random.normal(ks[6], (NSH, HID, DIM), jnp.float32) * sc, 'sw2': jax.random.normal(ks[7], (NSH, DIM, HID), jnp.float32) * sc}
    _L0_ffn_all = _L0_ffn_setup()
    _L0_ffn_in = {k: v for k, v in _L0_ffn_all.items() if k in ('router_w', 'expert_bias', 'w1', 'w3', 'w2', 'sw1', 'sw3', 'sw2')}
    del _L0_ffn_all

    def _L1_attn_setup():
        import jax, jax.numpy as jnp
        import numpy as np
        B, L, H = (2, 256, 128)
        E = H * 2
        K = 4
        N = 16
        DT_RANK = H // 8

        def _selective_scan(u, delta, A, Bm, Cm, Dp):

            def step(h, inp):
                d_t, u_t, b_t, c_t = inp
                dA = jnp.exp(d_t[..., None] * A)
                h = dA * h + (d_t * u_t)[..., None] * b_t[:, None, :]
                y = jnp.einsum('ben,bn->be', h, c_t)
                return (h, y)
            h0 = jnp.zeros((u.shape[0], A.shape[0], A.shape[1]), u.dtype)
            xs = (delta.transpose(1, 0, 2), u.transpose(1, 0, 2), Bm.transpose(1, 0, 2), Cm.transpose(1, 0, 2))
            _, ys = jax.lax.scan(step, h0, xs)
            return ys.transpose(1, 0, 2) + u * Dp
        key = jax.random.key(seed)
        ks = jax.random.split(key, 12)
        s = lambda fan_in: 1.0 / np.sqrt(fan_in)
        return {'x': jax.random.normal(ks[0], (B, L, H), jnp.float32), 'W_in': jax.random.normal(ks[1], (H, 2 * E), jnp.float32) * s(H), 'b_in': jnp.zeros((2 * E,), jnp.float32), 'conv_w': jax.random.normal(ks[2], (E, 1, K), jnp.float32) * s(K), 'conv_b': jnp.zeros((E,), jnp.float32), 'x_proj_w': jax.random.normal(ks[3], (E, DT_RANK + 2 * N), jnp.float32) * s(E), 'dt_proj_w': jax.random.normal(ks[4], (DT_RANK, E), jnp.float32) * s(DT_RANK), 'dt_bias': jax.random.uniform(ks[5], (E,), jnp.float32, -4.0, -2.0), 'A_log': jnp.log(jnp.broadcast_to(jnp.arange(1, N + 1, dtype=jnp.float32), (E, N))), 'D_param': jnp.ones((E,), jnp.float32), 'W_out': jax.random.normal(ks[6], (E, H), jnp.float32) * s(E), 'b_out': jnp.zeros((H,), jnp.float32)}
    _L1_attn_all = _L1_attn_setup()
    _L1_attn_in = {k: v for k, v in _L1_attn_all.items() if k in ('W_in', 'b_in', 'conv_w', 'conv_b', 'x_proj_w', 'dt_proj_w', 'dt_bias', 'A_log', 'D_param', 'W_out', 'b_out')}
    del _L1_attn_all

    def _L1_xattn_setup():
        import jax, jax.numpy as jnp
        import numpy as np
        N_HEAD, MODEL_DIM, KEY_DIM, VALUE_DIM = (16, 128, 64, 64)
        B, S = (4, 256)
        EPS = 1e-05
        TEMP = float(np.sqrt(KEY_DIM))
        key = jax.random.key(seed)
        ks = jax.random.split(key, 12)
        d = {'query': jax.random.normal(ks[0], (B, S, MODEL_DIM), jnp.float32), 'key': jax.random.normal(ks[1], (B, S, MODEL_DIM), jnp.float32), 'value': jax.random.normal(ks[2], (B, S, MODEL_DIM), jnp.float32), 'Wq': jax.random.normal(ks[3], (MODEL_DIM, N_HEAD * KEY_DIM), jnp.float32) * np.sqrt(2.0 / (MODEL_DIM + KEY_DIM)), 'bq': jnp.zeros((N_HEAD * KEY_DIM,), jnp.float32), 'Wk': jax.random.normal(ks[4], (MODEL_DIM, N_HEAD * KEY_DIM), jnp.float32) * np.sqrt(2.0 / (MODEL_DIM + KEY_DIM)), 'bk': jnp.zeros((N_HEAD * KEY_DIM,), jnp.float32), 'Wv': jax.random.normal(ks[5], (MODEL_DIM, N_HEAD * VALUE_DIM), jnp.float32) * np.sqrt(2.0 / (MODEL_DIM + VALUE_DIM)), 'bv': jnp.zeros((N_HEAD * VALUE_DIM,), jnp.float32), 'Wo': jax.random.normal(ks[6], (N_HEAD * VALUE_DIM, MODEL_DIM), jnp.float32) * np.sqrt(2.0 / (N_HEAD * VALUE_DIM + MODEL_DIM)), 'bo': jnp.zeros((MODEL_DIM,), jnp.float32), 'ln_gamma': jnp.ones((MODEL_DIM,), jnp.float32), 'ln_beta': jnp.zeros((MODEL_DIM,), jnp.float32)}
        return d
    _L1_xattn_all = _L1_xattn_setup()
    _L1_xattn_in = {k: v for k, v in _L1_xattn_all.items() if k in ('Wq', 'bq', 'Wk', 'bk', 'Wv', 'bv', 'Wo', 'bo', 'ln_gamma', 'ln_beta')}
    del _L1_xattn_all

    def _L1_ffn_setup():
        import jax, jax.numpy as jnp
        import numpy as np
        HIDDEN = 128
        INNER = 512

        def _weight_quant(w):
            scale = 1.0 / jnp.clip(jnp.mean(jnp.abs(w)), 1e-05)
            wq = jnp.clip(jnp.round(w * scale), -1.0, 1.0) / scale
            return w + jax.lax.stop_gradient(wq - w)

        def _act_quant(x):
            scale = 127.0 / jnp.clip(jnp.max(jnp.abs(x), axis=-1, keepdims=True), 1e-05)
            xq = jnp.clip(jnp.round(x * scale), -128.0, 127.0) / scale
            return x + jax.lax.stop_gradient(xq - x)

        def _bitlinear(x, w):
            return jnp.einsum('bsi,oi->bso', _act_quant(x), _weight_quant(w))
        key = jax.random.key(seed)
        k0, k1, k2, k3 = jax.random.split(key, 4)
        x = jax.random.normal(k0, (4, 256, HIDDEN), dtype=jnp.float32)
        w_gate = jax.random.normal(k1, (INNER, HIDDEN), dtype=jnp.float32) / np.sqrt(HIDDEN)
        w_up = jax.random.normal(k2, (INNER, HIDDEN), dtype=jnp.float32) / np.sqrt(HIDDEN)
        w_down = jax.random.normal(k3, (HIDDEN, INNER), dtype=jnp.float32) / np.sqrt(INNER)
        return {'x': x, 'w_gate': w_gate, 'w_up': w_up, 'w_down': w_down}
    _L1_ffn_all = _L1_ffn_setup()
    _L1_ffn_in = {k: v for k, v in _L1_ffn_all.items() if k in ('w_gate', 'w_up', 'w_down')}
    del _L1_ffn_all
    return {'x': x, 'ctx_1024': ctx_1024, 'fside_BxSxS2_0': fside_BxSxS2_0, 'mask_BxSxS2_ff0': mask_BxSxS2_ff0, 'L0_attn_w_qkv': _L0_attn_in['w_qkv'], 'L0_attn_w_swiglu': _L0_attn_in['w_swiglu'], 'L0_attn_w_out': _L0_attn_in['w_out'], 'L0_xattn_Wq': _L0_xattn_in['Wq'], 'L0_xattn_bq': _L0_xattn_in['bq'], 'L0_xattn_Wk': _L0_xattn_in['Wk'], 'L0_xattn_bk': _L0_xattn_in['bk'], 'L0_xattn_Wv': _L0_xattn_in['Wv'], 'L0_xattn_bv': _L0_xattn_in['bv'], 'L0_xattn_Wo': _L0_xattn_in['Wo'], 'L0_xattn_bo': _L0_xattn_in['bo'], 'L0_ffn_router_w': _L0_ffn_in['router_w'], 'L0_ffn_expert_bias': _L0_ffn_in['expert_bias'], 'L0_ffn_w1': _L0_ffn_in['w1'], 'L0_ffn_w3': _L0_ffn_in['w3'], 'L0_ffn_w2': _L0_ffn_in['w2'], 'L0_ffn_sw1': _L0_ffn_in['sw1'], 'L0_ffn_sw3': _L0_ffn_in['sw3'], 'L0_ffn_sw2': _L0_ffn_in['sw2'], 'L1_attn_W_in': _L1_attn_in['W_in'], 'L1_attn_b_in': _L1_attn_in['b_in'], 'L1_attn_conv_w': _L1_attn_in['conv_w'], 'L1_attn_conv_b': _L1_attn_in['conv_b'], 'L1_attn_x_proj_w': _L1_attn_in['x_proj_w'], 'L1_attn_dt_proj_w': _L1_attn_in['dt_proj_w'], 'L1_attn_dt_bias': _L1_attn_in['dt_bias'], 'L1_attn_A_log': _L1_attn_in['A_log'], 'L1_attn_D_param': _L1_attn_in['D_param'], 'L1_attn_W_out': _L1_attn_in['W_out'], 'L1_attn_b_out': _L1_attn_in['b_out'], 'L1_xattn_Wq': _L1_xattn_in['Wq'], 'L1_xattn_bq': _L1_xattn_in['bq'], 'L1_xattn_Wk': _L1_xattn_in['Wk'], 'L1_xattn_bk': _L1_xattn_in['bk'], 'L1_xattn_Wv': _L1_xattn_in['Wv'], 'L1_xattn_bv': _L1_xattn_in['bv'], 'L1_xattn_Wo': _L1_xattn_in['Wo'], 'L1_xattn_bo': _L1_xattn_in['bo'], 'L1_xattn_ln_gamma': _L1_xattn_in['ln_gamma'], 'L1_xattn_ln_beta': _L1_xattn_in['ln_beta'], 'L1_ffn_w_gate': _L1_ffn_in['w_gate'], 'L1_ffn_w_up': _L1_ffn_in['w_up'], 'L1_ffn_w_down': _L1_ffn_in['w_down']}

def reference(x, ctx_1024, fside_BxSxS2_0, mask_BxSxS2_ff0, L0_attn_w_qkv, L0_attn_w_swiglu, L0_attn_w_out, L0_xattn_Wq, L0_xattn_bq, L0_xattn_Wk, L0_xattn_bk, L0_xattn_Wv, L0_xattn_bv, L0_xattn_Wo, L0_xattn_bo, L0_ffn_router_w, L0_ffn_expert_bias, L0_ffn_w1, L0_ffn_w3, L0_ffn_w2, L0_ffn_sw1, L0_ffn_sw3, L0_ffn_sw2, L1_attn_W_in, L1_attn_b_in, L1_attn_conv_w, L1_attn_conv_b, L1_attn_x_proj_w, L1_attn_dt_proj_w, L1_attn_dt_bias, L1_attn_A_log, L1_attn_D_param, L1_attn_W_out, L1_attn_b_out, L1_xattn_Wq, L1_xattn_bq, L1_xattn_Wk, L1_xattn_bk, L1_xattn_Wv, L1_xattn_bv, L1_xattn_Wo, L1_xattn_bo, L1_xattn_ln_gamma, L1_xattn_ln_beta, L1_ffn_w_gate, L1_ffn_w_up, L1_ffn_w_down):
    import jax
    import jax.numpy as jnp

    def _L0_attn_ref(x, w_qkv, w_swiglu, w_out):
        import jax, jax.numpy as jnp
        import numpy as np
        FP32_EPS = 1.1920929e-07

        def rms_norm(x):
            return x * jax.lax.rsqrt(jnp.mean(x * x, axis=-1, keepdims=True) + FP32_EPS)
        qkv = jnp.einsum('btd,ed->bte', rms_norm(x), w_qkv)
        q, k, v = jnp.split(qkv, 3, axis=-1)
        q = rms_norm(q)
        k = rms_norm(k)
        w = jnp.exp(k)
        kv = w * v
        w = jnp.cumsum(w, axis=1)
        kv = jnp.cumsum(kv, axis=1)
        y = kv / (w + 1e-06)
        y = jax.nn.sigmoid(q) * y
        uv = jnp.einsum('bte,fe->btf', y, w_swiglu)
        u, g = jnp.split(uv, 2, axis=-1)
        return x + jnp.einsum('btd,ed->bte', u * jax.nn.silu(g), w_out)

    def _L0_xattn_ref(q, k, v, attn_bias, attention_mask, Wq, bq, Wk, bk, Wv, bv, Wo, bo):
        import jax, jax.numpy as jnp
        import numpy as np
        HIDDEN = 128
        HEADS = 16
        DK = HIDDEN // HEADS
        B, N = (2, 256)
        b, n, _ = q.shape
        scale = DK ** (-0.5)
        qh = (q @ Wq + bq).reshape(b, n, HEADS, DK).transpose(0, 2, 1, 3)
        kh = (k @ Wk + bk).reshape(b, -1, HEADS, DK).transpose(0, 2, 1, 3)
        vh = (v @ Wv + bv).reshape(b, -1, HEADS, DK).transpose(0, 2, 1, 3)
        scores = jnp.einsum('bhnd,bhmd->bhnm', qh * scale, kh)
        scores = scores + attn_bias[:, None, :, :] + attention_mask[:, None, :, :]
        probs = jax.nn.softmax(scores, axis=-1)
        ctx = jnp.einsum('bhnm,bhmd->bhnd', probs, vh)
        ctx = ctx.transpose(0, 2, 1, 3).reshape(b, n, HEADS * DK)
        return ctx @ Wo + bo

    def _L0_ffn_ref(x, router_w, expert_bias, w1, w3, w2, sw1, sw3, sw2):
        import jax, jax.numpy as jnp
        import numpy as np
        B, S, DIM = (2, 256, 128)
        HID = 256
        E, NSH, TOPK = (8, 2, 2)

        def _ffn(x, w1, w2, w3):
            return jax.nn.silu(x @ w1.T) * (x @ w3.T) @ w2.T
        bs, sl, d = x.shape
        xf = x.reshape(-1, d)
        shared = jnp.zeros_like(xf)
        for i in range(sw1.shape[0]):
            shared = shared + _ffn(xf, sw1[i], sw2[i], sw3[i])
        logits = xf @ router_w.T + expert_bias
        rw, sel = jax.lax.top_k(logits, TOPK)
        rw = jax.nn.softmax(rw.astype(jnp.float32), axis=-1).astype(x.dtype)
        onehot = jax.nn.one_hot(sel, E, dtype=x.dtype)
        combine = jnp.einsum('tk,tke->te', rw, onehot)

        def body(acc, ew):
            e1, e3, e2, cw = ew
            acc = acc + cw[:, None] * _ffn(xf, e1, e2, e3)
            return (acc, None)
        out, _ = jax.lax.scan(body, jnp.zeros_like(xf), (w1, w3, w2, combine.T))
        out = out + shared
        return out.reshape(bs, sl, -1)

    def _L1_attn_ref(x, W_in, b_in, conv_w, conv_b, x_proj_w, dt_proj_w, dt_bias, A_log, D_param, W_out, b_out):
        import jax, jax.numpy as jnp
        import numpy as np
        B, L, H = (2, 256, 128)
        E = H * 2
        K = 4
        N = 16
        DT_RANK = H // 8

        def _selective_scan(u, delta, A, Bm, Cm, Dp):

            def step(h, inp):
                d_t, u_t, b_t, c_t = inp
                dA = jnp.exp(d_t[..., None] * A)
                h = dA * h + (d_t * u_t)[..., None] * b_t[:, None, :]
                y = jnp.einsum('ben,bn->be', h, c_t)
                return (h, y)
            h0 = jnp.zeros((u.shape[0], A.shape[0], A.shape[1]), u.dtype)
            xs = (delta.transpose(1, 0, 2), u.transpose(1, 0, 2), Bm.transpose(1, 0, 2), Cm.transpose(1, 0, 2))
            _, ys = jax.lax.scan(step, h0, xs)
            return ys.transpose(1, 0, 2) + u * Dp
        silu = jax.nn.silu
        z = x @ W_in + b_in
        xc, xr = (z[..., :E], z[..., E:])
        xr = silu(xr)
        xt = xc.transpose(0, 2, 1)
        xt = jax.lax.conv_general_dilated(xt, conv_w, window_strides=(1,), padding=[(K - 1, 0)], feature_group_count=E, dimension_numbers=('NCH', 'OIH', 'NCH'))
        xc = silu((xt + conv_b[None, :, None]).transpose(0, 2, 1))
        proj = xc @ x_proj_w
        dt = proj[..., :DT_RANK]
        Bm = proj[..., DT_RANK:DT_RANK + N]
        Cm = proj[..., DT_RANK + N:]
        delta = jax.nn.softplus(dt @ dt_proj_w + dt_bias)
        A = -jnp.exp(A_log)
        y = _selective_scan(xc, delta, A, Bm, Cm, D_param)
        y = y * xr
        return y @ W_out + b_out

    def _L1_xattn_ref(query, key, value, Wq, bq, Wk, bk, Wv, bv, Wo, bo, ln_gamma, ln_beta):
        import jax, jax.numpy as jnp
        import numpy as np
        N_HEAD, MODEL_DIM, KEY_DIM, VALUE_DIM = (16, 128, 64, 64)
        B, S = (4, 256)
        EPS = 1e-05
        TEMP = float(np.sqrt(KEY_DIM))
        b, sq, _ = query.shape
        residual = query
        q = (query @ Wq + bq).reshape(b, sq, N_HEAD, KEY_DIM)
        k = (key @ Wk + bk).reshape(b, key.shape[1], N_HEAD, KEY_DIM)
        v = (value @ Wv + bv).reshape(b, value.shape[1], N_HEAD, VALUE_DIM)
        scores = jnp.einsum('bqhd,bkhd->bhqk', q, k) / TEMP
        attn = jax.nn.softmax(scores, axis=-1)
        out = jnp.einsum('bhqk,bkhd->bqhd', attn, v).reshape(b, sq, N_HEAD * VALUE_DIM)
        out = out @ Wo + bo + residual
        mu = jnp.mean(out, axis=-1, keepdims=True)
        var = jnp.var(out, axis=-1, keepdims=True)
        return (out - mu) * jax.lax.rsqrt(var + EPS) * ln_gamma + ln_beta

    def _L1_ffn_ref(x, w_gate, w_up, w_down):
        import jax, jax.numpy as jnp
        import numpy as np
        HIDDEN = 128
        INNER = 512

        def _weight_quant(w):
            scale = 1.0 / jnp.clip(jnp.mean(jnp.abs(w)), 1e-05)
            wq = jnp.clip(jnp.round(w * scale), -1.0, 1.0) / scale
            return w + jax.lax.stop_gradient(wq - w)

        def _act_quant(x):
            scale = 127.0 / jnp.clip(jnp.max(jnp.abs(x), axis=-1, keepdims=True), 1e-05)
            xq = jnp.clip(jnp.round(x * scale), -128.0, 127.0) / scale
            return x + jax.lax.stop_gradient(xq - x)

        def _bitlinear(x, w):
            return jnp.einsum('bsi,oi->bso', _act_quant(x), _weight_quant(w))
        gate = jax.nn.silu(_bitlinear(x, w_gate))
        up = _bitlinear(x, w_up)
        return _bitlinear(gate * up, w_down)
    x = _layernorm(x + _L0_attn_ref(x, L0_attn_w_qkv, L0_attn_w_swiglu, L0_attn_w_out), axis=-1)
    x = _layernorm(x + _L0_xattn_ref(x, ctx_1024, ctx_1024, fside_BxSxS2_0, mask_BxSxS2_ff0, L0_xattn_Wq, L0_xattn_bq, L0_xattn_Wk, L0_xattn_bk, L0_xattn_Wv, L0_xattn_bv, L0_xattn_Wo, L0_xattn_bo), axis=-1)
    x = _layernorm(x + _L0_ffn_ref(x, L0_ffn_router_w, L0_ffn_expert_bias, L0_ffn_w1, L0_ffn_w3, L0_ffn_w2, L0_ffn_sw1, L0_ffn_sw3, L0_ffn_sw2), axis=-1)
    x = _layernorm(x + _L1_attn_ref(x, L1_attn_W_in, L1_attn_b_in, L1_attn_conv_w, L1_attn_conv_b, L1_attn_x_proj_w, L1_attn_dt_proj_w, L1_attn_dt_bias, L1_attn_A_log, L1_attn_D_param, L1_attn_W_out, L1_attn_b_out), axis=-1)
    x = _layernorm(x + _L1_xattn_ref(x, ctx_1024, ctx_1024, L1_xattn_Wq, L1_xattn_bq, L1_xattn_Wk, L1_xattn_bk, L1_xattn_Wv, L1_xattn_bv, L1_xattn_Wo, L1_xattn_bo, L1_xattn_ln_gamma, L1_xattn_ln_beta), axis=-1)
    x = _layernorm(x + _L1_ffn_ref(x, L1_ffn_w_gate, L1_ffn_w_up, L1_ffn_w_down), axis=-1)
    return x

_drawn_inputs = setup_inputs


def setup_inputs(seed=0):
    import zlib

    import numpy as np

    out = dict(_drawn_inputs(seed))
    spreads = {'L0_xattn_bq': (0.0, 0.8),
     'L0_xattn_bk': (0.0, 0.8),
     'L0_xattn_bv': (0.0, 0.365),
     'L0_xattn_bo': (0.0, 0.1),
     'L0_ffn_expert_bias': (0.0, 0.8),
     'L1_attn_b_in': (0.0, 0.1),
     'L1_attn_conv_b': (0.0, 0.1),
     'L1_attn_D_param': (1.0, 0.2),
     'L1_attn_b_out': (0.0, 0.1),
     'L1_xattn_bq': (0.0, 0.412),
     'L1_xattn_bk': (0.0, 0.8),
     'L1_xattn_bv': (0.0, 0.1),
     'L1_xattn_bo': (0.0, 0.1),
     'L1_xattn_ln_gamma': (1.0, 0.2),
     'L1_xattn_ln_beta': (0.0, 0.1)}
    factors = {'fside_BxSxS2_0': 8.0,
     'L0_attn_w_qkv': 4.362,
     'L0_attn_w_swiglu': 4.216,
     'L0_attn_w_out': 4.181,
     'L0_xattn_Wq': 8.0,
     'L0_xattn_Wk': 8.0,
     'L0_ffn_router_w': 8.0,
     'L0_ffn_w1': 8.0,
     'L0_ffn_w3': 8.0,
     'L0_ffn_w2': 8.0,
     'L0_ffn_sw1': 4.577,
     'L0_ffn_sw3': 4.547,
     'L0_ffn_sw2': 4.561}
    for name, (base, spread) in spreads.items():
        noise = np.random.default_rng([zlib.crc32(name.encode()), seed]).standard_normal(out[name].shape)
        drawn = base * np.exp(spread * noise) if base else spread * noise
        out[name] = jnp.asarray(drawn.astype(out[name].dtype))
    for name, factor in factors.items():
        out[name] = (out[name] * factor).astype(out[name].dtype)
    return out
```

```python
from contextlib import ExitStack

import numpy as np

import concourse.bass as bass
from concourse import mybir

F32 = mybir.dt.float32
BF16 = mybir.dt.bfloat16
ALU = mybir.AluOpType
ACT = mybir.ActivationFunctionType
AX = mybir.AxisListType
ds = bass.ds

B, T, D = 64, 128, 128
S2 = 77
GB = 4
NG = B // GB
GT = GB * T
LN_EPS = 1e-5
RMS_EPS = 1.1920929e-07
LAST_PHASE = 6


class Signal:

    def __init__(self, sem, per_pass=1):
        self.sem = sem
        self.per_pass = per_pass

    def at(self, done, k):
        return done * self.per_pass + k + 1


def behind(i, n):
    return not isinstance(i, int) or i >= n


def open_signals(nc, signals, landed):
    with nc.Block() as block:

        @block.sync
        def _(sp):
            for weights in landed:
                sp.wait_ge(weights.sem, weights.value)
            for signal in signals:
                sp.sem_inc(signal.sem, 1)


class Core:

    def __init__(self, nc, ctx, ins, out):
        self.nc, self.ctx, self.ins, self.out = nc, ctx, ins, out

    def sb(self, name, shape, dt=F32):
        return self.ctx.enter_context(self.nc.sbuf_tensor(name, shape, dt))


def setup(core):
    nc = core.nc
    with nc.Block() as block:

        @block.sync
        def _(sp):
            for phase in "a":
                for name in WEIGHTS[phase]:
                    sp.dma_start(core.w[name][:], core.ins[name]).then_inc(core.landed[phase].sem, 16)

        @block.scalar
        def _(act):
            for phase in "sbmcq":
                for name in WEIGHTS[phase]:
                    act.dma_start(core.w[name][:], core.ins[name]).then_inc(core.landed[phase].sem, 16)

        @block.gpsimd
        def _(pool):
            nc.gpsimd.memset(core.minus_half[:, :], -0.5)
            nc.gpsimd.memset(core.euler[:, :], float(np.e))
            nc.gpsimd.memset(core.ln_eps[:, :], LN_EPS)
            nc.gpsimd.memset(core.rms_eps[:, 0:GB], 4 * RMS_EPS)
            nc.gpsimd.memset(core.rms_eps[:, GB:2 * GB], RMS_EPS)


def finish_statistics(core, name):
    nc = core.nc
    half_n = D // 2
    with nc.sbuf_tensor(f"{name}_gap", [128, B], F32) as gap, nc.semaphore(f"{name}_folded") as folded, \
            nc.semaphore(f"{name}_rstd") as rstd_ready, nc.Block() as block:
        mean_even, spread_even = core.stats[:, :, 1], core.stats[:, :, 2]
        mean_odd, spread_odd = core.stats[:, :, 4], core.stats[:, :, 5]

        @block.vector
        def _(dve):
            nc.vector.tensor_tensor(gap[:, :], mean_even, mean_odd, ALU.subtract)
            nc.vector.tensor_tensor(core.mean[:, :], mean_even, mean_odd, ALU.add)
            nc.vector.tensor_tensor(core.rstd[:, :], spread_even, spread_odd, ALU.add).then_inc(folded, 1)
            dve.wait_ge(folded, 1)
            nc.vector.tensor_scalar(core.mean[:, :], core.mean[:, :], 0.5, None, ALU.mult)
            nc.vector.scalar_tensor_tensor(gap[:, :], gap[:, :], half_n / 2.0, gap[:, :],
                                           ALU.mult, ALU.mult).then_inc(folded, 1)
            dve.wait_ge(folded, 2)
            nc.vector.tensor_tensor(core.rstd[:, :], core.rstd[:, :], gap[:, :], ALU.add).then_inc(folded, 1)
            dve.wait_ge(folded, 3)
            nc.vector.tensor_scalar(core.rstd[:, :], core.rstd[:, :], 1.0 / D, LN_EPS,
                                    ALU.mult, ALU.add).then_inc(folded, 1)

        @block.gpsimd
        def _(pool):
            pool.wait_ge(folded, 4)
            nc.gpsimd.tensor_tensor(core.rstd[:, :], core.rstd[:, :], core.minus_half[:, 0:B],
                                    ALU.pow).then_inc(rstd_ready, 1)
            pool.wait_ge(rstd_ready, 1)


def leave(dve, nc, core, g, steps, total, stats):
    dve.wait_ge(steps.sem, steps.at(g, 1))
    for j in range(GB):
        last = nc.vector.bn_stats(stats[:, j, :], total[:, j, :])
    last.then_inc(steps.sem, 1)
    nc.vector.tensor_copy(core.x[:, ds(g * GB, GB), :], total[:, :, :])
    dve.wait_ge(steps.sem, steps.at(g, 2))
    nc.vector.tensor_copy(core.stats[:, ds(g * GB, GB), :], stats[:, :, :]).then_inc(steps.sem, 1)


def leave_one(dve, nc, core, i, steps, total, stats):
    dve.wait_ge(steps.sem, steps.at(i, 1))
    nc.vector.bn_stats(stats, total).then_inc(steps.sem, 1)
    nc.vector.tensor_copy(core.x[:, i, :], total)
    dve.wait_ge(steps.sem, steps.at(i, 2))
    nc.vector.tensor_copy(core.stats[:, i, :], stats).then_inc(steps.sem, 1)


def phase_aft(core):
    nc = core.nc
    x = core.x
    with ExitStack() as ctx:
        def sb(name, shape, dt=F32):
            return ctx.enter_context(nc.sbuf_tensor(name, shape, dt))

        def ps(name, shape, dt=F32):
            return ctx.enter_context(nc.psum_tensor(name, shape, dt))

        signals = []

        def sig(name, per_pass=1):
            signals.append(Signal(ctx.enter_context(nc.semaphore(name)), per_pass))
            return signals[-1]

        square = sb("a_square", [128, 3, GB, 128])
        x_ms = sb("a_x_ms", [128, GB])
        qk_ms = sb("a_qk_ms", [128, 2, GB])
        xn = sb("a_xn", [128, GB, 128])
        xnT = sb("a_xnT", [128, GT])
        th_q = sb("a_th_q", [128, GB, 128])
        w_kv = sb("a_w_kv", [128, 2, GB, 128])
        den = sb("a_den", [128, GT])
        gate = sb("a_gate", [128, GT])
        y = sb("a_y", [128, GT])
        yT = sb("a_yT", [128, GT])
        th_g = sb("a_th_g", [128, GT])
        h = sb("a_h", [128, GT])
        total = sb("a_total", [128, GB, 128])
        stats = sb("a_stats", [128, GB, 6])

        turn_ps = ps("a_turn_ps", [128, GT])
        q_ps = ps("a_q_ps", [128, GB, 128])
        k_ps = ps("a_k_ps", [128, GB, 128])
        v_ps = ps("a_v_ps", [128, GB, 128])
        wsum_ps = ps("a_wsum_ps", [128, GT])
        kvsum_ps = ps("a_kvsum_ps", [128, GT])
        u_ps = ps("a_u_ps", [128, GT])
        g_ps = ps("a_g_ps", [128, GT])
        o_ps = q_ps

        x_in = sig("a_x_in", 16)
        x_squared = sig("a_x_squared")
        x_eps = sig("a_x_eps")
        x_rms = sig("a_x_rms")
        x_normed = sig("a_x_normed")
        x_turned = sig("a_x_turned")
        xnT_ready = sig("a_xnT_ready")
        qkv_ready = sig("a_qkv_ready")
        qk_squared = sig("a_qk_squared")
        qk_eps = sig("a_qk_eps")
        qk_rms = sig("a_qk_rms")
        w_ready = sig("a_w_ready")
        th_q_ready = sig("a_th_q_ready")
        kv_ready = sig("a_kv_ready")
        sums_ready = sig("a_sums_ready")
        y_steps = sig("a_y_steps", 4)
        y_turned = sig("a_y_turned")
        yT_ready = sig("a_yT_ready")
        ug_ready = sig("a_ug_ready")
        th_g_ready = sig("a_th_g_ready")
        h_steps = sig("a_h_steps", 2)
        o_ready = sig("a_o_ready")
        x_steps = sig("a_x_steps", 3)

        open_signals(nc, signals, [core.landed["a"], core.landed["s"]])
        block = ctx.enter_context(nc.Block())

        @block.sync
        def _(sp):
            with sp.Fori(0, NG) as g:
                sp.wait_ge(x_in.sem, x_in.at(g, 0))
                sp.dma_start(x[:, ds(g * GB, GB), :],
                             core.ins["x"][ds(g * GB, GB), :, :].rearrange("b t d -> t b d")
                             ).then_inc(x_in.sem, 16)

        @block.gpsimd
        def _(pool):
            with pool.Fori(0, NG) as g:
                pool.wait_ge(x_squared.sem, x_squared.at(g, 1))
                nc.gpsimd.tensor_tensor(x_ms[:, :], x_ms[:, :], core.rms_eps[:, GB:2 * GB],
                                        ALU.add).then_inc(x_eps.sem, 1)
                pool.wait_ge(x_eps.sem, x_eps.at(g, 1))
                nc.gpsimd.tensor_tensor(x_ms[:, :], x_ms[:, :], core.minus_half[:, 0:GB],
                                        ALU.pow).then_inc(x_rms.sem, 1)
                pool.wait_ge(qk_squared.sem, qk_squared.at(g, 1))
                nc.gpsimd.tensor_tensor(qk_ms[:, :, :].rearrange("p a b -> p (a b)"),
                                        qk_ms[:, :, :].rearrange("p a b -> p (a b)"),
                                        core.rms_eps[:, :], ALU.add).then_inc(qk_eps.sem, 1)
                pool.wait_ge(qk_eps.sem, qk_eps.at(g, 1))
                nc.gpsimd.tensor_tensor(qk_ms[:, :, :].rearrange("p a b -> p (a b)"),
                                        qk_ms[:, :, :].rearrange("p a b -> p (a b)"),
                                        core.minus_half[:, 0:2 * GB], ALU.pow).then_inc(qk_rms.sem, 1)

        @block.scalar
        def _(act):
            with act.Fori(0, NG) as g:
                act.wait_ge(x_in.sem, x_in.at(g, 16))
                act.wait_ge(x_normed.sem, x_normed.at(g, 0))
                act.wait_ge(qk_squared.sem, qk_squared.at(g, 0))
                for j in range(GB):
                    last = nc.scalar.activation(square[:, 0, j, :], x[:, g * GB + j, :], ACT.Square,
                                                scale=D ** -0.5, accum_out=x_ms[:, j:j + 1])
                last.then_inc(x_squared.sem, 1)
                act.wait_ge(x_turned.sem, x_turned.at(g, 1))
                act.wait_ge(qkv_ready.sem, qkv_ready.at(g, 0))
                nc.scalar.activation(xnT[:, :], turn_ps[:, :], ACT.Copy).then_inc(xnT_ready.sem, 1)
                act.wait_ge(qkv_ready.sem, qkv_ready.at(g, 1))
                for j in range(GB):
                    nc.scalar.activation(square[:, 1, j, :], q_ps[:, j, :], ACT.Square,
                                         scale=2 * D ** -0.5, accum_out=qk_ms[:, 0, j:j + 1])
                for j in range(GB):
                    last = nc.scalar.activation(square[:, 2, j, :], k_ps[:, j, :], ACT.Square,
                                                scale=D ** -0.5, accum_out=qk_ms[:, 1, j:j + 1])
                last.then_inc(qk_squared.sem, 1)
                act.wait_ge(qk_rms.sem, qk_rms.at(g, 1))
                act.wait_ge(sums_ready.sem, sums_ready.at(g, 0))
                for j in range(GB):
                    last = nc.scalar.activation(w_kv[:, 0, j, :], k_ps[:, j, :], ACT.Exp,
                                                scale=qk_ms[:, 1, j:j + 1])
                last.then_inc(w_ready.sem, 1)
                for j in range(GB):
                    last = nc.scalar.activation(th_q[:, j, :], q_ps[:, j, :], ACT.Tanh,
                                                scale=qk_ms[:, 0, j:j + 1])
                last.then_inc(th_q_ready.sem, 1)
                act.wait_ge(y_turned.sem, y_turned.at(g, 1))
                nc.scalar.activation(yT[:, :], turn_ps[:, :], ACT.Copy).then_inc(yT_ready.sem, 1)
                act.wait_ge(ug_ready.sem, ug_ready.at(g, 1))
                nc.scalar.activation(th_g[:, :], g_ps[:, :], ACT.Tanh, scale=0.5).then_inc(th_g_ready.sem, 1)

        @block.vector
        def _(dve):
            with dve.Fori(0, NG) as g:
                dve.wait_ge(x_rms.sem, x_rms.at(g, 1))
                dve.wait_ge(x_turned.sem, x_turned.at(g, 0))
                for j in range(GB):
                    last = nc.vector.tensor_scalar(xn[:, j, :], x[:, g * GB + j, :], x_ms[:, j:j + 1],
                                                   None, ALU.mult)
                last.then_inc(x_normed.sem, 1)
                dve.wait_ge(w_ready.sem, w_ready.at(g, 1))
                nc.vector.tensor_tensor(w_kv[:, 1, :, :], w_kv[:, 0, :, :], v_ps[:, :, :],
                                        ALU.mult).then_inc(kv_ready.sem, 1)
                dve.wait_ge(sums_ready.sem, sums_ready.at(g, 1))
                nc.vector.tensor_scalar(den[:, :], wsum_ps[:, :], 1e-6, None,
                                        ALU.add).then_inc(y_steps.sem, 1)
                dve.wait_ge(y_steps.sem, y_steps.at(g, 1))
                nc.vector.reciprocal(den[:, :], den[:, :]).then_inc(y_steps.sem, 1)
                dve.wait_ge(th_q_ready.sem, th_q_ready.at(g, 1))
                dve.wait_ge(y_steps.sem, y_steps.at(g, 2))
                nc.vector.scalar_tensor_tensor(gate[:, :], th_q[:, :, :].rearrange("p a b -> p (a b)"),
                                               1.0, den[:, :], ALU.add, ALU.mult).then_inc(y_steps.sem, 1)
                dve.wait_ge(y_steps.sem, y_steps.at(g, 3))
                dve.wait_ge(y_turned.sem, y_turned.at(g, 0))
                nc.vector.scalar_tensor_tensor(y[:, :], kvsum_ps[:, :], 0.5, gate[:, :],
                                               ALU.mult, ALU.mult).then_inc(y_steps.sem, 1)
                dve.wait_ge(th_g_ready.sem, th_g_ready.at(g, 1))
                dve.wait_ge(o_ready.sem, o_ready.at(g, 0))
                nc.vector.scalar_tensor_tensor(th_g[:, :], th_g[:, :], 1.0, g_ps[:, :],
                                               ALU.add, ALU.mult).then_inc(h_steps.sem, 1)
                dve.wait_ge(h_steps.sem, h_steps.at(g, 1))
                nc.vector.scalar_tensor_tensor(h[:, :], th_g[:, :], 0.5, u_ps[:, :],
                                               ALU.mult, ALU.mult).then_inc(h_steps.sem, 1)
                dve.wait_ge(o_ready.sem, o_ready.at(g, 1))
                nc.vector.scalar_tensor_tensor(total[:, :, :], x[:, ds(g * GB, GB), :], 2.0,
                                               o_ps[:, :, :], ALU.mult, ALU.add).then_inc(x_steps.sem, 1)
                leave(dve, nc, core, g, x_steps, total, stats)

        @block.tensor
        def _(pe):
            with pe.Fori(0, NG) as g:
                pe.wait_ge(x_normed.sem, x_normed.at(g, 1))
                pe.wait_ge(yT_ready.sem, yT_ready.at(g, 0))
                for j in range(GB):
                    last = nc.tensor.transpose(turn_ps[:, j * 128:(j + 1) * 128], xn[:, j, :], core.ident[:, :])
                last.then_inc(x_turned.sem, 1)
                pe.wait_ge(xnT_ready.sem, xnT_ready.at(g, 1))
                pe.wait_ge(x_steps.sem, x_steps.at(g, 0))
                for j in range(GB):
                    for which, bank in enumerate((q_ps, k_ps, v_ps)):
                        last = nc.tensor.matmul(bank[:, j, :], xnT[:, j * 128:(j + 1) * 128],
                                                core.w["a_wqkvT"][:, which * 128:(which + 1) * 128],
                                                start=True, stop=True)
                last.then_inc(qkv_ready.sem, 1)
                pe.wait_ge(w_ready.sem, w_ready.at(g, 1))
                pe.wait_ge(y_steps.sem, y_steps.at(g, 0))
                nc.tensor.matmul(wsum_ps[:, :], core.upper[:, :],
                                 w_kv[:, 0, :, :].rearrange("p a b -> p (a b)"), start=True, stop=True)
                pe.wait_ge(kv_ready.sem, kv_ready.at(g, 1))
                nc.tensor.matmul(kvsum_ps[:, :], core.upper[:, :],
                                 w_kv[:, 1, :, :].rearrange("p a b -> p (a b)"),
                                 start=True, stop=True).then_inc(sums_ready.sem, 1)
                pe.wait_ge(y_steps.sem, y_steps.at(g, 4))
                for j in range(GB):
                    last = nc.tensor.transpose(turn_ps[:, j * 128:(j + 1) * 128],
                                               y[:, j * 128:(j + 1) * 128], core.ident[:, :])
                last.then_inc(y_turned.sem, 1)
                pe.wait_ge(yT_ready.sem, yT_ready.at(g, 1))
                pe.wait_ge(h_steps.sem, h_steps.at(g, 0))
                nc.tensor.matmul(u_ps[:, :], core.w["a_wuvT"][:, 0:128], yT[:, :], start=True, stop=True)
                nc.tensor.matmul(g_ps[:, :], core.w["a_wuvT"][:, 128:256], yT[:, :],
                                 start=True, stop=True).then_inc(ug_ready.sem, 1)
                pe.wait_ge(h_steps.sem, h_steps.at(g, 2))
                for j in range(GB):
                    last = nc.tensor.matmul(o_ps[:, j, :], h[:, j * 128:(j + 1) * 128],
                                            core.w["a_woutT"][:, :], start=True, stop=True)
                last.then_inc(o_ready.sem, 1)


def in_steps(eng, step):
    step(-2, 0, "a")
    step(-1, 1, "ab")
    step(0, 0, "abc")
    with eng.Fori(1, B - 4, 2) as i:
        step(i, 1, "abcd")
        step(i + 1, 0, "abcd")
    step(B - 3, 1, "abcd")
    step(B - 2, 0, "bcd")
    step(B - 1, 1, "cd")
    step(B, 0, "d")


def phase_cross0(core):
    nc = core.nc
    x = core.x
    heads, dk, quads = 16, 8, 4
    per = heads // quads
    with ExitStack() as ctx:
        def sb(name, shape, dt=F32):
            return ctx.enter_context(nc.sbuf_tensor(name, shape, dt))

        def ps(name, shape, dt=F32):
            return ctx.enter_context(nc.psum_tensor(name, shape, dt))

        signals = []

        def sig(name, per_pass=1):
            signals.append(Signal(ctx.enter_context(nc.semaphore(name)), per_pass))
            return signals[-1]

        ctxT = sb("b_ctxT", [128, 2, S2])
        side = sb("b_side", [128, 2, 2, S2])
        side_sum = sb("b_side_sum", [128, 2, S2])
        xs = sb("b_xs", [128, 2, 128])
        xs_bo = sb("b_xs_bo", [128, 2, 128])
        xT = sb("b_xT", [128, 2, 128])
        qT = sb("b_qT", [128, 2, 128])
        k_own = sb("b_k_own", [128, 2, per, S2])
        v = sb("b_v", [S2, 2, 128])
        p = sb("b_p", [128, 2, heads, S2])
        pT = sb("b_pT", [S2, 2, heads, 128])
        top = sb("b_top", [128, 2, heads])
        norm = sb("b_norm", [128, 2, heads])
        c = sb("b_c", [128, 2, 128])
        cT = sb("b_cT", [128, 2, 128])
        total = sb("b_total", [128, 2, 128])
        stats = sb("b_stats", [128, 2, 6])

        s_ps = ps("b_s_ps", [128, quads, 512])
        turn_ps = ps("b_turn_ps", [128, 2, 512])
        in_ps = ps("b_in_ps", [128, 512])
        out_ps = ps("b_out_ps", [128, 512])
        xT_ps, q_ps, k_ps = in_ps[:, 384:512], in_ps[:, 0:128], in_ps[:, 128:128 + S2]
        v_ps = in_ps[0:S2, 256:384]
        c_ps, cT_ps, y_ps = out_ps[:, 0:128], out_ps[:, 128:256], out_ps[:, 256:384]
        scores = s_ps[:, :, 0:per * S2].rearrange("p r (j s) -> p r j s", s=S2)

        loaded = sig("b_loaded", 48)
        side_ready = sig("b_side_ready")
        x_normed = sig("b_x_normed")
        bo_added = sig("b_bo_added")
        x_turned = sig("b_x_turned")
        xT_ready = sig("b_xT_ready")
        projected = sig("b_projected")
        kv_ready = sig("b_kv_ready")
        scored = sig("b_scored")
        biased = sig("b_biased")
        top_ready = sig("b_top_ready")
        lowered = sig("b_lowered")
        exped = sig("b_exped")
        norm_steps = sig("b_norm_steps", 2)
        p_turned = sig("b_p_turned", quads)
        pT_ready = sig("b_pT_ready", quads)
        mixed = sig("b_mixed")
        c_ready = sig("b_c_ready")
        c_turned = sig("b_c_turned")
        cT_ready = sig("b_cT_ready")
        y_ready = sig("b_y_ready")
        x_steps = sig("b_x_steps", 3)

        open_signals(nc, signals, [core.landed["b"]])
        block = ctx.enter_context(nc.Block())

        @block.sync
        def _(sp):
            def load(i, s):
                sp.wait_ge(loaded.sem, loaded.at(i, 0))
                if behind(i, 2):
                    sp.wait_ge(kv_ready.sem, kv_ready.at(i - 1, 0))
                sp.dma_start(ctxT[:, s, :], core.ins["ctxT"][:, ds(i, 1), :].rearrange("p a s -> p (a s)")
                             ).then_inc(loaded.sem, 16)
                if behind(i, 2):
                    sp.wait_ge(side_ready.sem, side_ready.at(i - 1, 0))
                for n, name in enumerate(("fside", "mask")):
                    sp.dma_start(side[:, s, n, :], core.ins[name][ds(i, 1), :, :].rearrange("a t s -> (a t) s")
                                 ).then_inc(loaded.sem, 16)

            load(0, 0)
            with sp.Fori(1, B - 2, 2) as i:
                load(i, 1)
                load(i + 1, 0)
            load(B - 1, 1)

        @block.gpsimd
        def _(pool):
            def front(i, s):
                pool.wait_ge(loaded.sem, loaded.at(i, 48))
                if behind(i, 2):
                    pool.wait_ge(biased.sem, biased.at(i - 1, 0))
                nc.gpsimd.tensor_tensor(side_sum[:, s, :], side[:, s, 0, :], side[:, s, 1, :],
                                        ALU.add).then_inc(side_ready.sem, 1)
                pool.wait_ge(x_normed.sem, x_normed.at(i, 1))
                if behind(i, 2):
                    pool.wait_ge(x_steps.sem, x_steps.at(i - 1, 0))
                nc.gpsimd.tensor_tensor(xs_bo[:, s, :], xs[:, s, :], core.w["b_bo"][:, :],
                                        ALU.add).then_inc(bo_added.sem, 1)
                pool.wait_ge(top_ready.sem, top_ready.at(i, 1))
                nc.gpsimd.tensor_tensor(p[:, s, :, :], p[:, s, :, :],
                                        top[:, s, :].unsqueeze(2).broadcast_to([128, heads, S2]),
                                        ALU.subtract).then_inc(lowered.sem, 1)

            def step(i, s, stages):
                if "b" in stages:
                    front(i + 1, 1 - s)

            in_steps(pool, step)

        @block.scalar
        def _(act):
            def turn_x(i, s):
                act.wait_ge(x_turned.sem, x_turned.at(i, 1))
                if behind(i, 2):
                    act.wait_ge(projected.sem, projected.at(i - 1, 0))
                nc.scalar.activation(xT[:, s, :], xT_ps, ACT.Copy).then_inc(xT_ready.sem, 1)

            def exp(i, s):
                act.wait_ge(lowered.sem, lowered.at(i, 1))
                nc.scalar.activation(p[:, s, :, :], p[:, s, :, :], ACT.Exp).then_inc(exped.sem, 1)

            def copy_p(i, s, r):
                act.wait_ge(p_turned.sem, p_turned.at(i, r + 1))
                if r == 0:
                    if behind(i, 2):
                        act.wait_ge(mixed.sem, mixed.at(i - 1, 0))
                nc.scalar.activation(pT[:, s, per * r:per * (r + 1), :],
                                     turn_ps[0:S2, r % 2, :].rearrange("p (j t) -> p j t", t=128),
                                     ACT.Copy).then_inc(pT_ready.sem, 1)

            def copy_c(i, s):
                act.wait_ge(c_turned.sem, c_turned.at(i, 1))
                if behind(i, 2):
                    act.wait_ge(y_ready.sem, y_ready.at(i - 1, 0))
                nc.scalar.activation(cT[:, s, :], cT_ps, ACT.Copy).then_inc(cT_ready.sem, 1)

            def step(i, s, stages):
                if "c" in stages:
                    for r in range(quads):
                        copy_p(i, s, r)
                if "a" in stages:
                    turn_x(i + 2, s)
                if "c" in stages:
                    copy_c(i, s)
                if "b" in stages:
                    exp(i + 1, 1 - s)

            in_steps(act, step)

        @block.vector
        def _(dve):
            def normalise(i, s):
                if behind(i, 2):
                    dve.wait_ge(bo_added.sem, bo_added.at(i - 1, 0))
                if behind(i, 2):
                    dve.wait_ge(x_turned.sem, x_turned.at(i - 1, 0))
                nc.vector.tensor_scalar(xs[:, s, :], x[:, i, :], core.mean[:, ds(i, 1)],
                                        core.rstd[:, ds(i, 1)], ALU.subtract,
                                        ALU.mult).then_inc(x_normed.sem, 1)

            def keys_values(i, s):
                dve.wait_ge(projected.sem, projected.at(i, 1))
                if behind(i, 2):
                    dve.wait_ge(scored.sem, scored.at(i - 1, 0))
                nc.vector.tensor_scalar(qT[:, s, :], q_ps, core.w["b_bq"][:, :], None, ALU.add)
                nc.vector.scalar_tensor_tensor(
                    k_own[:, s, :, :], k_ps.unsqueeze(1).broadcast_to([128, per, S2]),
                    core.w["b_bk"][:, :], core.w["head_mask"][:, :].unsqueeze(2).broadcast_to([128, per, S2]),
                    ALU.add, ALU.mult)
                if behind(i, 2):
                    dve.wait_ge(mixed.sem, mixed.at(i - 1, 0))
                nc.vector.tensor_tensor(v[:, s, :], v_ps, core.w["b_bv"][0:S2, :],
                                        ALU.add).then_inc(kv_ready.sem, 1)

            def bias_max(i, s):
                dve.wait_ge(scored.sem, scored.at(i, 1))
                dve.wait_ge(side_ready.sem, side_ready.at(i, 1))
                if behind(i, 2):
                    dve.wait_ge(p_turned.sem, p_turned.at(i - 1, 0))
                nc.vector.tensor_tensor(
                    p[:, s, :, :].rearrange("p (r j) s -> p r j s", r=quads), scores,
                    side_sum[:, s, :].unsqueeze(1).unsqueeze(1).broadcast_to([128, quads, per, S2]),
                    ALU.add).then_inc(biased.sem, 1)
                dve.wait_ge(biased.sem, biased.at(i, 1))
                nc.vector.tensor_reduce(top[:, s, :], p[:, s, :, :], AX.X, ALU.max).then_inc(top_ready.sem, 1)

            def sums(i, s):
                dve.wait_ge(exped.sem, exped.at(i, 1))
                if behind(i, 2):
                    dve.wait_ge(c_ready.sem, c_ready.at(i - 1, 0))
                nc.vector.tensor_reduce(norm[:, s, :], p[:, s, :, :], AX.X, ALU.add).then_inc(norm_steps.sem, 1)
                dve.wait_ge(norm_steps.sem, norm_steps.at(i, 1))
                nc.vector.reciprocal(norm[:, s, :], norm[:, s, :]).then_inc(norm_steps.sem, 1)

            def divide(i, s):
                dve.wait_ge(norm_steps.sem, norm_steps.at(i, 2))
                dve.wait_ge(mixed.sem, mixed.at(i, 1))
                nc.vector.tensor_tensor(
                    c[:, s, :].rearrange("p (h d) -> p h d", d=dk), c_ps.rearrange("p (h d) -> p h d", d=dk),
                    norm[:, s, :].unsqueeze(2).broadcast_to([128, heads, dk]), ALU.mult).then_inc(c_ready.sem, 1)

            def add_up(i, s):
                dve.wait_ge(y_ready.sem, y_ready.at(i, 1))
                dve.wait_ge(bo_added.sem, bo_added.at(i, 1))
                nc.vector.tensor_tensor(total[:, s, :], y_ps, xs_bo[:, s, :], ALU.add).then_inc(x_steps.sem, 1)
                leave_one(dve, nc, core, i, x_steps, total[:, s, :], stats[:, s, :])

            def step(i, s, stages):
                if "a" in stages:
                    normalise(i + 2, s)
                if "c" in stages:
                    sums(i, s)
                if "b" in stages:
                    bias_max(i + 1, 1 - s)
                if "c" in stages:
                    divide(i, s)
                if "a" in stages:
                    keys_values(i + 2, s)
                if "c" in stages:
                    add_up(i, s)

            in_steps(dve, step)

        @block.tensor
        def _(pe):
            def turn_x(i, s):
                pe.wait_ge(x_normed.sem, x_normed.at(i, 1))
                if behind(i, 1):
                    pe.wait_ge(kv_ready.sem, kv_ready.at(i, 0))
                nc.tensor.transpose(xT_ps, xs[:, s, :], core.ident[:, :]).then_inc(x_turned.sem, 1)

            def project(i, s):
                pe.wait_ge(xT_ready.sem, xT_ready.at(i, 1))
                pe.wait_ge(loaded.sem, loaded.at(i, 48))
                nc.tensor.matmul(q_ps, core.w["b_wq"][:, :], xT[:, s, :], start=True, stop=True)
                nc.tensor.matmul(k_ps, core.w["b_wk"][:, :], ctxT[:, s, :], start=True, stop=True)
                nc.tensor.matmul(v_ps, ctxT[:, s, :], core.w["b_wv"][:, :],
                                 start=True, stop=True).then_inc(projected.sem, 1)

            def score(i, s):
                pe.wait_ge(kv_ready.sem, kv_ready.at(i, 1))
                if behind(i, 1):
                    pe.wait_ge(biased.sem, biased.at(i, 0))
                for r in range(quads):
                    rows = slice(32 * r, 32 * r + 32)
                    last = nc.tensor.matmul(s_ps[:, r, 0:per * S2], qT[rows, s, :],
                                            k_own[rows, s, :, :].rearrange("p j s -> p (j s)"),
                                            start=True, stop=True)
                last.then_inc(scored.sem, 1)

            def turn_p(i, s, r):
                if r == 0:
                    pe.wait_ge(exped.sem, exped.at(i, 1))
                if r < 2:
                    if behind(i, 1):
                        pe.wait_ge(pT_ready.sem, pT_ready.at(i - 1, r + 3))
                else:
                    pe.wait_ge(pT_ready.sem, pT_ready.at(i, r - 1))
                for j in range(per):
                    last = nc.tensor.transpose(turn_ps[0:S2, r % 2, j * 128:(j + 1) * 128],
                                               p[:, s, per * r + j, :], core.ident[:, :])
                last.then_inc(p_turned.sem, 1)

            def mix(i, s):
                if behind(i, 1):
                    pe.wait_ge(x_steps.sem, x_steps.at(i - 1, 1))
                for h in range(heads):
                    if h % per == 0:
                        pe.wait_ge(pT_ready.sem, pT_ready.at(i, h // per + 1))
                    last = nc.tensor.matmul(c_ps[:, dk * h:dk * (h + 1)], pT[:, s, h, :],
                                            v[:, s, dk * h:dk * (h + 1)], start=True, stop=True)
                last.then_inc(mixed.sem, 1)

            def turn_c(i, s):
                pe.wait_ge(c_ready.sem, c_ready.at(i, 1))
                nc.tensor.transpose(cT_ps, c[:, s, :], core.ident[:, :]).then_inc(c_turned.sem, 1)

            def project_out(i, s):
                pe.wait_ge(cT_ready.sem, cT_ready.at(i, 1))
                nc.tensor.matmul(y_ps, cT[:, s, :], core.w["b_wo"][:, :],
                                 start=True, stop=True).then_inc(y_ready.sem, 1)

            def step(i, s, stages):
                if "b" in stages:
                    score(i + 1, 1 - s)
                if "c" in stages:
                    for r in range(quads):
                        turn_p(i, s, r)
                    mix(i, s)
                if "a" in stages:
                    turn_x(i + 2, s)
                if "c" in stages:
                    turn_c(i, s)
                if "a" in stages:
                    project(i + 2, s)
                if "c" in stages:
                    project_out(i, s)

            in_steps(pe, step)


def phase_moe(core):
    nc = core.nc
    x = core.x
    shared, routed, halves, top_k = 2, 8, 2, 2
    units = (shared + routed) * halves
    h_slots = 6
    with ExitStack() as ctx:
        def sb(name, shape, dt=F32):
            return ctx.enter_context(nc.sbuf_tensor(name, shape, dt))

        def ps(name, shape, dt=F32):
            return ctx.enter_context(nc.psum_tensor(name, shape, dt))

        signals = []

        def sig(name, per_pass=1):
            signals.append(Signal(ctx.enter_context(nc.semaphore(name)), per_pass))
            return signals[-1]

        xs = sb("m_xs", [128, GB, 128])
        xT = sb("m_xT", [128, GT])
        logits = sb("m_logits", [128, GB, routed])
        above = sb("m_above", [128, GB, routed, routed])
        tied = sb("m_tied", [128, GB, routed, routed])
        rank = sb("m_rank", [128, GB, routed])
        top = sb("m_top", [128, GB])
        share = sb("m_share", [128, GB, routed])
        share_sum = sb("m_share_sum", [128, GB])
        weight = sb("m_weight", [128, GB, routed])
        silu = sb("m_silu", [128, 2, GT])
        h = sb("m_h", [128, h_slots, GT])
        acc = sb("m_acc", [128, GB, 128])
        stats = sb("m_stats", [128, GB, 6])

        g_ps = ps("m_g_ps", [128, 2, GT])
        u_ps = ps("m_u_ps", [128, 2, GT])
        o_ps = ps("m_o_ps", [128, 2, GT])
        turn_ps = ps("m_turn_ps", [128, GT])
        r_ps = ps("m_r_ps", [128, GB, routed])

        x_normed = sig("m_x_normed")
        x_turned = sig("m_x_turned")
        xT_ready = sig("m_xT_ready")
        routed_ready = sig("m_routed_ready")
        route_steps = sig("m_route_steps", 8)
        powered = sig("m_powered")
        divided = sig("m_divided", 2)
        up_ready = sig("m_up_ready", units)
        silu_ready = sig("m_silu_ready", units)
        h_ready = sig("m_h_ready", units)
        down_ready = sig("m_down_ready", 1 + routed)
        acc_steps = sig("m_acc_steps", 1 + routed)
        left_steps = sig("m_left_steps", 3)

        def over_groups(eng, body):
            with eng.Fori(0, NG - 1) as g:
                body(g, True)
            body(NG - 1, False)

        open_signals(nc, signals, [core.landed["m"]])
        block = ctx.enter_context(nc.Block())

        @block.gpsimd
        def _(pool):
            def body(g, more):
                pool.wait_ge(route_steps.sem, route_steps.at(g, 3))
                nc.gpsimd.tensor_tensor(share[:, :, :], core.euler[:, :].rearrange("p (a b) -> p a b", a=GB),
                                        share[:, :, :], ALU.pow).then_inc(powered.sem, 1)

            over_groups(pool, body)

        @block.scalar
        def _(act):
            def copy_xT(g):
                act.wait_ge(x_turned.sem, x_turned.at(g, 1))
                if behind(g, 1):
                    act.wait_ge(up_ready.sem, up_ready.at(g - 1, units))
                nc.scalar.activation(xT[:, :], turn_ps[:, :], ACT.Copy).then_inc(xT_ready.sem, 1)

            def body(g, more):
                for n in range(units):
                    act.wait_ge(up_ready.sem, up_ready.at(g, n + 1))
                    if n < 2:
                        act.wait_ge(h_ready.sem, h_ready.at(g, 0))
                    else:
                        act.wait_ge(h_ready.sem, h_ready.at(g, n - 1))
                    nc.scalar.activation(silu[:, n % 2, :], g_ps[:, n % 2, :],
                                         ACT.Silu).then_inc(silu_ready.sem, 1)
                if more:
                    copy_xT(g + 1)

            copy_xT(0)
            over_groups(act, body)

        @block.vector
        def _(dve):
            def normalise(g):
                if behind(g, 1):
                    dve.wait_ge(acc_steps.sem, acc_steps.at(g - 1, 1))
                for j in range(GB):
                    last = nc.vector.tensor_scalar(xs[:, j, :], x[:, g * GB + j, :],
                                                   core.mean[:, ds(g * GB + j, 1)],
                                                   core.rstd[:, ds(g * GB + j, 1)], ALU.subtract, ALU.mult)
                last.then_inc(x_normed.sem, 1)

            def route(g):
                grid = [128, GB, routed, routed]
                dve.wait_ge(routed_ready.sem, routed_ready.at(g, 1))
                nc.vector.tensor_tensor(logits[:, :, :], r_ps[:, :, :],
                                        core.w["m_bias"][:, :].unsqueeze(1).broadcast_to([128, GB, routed]),
                                        ALU.add).then_inc(route_steps.sem, 1)
                dve.wait_ge(route_steps.sem, route_steps.at(g, 1))
                other = logits[:, :, :].unsqueeze(2).broadcast_to(grid)
                own = logits[:, :, :].unsqueeze(3).broadcast_to(grid)
                nc.vector.tensor_tensor(above[:, :, :, :], other, own, ALU.is_gt)
                nc.vector.tensor_tensor(tied[:, :, :, :], other, own, ALU.is_equal)
                nc.vector.tensor_reduce(top[:, :], logits[:, :, :], AX.X, ALU.max).then_inc(route_steps.sem, 1)
                dve.wait_ge(route_steps.sem, route_steps.at(g, 2))
                nc.vector.tensor_tensor(share[:, :, :], logits[:, :, :],
                                        top[:, :].unsqueeze(2).broadcast_to([128, GB, routed]),
                                        ALU.subtract).then_inc(route_steps.sem, 1)
                nc.vector.tensor_tensor(tied[:, :, :, :].rearrange("p b e f -> p b (e f)"),
                                        tied[:, :, :, :].rearrange("p b e f -> p b (e f)"),
                                        core.w["m_earlier"][:, :].unsqueeze(1).broadcast_to(
                                            [128, GB, routed * routed]), ALU.mult).then_inc(route_steps.sem, 1)
                dve.wait_ge(route_steps.sem, route_steps.at(g, 4))
                nc.vector.tensor_tensor(above[:, :, :, :], above[:, :, :, :], tied[:, :, :, :],
                                        ALU.add).then_inc(route_steps.sem, 1)
                dve.wait_ge(route_steps.sem, route_steps.at(g, 5))
                nc.vector.tensor_reduce(rank[:, :, :], above[:, :, :, :], AX.X, ALU.add).then_inc(route_steps.sem, 1)
                dve.wait_ge(route_steps.sem, route_steps.at(g, 6))
                dve.wait_ge(powered.sem, powered.at(g, 1))
                nc.vector.scalar_tensor_tensor(weight[:, :, :], rank[:, :, :], float(top_k), share[:, :, :],
                                               ALU.is_lt, ALU.mult).then_inc(route_steps.sem, 1)
                dve.wait_ge(route_steps.sem, route_steps.at(g, 7))
                nc.vector.tensor_reduce(share_sum[:, :], weight[:, :, :], AX.X, ALU.add).then_inc(route_steps.sem, 1)
                dve.wait_ge(route_steps.sem, route_steps.at(g, 8))

            def divide(g):
                nc.vector.reciprocal(share_sum[:, :], share_sum[:, :]).then_inc(divided.sem, 1)
                dve.wait_ge(divided.sem, divided.at(g, 1))
                nc.vector.tensor_tensor(weight[:, :, :], weight[:, :, :],
                                        share_sum[:, :].unsqueeze(2).broadcast_to([128, GB, routed]),
                                        ALU.mult).then_inc(divided.sem, 1)
                dve.wait_ge(divided.sem, divided.at(g, 2))

            def hidden(g, n):
                dve.wait_ge(silu_ready.sem, silu_ready.at(g, n + 1))
                if n < h_slots:
                    dve.wait_ge(down_ready.sem, down_ready.at(g, 0))
                else:
                    dve.wait_ge(down_ready.sem, down_ready.at(g, max(0, (n - h_slots) // 2 - 1) + 1))
                nc.vector.tensor_tensor(h[:, n % h_slots, :], silu[:, n % 2, :], u_ps[:, n % 2, :],
                                        ALU.mult).then_inc(h_ready.sem, 1)

            def gather(g, d):
                dve.wait_ge(down_ready.sem, down_ready.at(g, d + 1))
                if d == 0:
                    dve.wait_ge(left_steps.sem, left_steps.at(g, 0))
                    nc.vector.tensor_tensor(acc[:, :, :].rearrange("p b d -> p (b d)"),
                                            xs[:, :, :].rearrange("p b d -> p (b d)"), o_ps[:, 0, :],
                                            ALU.add).then_inc(acc_steps.sem, 1)
                    return
                dve.wait_ge(acc_steps.sem, acc_steps.at(g, d))
                for j in range(GB):
                    last = nc.vector.scalar_tensor_tensor(
                        acc[:, j, :], o_ps[:, d % 2, j * 128:(j + 1) * 128], weight[:, j, d - 1:d],
                        acc[:, j, :], ALU.mult, ALU.add)
                last.then_inc(acc_steps.sem, 1)

            def body(g, more):
                hidden(g, 0)
                hidden(g, 1)
                route(g)
                divide(g)
                hidden(g, 2)
                hidden(g, 3)
                for d in range(1 + routed):
                    if d < routed:
                        hidden(g, 2 * d + 4)
                        hidden(g, 2 * d + 5)
                    gather(g, d)
                    if d == 4 and more:
                        normalise(g + 1)
                dve.wait_ge(acc_steps.sem, acc_steps.at(g, 1 + routed))
                for j in range(GB):
                    last = nc.vector.bn_stats(stats[:, j, :], acc[:, j, :])
                last.then_inc(left_steps.sem, 1)
                nc.vector.tensor_copy(core.x[:, ds(g * GB, GB), :], acc[:, :, :]).then_inc(left_steps.sem, 1)
                dve.wait_ge(left_steps.sem, left_steps.at(g, 2))
                nc.vector.tensor_copy(core.stats[:, ds(g * GB, GB), :], stats[:, :, :]).then_inc(left_steps.sem, 1)

            normalise(0)
            over_groups(dve, body)

        @block.tensor
        def _(pe):
            def turn(g):
                pe.wait_ge(x_normed.sem, x_normed.at(g, 1))
                if behind(g, 1):
                    pe.wait_ge(xT_ready.sem, xT_ready.at(g - 1, 1))
                for j in range(GB):
                    last = nc.tensor.transpose(turn_ps[:, j * 128:(j + 1) * 128], xs[:, j, :], core.ident[:, :])
                last.then_inc(x_turned.sem, 1)

            def router(g):
                pe.wait_ge(xT_ready.sem, xT_ready.at(g, 1))
                pe.wait_ge(route_steps.sem, route_steps.at(g, 0))
                for j in range(GB):
                    last = nc.tensor.matmul(r_ps[:, j, :], xT[:, j * 128:(j + 1) * 128], core.w["m_router"][:, :],
                                            start=True, stop=True)
                last.then_inc(routed_ready.sem, 1)

            def up(g, n):
                if n < 2:
                    pe.wait_ge(h_ready.sem, h_ready.at(g, 0))
                else:
                    pe.wait_ge(h_ready.sem, h_ready.at(g, n - 1))
                nc.tensor.matmul(g_ps[:, n % 2, :], core.w["m_w1"][:, n, :], xT[:, :], start=True, stop=True)
                nc.tensor.matmul(u_ps[:, n % 2, :], core.w["m_w3"][:, n, :], xT[:, :],
                                 start=True, stop=True).then_inc(up_ready.sem, 1)

            def down(g, d):
                mine = range(0, shared * halves) if d == 0 else range(2 * d + 2, 2 * d + 4)
                pe.wait_ge(h_ready.sem, h_ready.at(g, mine[-1] + 1))
                pe.wait_ge(acc_steps.sem, acc_steps.at(g, max(0, d - 1)))
                for j in range(GB):
                    for n in mine:
                        last = nc.tensor.matmul(o_ps[:, d % 2, j * 128:(j + 1) * 128],
                                                h[:, n % h_slots, j * 128:(j + 1) * 128],
                                                core.w["m_w2"][:, n, :], start=(n == mine[0]), stop=(n == mine[-1]))
                last.then_inc(down_ready.sem, 1)

            def body(g, more):
                router(g)
                for n in range(4):
                    up(g, n)
                for d in range(1 + routed):
                    if d < routed:
                        up(g, 2 * d + 4)
                        up(g, 2 * d + 5)
                    elif more:
                        turn(g + 1)
                    down(g, d)

            turn(0)
            over_groups(pe, body)


def phase_scan(core):
    nc = core.nc
    x = core.x
    halves, states, rank, taps = 2, 16, 16, 4
    parts = 3
    with ExitStack() as ctx:
        def sb(name, shape, dt=F32):
            return ctx.enter_context(nc.sbuf_tensor(name, shape, dt))

        def ps(name, shape, dt=F32):
            return ctx.enter_context(nc.psum_tensor(name, shape, dt))

        signals = []

        def sig(name, per_pass=1):
            signals.append(Signal(ctx.enter_context(nc.semaphore(name)), per_pass))
            return signals[-1]

        decay_rate = sb("s_decay_rate", [128, halves, states])
        pick = sb("s_pick", [parts * 32, 2 * states, 128], BF16)
        xs = sb("s_xs", [128, GB, 128])
        xs_bo = sb("s_xs_bo", [128, 2, GB, 128])
        xT = sb("s_xT", [128, GT])
        padded = sb("s_padded", [128, halves, GB, taps - 1 + T])
        conv = sb("s_conv", [128, halves, GB, T])
        conv_sig = sb("s_conv_sig", [128, halves, GT])
        u = sb("s_u", [128, 2, halves, GT])
        res = sb("s_res", [128, halves, GT])
        res_th = sb("s_res_th", [128, halves, GT])
        res_gate = sb("s_res_gate", [128, 2, halves, GT])
        dtT = sb("s_dtT", [rank, GT])
        rest1 = sb("s_rest1", [32, GT])
        middle = sb("s_middle", [32, GT], BF16)
        bc_parts = sb("s_bc_parts", [parts * 32, 2, GT], BF16)
        raw = sb("s_raw", [128, halves, GT])
        soft = sb("s_soft", [128, halves, GT])
        delta = sb("s_delta", [128, 2, halves, GT])
        du = sb("s_du", [128, 2, halves, GT])
        decay = sb("s_decay", [128, 2, halves, GB, T])
        b_sb = sb("s_b_sb", [128, 2, GT])
        drive = sb("s_drive", [128, 2, halves, GT])
        state = sb("s_state", [128, 2, halves, GT])
        read = sb("s_read", [128, 2, halves, GT])
        y = sb("s_y", [128, halves, GT])
        total = sb("s_total", [128, GB, 128])
        stats = sb("s_stats", [128, GB, 6])

        b_ps = ps("s_b_ps", [128, 2, GT])
        c_ps = ps("s_c_ps", [128, 2, GT])
        y_ps = ps("s_y_ps", [128, halves, GT])
        f0_ps = ps("s_f0_ps", [128, GT])
        f1_ps = ps("s_f1_ps", [128, GT])

        prepared = sig("s_prepared", 4)
        x_normed = sig("s_x_normed")
        bo_added = sig("s_bo_added")
        x_turned = sig("s_x_turned")
        xT_ready = sig("s_xT_ready")
        z_ready = sig("s_z_ready", 4)
        z_copied = sig("s_z_copied", 4)
        conv_steps = sig("s_conv_steps", halves * taps)
        res_tanh = sig("s_res_tanh")
        res_ready = sig("s_res_ready")
        conv_th = sig("s_conv_th")
        conv_gate = sig("s_conv_gate")
        u_ready = sig("s_u_ready")
        bc_ready = sig("s_bc_ready")
        dt_ready = sig("s_dt_ready")
        dt_copied = sig("s_dt_copied")
        split_steps = sig("s_split_steps", 5)
        raw_ps_ready = sig("s_raw_ps_ready", halves)
        raw_ready = sig("s_raw_ready", halves)
        soft_steps = sig("s_soft_steps", 3)
        delta_ready = sig("s_delta_ready")
        du_ready = sig("s_du_ready")
        b_spread = sig("s_b_spread", states)
        c_spread = sig("s_c_spread", states)
        decay_ready = sig("s_decay_ready", states)
        b_copied = sig("s_b_copied", states)
        driven = sig("s_driven", states)
        scanned = sig("s_scanned", states)
        read_out = sig("s_read_out", states)
        summed = sig("s_summed", states)
        y_steps = sig("s_y_steps", 3)
        o_ready = sig("s_o_ready")
        x_steps = sig("s_x_steps", 3)

        def over_groups(eng, front, body):
            front(0, 0)
            body(0, 0, True)
            with eng.Fori(1, NG - 2, 2) as g:
                body(g, 1, True)
                body(g + 1, 0, True)
            body(NG - 1, 1, False)

        def pieces_of(pieces):
            def front(g, s):
                for piece in pieces.values():
                    piece(g, s)
            return front

        open_signals(nc, signals, [core.landed["s"]])
        block = ctx.enter_context(nc.Block())

        @block.gpsimd
        def _(pool):
            nc.gpsimd.memset(padded[:, :, :, 0:taps - 1], 0.0).then_inc(prepared.sem, 1)
            nc.gpsimd.memset(decay[:, :, :, :, 0:1], 0.0).then_inc(prepared.sem, 1)

            def add_bo(g, s):
                pool.wait_ge(x_normed.sem, x_normed.at(g, 1))
                if behind(g, 2):
                    pool.wait_ge(x_steps.sem, x_steps.at(g - 1, 0))
                nc.gpsimd.tensor_tensor(xs_bo[:, s, :, :], xs[:, :, :],
                                        core.w["s_bo"][:, :].unsqueeze(1).broadcast_to([128, GB, 128]),
                                        ALU.add).then_inc(bo_added.sem, 1)

            def gate_u(g, s):
                pool.wait_ge(conv_gate.sem, conv_gate.at(g, 1))
                if behind(g, 2):
                    pool.wait_ge(y_steps.sem, y_steps.at(g - 1, 0))
                nc.gpsimd.tensor_tensor(u[:, s, :, :], conv_sig[:, :, :],
                                        conv[:, :, :, :].rearrange("p h b t -> p h (b t)"),
                                        ALU.mult).then_inc(u_ready.sem, 1)

            def mult_du(g, s):
                pool.wait_ge(delta_ready.sem, delta_ready.at(g, 1))
                nc.gpsimd.tensor_tensor(du[:, s, :, :], delta[:, s, :, :], u[:, s, :, :],
                                        ALU.mult).then_inc(du_ready.sem, 1)

            def drive_state(g, s, n):
                if n == 0:
                    pool.wait_ge(du_ready.sem, du_ready.at(g, 1))
                pool.wait_ge(b_copied.sem, b_copied.at(g, n + 1))
                if n:
                    pool.wait_ge(scanned.sem, scanned.at(g, n - 1))
                elif behind(g, 1):
                    pool.wait_ge(scanned.sem, scanned.at(g - 1, states - 1))
                nc.gpsimd.tensor_tensor(drive[:, n % 2, :, :], du[:, s, :, :],
                                        b_sb[:, n % 2, :].unsqueeze(1).broadcast_to([128, halves, GT]),
                                        ALU.mult).then_inc(driven.sem, 1)

            pieces = {2: add_bo, 8: gate_u, 14: mult_du}

            def body(g, s, more):
                for n in range(states):
                    drive_state(g, s, n)
                    if more and n in pieces:
                        pieces[n](g + 1, 1 - s)

            over_groups(pool, pieces_of(pieces), body)

        @block.scalar
        def _(act):
            nc.scalar.activation(decay_rate[:, :, :], core.w["s_A_log"][:, :, :], ACT.Exp).then_inc(prepared.sem, 1)

            def copy_xT(g, s):
                act.wait_ge(x_turned.sem, x_turned.at(g, 1))
                nc.scalar.activation(xT[:, :], f0_ps[:, :], ACT.Copy).then_inc(xT_ready.sem, 1)

            def copy_z(g, s, m):
                act.wait_ge(z_ready.sem, z_ready.at(g, m + 1))
                bank = (f1_ps, f0_ps)[m % 2]
                bias = core.w["s_b_in"][:, m:m + 1]
                if m < 2:
                    if behind(g, 1):
                        act.wait_ge(conv_steps.sem, conv_steps.at(g - 1, halves * taps))
                    out = padded[:, m, :, taps - 1:]
                    nc.scalar.activation(out, bank[:, :].rearrange("p (b t) -> p b t", t=T), ACT.Identity,
                                         bias=bias).then_inc(z_copied.sem, 1)
                else:
                    if behind(g, 1):
                        act.wait_ge(res_ready.sem, res_ready.at(g - 1, 1))
                    nc.scalar.activation(res[:, m - 2, :], bank[:, :], ACT.Identity,
                                         bias=bias).then_inc(z_copied.sem, 1)

            def tanhs(g, s):
                act.wait_ge(z_copied.sem, z_copied.at(g, 4))
                if behind(g, 1):
                    act.wait_ge(res_ready.sem, res_ready.at(g - 1, 1))
                nc.scalar.activation(res_th[:, :, :], res[:, :, :], ACT.Tanh, scale=0.5).then_inc(res_tanh.sem, 1)
                act.wait_ge(conv_steps.sem, conv_steps.at(g, halves * taps))
                if behind(g, 1):
                    act.wait_ge(u_ready.sem, u_ready.at(g - 1, 1))
                nc.scalar.activation(conv_sig[:, :, :], conv[:, :, :, :].rearrange("p h b t -> p h (b t)"),
                                     ACT.Tanh, scale=0.5).then_inc(conv_th.sem, 1)
                act.wait_ge(conv_th.sem, conv_th.at(g, 1))
                nc.scalar.activation(conv_sig[:, :, :], conv_sig[:, :, :], ACT.Copy, scale=0.5,
                                     bias=0.5).then_inc(conv_gate.sem, 1)

            def copy_raw(g, s):
                for m in range(halves):
                    act.wait_ge(raw_ps_ready.sem, raw_ps_ready.at(g, m + 1))
                    if m == 0:
                        if behind(g, 1):
                            act.wait_ge(delta_ready.sem, delta_ready.at(g - 1, 1))
                    nc.scalar.activation(raw[:, m, :], (f1_ps, f0_ps)[m][:, :], ACT.Identity,
                                         bias=core.w["s_dt_bias"][:, m:m + 1]).then_inc(raw_ready.sem, 1)

            def softplus(g, s):
                act.wait_ge(raw_ready.sem, raw_ready.at(g, halves))
                nc.scalar.activation(soft[:, :, :], raw[:, :, :], ACT.Abs).then_inc(soft_steps.sem, 1)
                act.wait_ge(soft_steps.sem, soft_steps.at(g, 1))
                nc.scalar.activation(soft[:, :, :], soft[:, :, :], ACT.Exp, scale=-1.0).then_inc(soft_steps.sem, 1)
                act.wait_ge(soft_steps.sem, soft_steps.at(g, 2))
                nc.scalar.activation(soft[:, :, :], soft[:, :, :], ACT.Ln, bias=1.0).then_inc(soft_steps.sem, 1)

            def spread_state(g, s, n):
                if n == 0:
                    act.wait_ge(delta_ready.sem, delta_ready.at(g, 1))
                    if isinstance(g, int) and g == 0:
                        act.wait_ge(prepared.sem, 1 + 4)
                if n:
                    act.wait_ge(scanned.sem, scanned.at(g, n - 1))
                elif behind(g, 1):
                    act.wait_ge(scanned.sem, scanned.at(g - 1, states - 1))
                for m in range(halves):
                    last = nc.scalar.activation(
                        decay[:, n % 2, m, :, 1:], delta[:, s, m, :].rearrange("p (b t) -> p b t", t=T)[:, :, 1:],
                        ACT.Exp, scale=core.neg_rate[:, m, n:n + 1])
                last.then_inc(decay_ready.sem, 1)
                act.wait_ge(b_spread.sem, b_spread.at(g, n + 1))
                if n:
                    act.wait_ge(driven.sem, driven.at(g, n - 1))
                elif behind(g, 1):
                    act.wait_ge(driven.sem, driven.at(g - 1, states - 1))
                nc.scalar.activation(b_sb[:, n % 2, :], b_ps[:, n % 2, :], ACT.Copy).then_inc(b_copied.sem, 1)

            def copy_conv(g, s):
                copy_z(g, s, 0)
                copy_z(g, s, 1)

            def copy_res(g, s):
                copy_z(g, s, 2)
                copy_z(g, s, 3)

            pieces = {2: copy_xT, 4: copy_conv, 6: copy_res, 7: tanhs, 12: copy_raw, 13: softplus}

            def body(g, s, more):
                for n in range(states):
                    spread_state(g, s, n)
                    if more and n in pieces:
                        pieces[n](g + 1, 1 - s)

            over_groups(act, pieces_of(pieces), body)

        @block.vector
        def _(dve):
            dve.wait_ge(prepared.sem, 1 + 3)
            nc.vector.tensor_scalar(core.neg_rate[:, :, :], decay_rate[:, :, :], -1.0, None, ALU.mult)
            nc.vector.tensor_copy(pick[:, :, :], core.w["s_pick"][:, :].unsqueeze(2).broadcast_to(
                [parts * 32, 2 * states, 128])).then_inc(prepared.sem, 1)

            def normalise(g, s):
                if behind(g, 1):
                    dve.wait_ge(bo_added.sem, bo_added.at(g - 1, 1))
                if behind(g, 1):
                    dve.wait_ge(x_turned.sem, x_turned.at(g - 1, 1))
                for j in range(GB):
                    last = nc.vector.tensor_scalar(xs[:, j, :], x[:, g * GB + j, :],
                                                   core.mean[:, ds(g * GB + j, 1)],
                                                   core.rstd[:, ds(g * GB + j, 1)], ALU.subtract, ALU.mult)
                last.then_inc(x_normed.sem, 1)

            def convolve(g, s, m):
                dve.wait_ge(z_copied.sem, z_copied.at(g, m + 1))
                if behind(g, 1):
                    dve.wait_ge(u_ready.sem, u_ready.at(g - 1, 1))
                for k in range(taps):
                    tap = core.w["s_conv_w"][:, m, k:k + 1]
                    shifted = padded[:, m, :, k:k + T]
                    if k == 0:
                        nc.vector.tensor_scalar(conv[:, m, :, :], shifted, tap, core.w["s_conv_b"][:, m:m + 1],
                                                ALU.mult, ALU.add).then_inc(conv_steps.sem, 1)
                    else:
                        dve.wait_ge(conv_steps.sem, conv_steps.at(g, taps * m + k))
                        nc.vector.scalar_tensor_tensor(conv[:, m, :, :], shifted, tap, conv[:, m, :, :],
                                                       ALU.mult, ALU.add).then_inc(conv_steps.sem, 1)

            def gate_res(g, s):
                dve.wait_ge(res_tanh.sem, res_tanh.at(g, 1))
                if behind(g, 2):
                    dve.wait_ge(y_steps.sem, y_steps.at(g - 1, 0))
                nc.vector.scalar_tensor_tensor(res_gate[:, s, :, :], res_th[:, :, :], 1.0, res[:, :, :],
                                               ALU.add, ALU.mult).then_inc(res_ready.sem, 1)

            def split_bc(g, s):
                dve.wait_ge(dt_ready.sem, dt_ready.at(g, 1))
                if behind(g, 1):
                    dve.wait_ge(raw_ps_ready.sem, raw_ps_ready.at(g - 1, halves))
                nc.vector.tensor_copy(dtT[:, :], f0_ps[0:rank, :]).then_inc(dt_copied.sem, 1)
                dve.wait_ge(bc_ready.sem, bc_ready.at(g, 1))
                if behind(g, 2):
                    dve.wait_ge(c_spread.sem, c_spread.at(g - 1, 0))
                nc.vector.tensor_copy(bc_parts[0:32, s, :], f1_ps[0:32, :]).then_inc(split_steps.sem, 1)
                dve.wait_ge(split_steps.sem, split_steps.at(g, 1))
                nc.vector.tensor_tensor(rest1[:, :], f1_ps[0:32, :], bc_parts[0:32, s, :],
                                        ALU.subtract).then_inc(split_steps.sem, 1)
                dve.wait_ge(split_steps.sem, split_steps.at(g, 2))
                nc.vector.tensor_copy(middle[:, :], rest1[:, :]).then_inc(split_steps.sem, 1)
                dve.wait_ge(split_steps.sem, split_steps.at(g, 3))
                nc.vector.tensor_copy(bc_parts[32:64, s, :], middle[:, :]).then_inc(split_steps.sem, 1)
                nc.vector.tensor_tensor(bc_parts[64:96, s, :], rest1[:, :], middle[:, :],
                                        ALU.subtract).then_inc(split_steps.sem, 1)

            def make_delta(g, s):
                dve.wait_ge(soft_steps.sem, soft_steps.at(g, 3))
                if behind(g, 2):
                    dve.wait_ge(decay_ready.sem, decay_ready.at(g - 1, 0))
                if behind(g, 2):
                    dve.wait_ge(du_ready.sem, du_ready.at(g - 1, 0))
                nc.vector.scalar_tensor_tensor(delta[:, s, :, :], raw[:, :, :], 0.0, soft[:, :, :],
                                               ALU.max, ALU.add).then_inc(delta_ready.sem, 1)

            def scan_state(g, s, n):
                dve.wait_ge(decay_ready.sem, decay_ready.at(g, n + 1))
                dve.wait_ge(driven.sem, driven.at(g, n + 1))
                if n:
                    dve.wait_ge(read_out.sem, read_out.at(g, n - 1))
                elif behind(g, 1):
                    dve.wait_ge(read_out.sem, read_out.at(g - 1, states - 1))
                nc.vector.tensor_tensor_scan(state[:, n % 2, :, :].rearrange("p h t -> p (h t)"),
                                             decay[:, n % 2, :, :, :].rearrange("p h b t -> p (h b t)"),
                                             drive[:, n % 2, :, :].rearrange("p h t -> p (h t)"),
                                             0.0, ALU.mult, ALU.add).then_inc(scanned.sem, 1)

            def read_state(g, s, n):
                dve.wait_ge(scanned.sem, scanned.at(g, n + 1))
                if n:
                    dve.wait_ge(summed.sem, summed.at(g, n - 1))
                elif behind(g, 1):
                    dve.wait_ge(summed.sem, summed.at(g - 1, states - 1))
                dve.wait_ge(c_spread.sem, c_spread.at(g, n + 1))
                nc.vector.tensor_tensor(read[:, n % 2, :, :], state[:, n % 2, :, :],
                                        c_ps[:, n % 2, :].unsqueeze(1).broadcast_to([128, halves, GT]),
                                        ALU.mult).then_inc(read_out.sem, 1)

            def finish(g, s):
                dve.wait_ge(summed.sem, summed.at(g, states))
                if behind(g, 1):
                    dve.wait_ge(o_ready.sem, o_ready.at(g - 1, 1))
                for m in range(halves):
                    nc.vector.scalar_tensor_tensor(y[:, m, :], u[:, s, m, :], core.w["s_D"][:, m:m + 1],
                                                   y_ps[:, m, :], ALU.mult, ALU.add).then_inc(y_steps.sem, 1)
                dve.wait_ge(y_steps.sem, y_steps.at(g, 2))
                nc.vector.scalar_tensor_tensor(y[:, :, :], y[:, :, :], 0.5, res_gate[:, s, :, :],
                                               ALU.mult, ALU.mult).then_inc(y_steps.sem, 1)
                dve.wait_ge(o_ready.sem, o_ready.at(g, 1))
                dve.wait_ge(bo_added.sem, bo_added.at(g, 1))
                nc.vector.tensor_tensor(total[:, :, :].rearrange("p b d -> p (b d)"), f1_ps[:, :],
                                        xs_bo[:, s, :, :].rearrange("p b d -> p (b d)"),
                                        ALU.add).then_inc(x_steps.sem, 1)
                leave(dve, nc, core, g, x_steps, total, stats)

            pieces = {0: normalise, 5: lambda g, s: convolve(g, s, 0), 6: lambda g, s: convolve(g, s, 1),
                      8: gate_res, 10: split_bc, 14: make_delta}

            def body(g, s, more):
                for n in range(states):
                    scan_state(g, s, n)
                    if n:
                        read_state(g, s, n - 1)
                    if more and n in pieces:
                        pieces[n](g + 1, 1 - s)
                read_state(g, s, states - 1)
                finish(g, s)

            over_groups(dve, pieces_of(pieces), body)

        @block.tensor
        def _(pe):
            def turn(g, s):
                pe.wait_ge(x_normed.sem, x_normed.at(g, 1))
                if behind(g, 1):
                    pe.wait_ge(raw_ready.sem, raw_ready.at(g - 1, halves))
                for j in range(GB):
                    last = nc.tensor.transpose(f0_ps[:, j * 128:(j + 1) * 128], xs[:, j, :], core.ident[:, :])
                last.then_inc(x_turned.sem, 1)

            def project_z(g, s, m):
                if m == 0:
                    pe.wait_ge(xT_ready.sem, xT_ready.at(g, 1))
                    if behind(g, 2):
                        pe.wait_ge(x_steps.sem, x_steps.at(g - 2, 1))
                    if behind(g, 1):
                        pe.wait_ge(raw_ready.sem, raw_ready.at(g - 1, 1))
                elif m > 1:
                    pe.wait_ge(z_copied.sem, z_copied.at(g, m - 1))
                nc.tensor.matmul((f1_ps, f0_ps)[m % 2][:, :], core.w["s_w_in"][:, m * 128:(m + 1) * 128],
                                 xT[:, :], start=True, stop=True).then_inc(z_ready.sem, 1)

            def project_bc(g, s):
                pe.wait_ge(u_ready.sem, u_ready.at(g, 1))
                pe.wait_ge(z_copied.sem, z_copied.at(g, 4))
                for cols, bank, rows, signal in ((slice(rank, rank + 2 * states), f1_ps, 2 * states, bc_ready),
                                                 (slice(0, rank), f0_ps, rank, dt_ready)):
                    for m in range(halves):
                        last = nc.tensor.matmul(bank[0:rows, :], core.w["s_x_proj"][:, m, cols], u[:, s, m, :],
                                                start=(m == 0), stop=(m == halves - 1))
                    last.then_inc(signal.sem, 1)

            def project_dt(g, s):
                pe.wait_ge(dt_copied.sem, dt_copied.at(g, 1))
                pe.wait_ge(split_steps.sem, split_steps.at(g, 2))
                for m in range(halves):
                    nc.tensor.matmul((f1_ps, f0_ps)[m][:, :], core.w["s_dt_proj"][:, m * 128:(m + 1) * 128],
                                     dtT[:, :], start=True, stop=True).then_inc(raw_ps_ready.sem, 1)

            def spread_b(g, s, n):
                if n == 0:
                    if isinstance(g, int) and g == 0:
                        pe.wait_ge(prepared.sem, 1 + 4)
                    pe.wait_ge(split_steps.sem, split_steps.at(g, 5))
                if n >= 2:
                    pe.wait_ge(b_copied.sem, b_copied.at(g, n - 1))
                elif behind(g, 1):
                    pe.wait_ge(b_copied.sem, b_copied.at(g - 1, states + n - 1))
                nc.tensor.matmul(b_ps[:, n % 2, :], pick[:, n, :], bc_parts[:, s, :],
                                 start=True, stop=True).then_inc(b_spread.sem, 1)

            def spread_c(g, s, n):
                if n >= 2:
                    pe.wait_ge(read_out.sem, read_out.at(g, n - 1))
                elif behind(g, 1):
                    pe.wait_ge(read_out.sem, read_out.at(g - 1, states + n - 1))
                nc.tensor.matmul(c_ps[:, n % 2, :], pick[:, states + n, :], bc_parts[:, s, :],
                                 start=True, stop=True).then_inc(c_spread.sem, 1)

            def sum_state(g, s, n):
                pe.wait_ge(read_out.sem, read_out.at(g, n + 1))
                if n == 0:
                    if behind(g, 1):
                        pe.wait_ge(y_steps.sem, y_steps.at(g - 1, 2))
                for m in range(halves):
                    last = nc.tensor.matmul(y_ps[:, m, :], core.ident[:, :], read[:, n % 2, m, :],
                                            start=(n == 0), stop=(n == states - 1))
                last.then_inc(summed.sem, 1)

            def project_out(g, s, more):
                pe.wait_ge(y_steps.sem, y_steps.at(g, 3))
                if more:
                    pe.wait_ge(raw_ready.sem, raw_ready.at(g + 1, 1))
                else:
                    pe.wait_ge(raw_ready.sem, raw_ready.at(g, 1))
                for j in range(GB):
                    for m in range(halves):
                        last = nc.tensor.matmul(f1_ps[:, j * 128:(j + 1) * 128], y[:, m, j * 128:(j + 1) * 128],
                                                core.w["s_w_out"][:, m, :], start=(m == 0), stop=(m == halves - 1))
                last.then_inc(o_ready.sem, 1)

            def project_conv(g, s):
                project_z(g, s, 0)
                project_z(g, s, 1)

            def project_res(g, s):
                project_z(g, s, 2)
                project_z(g, s, 3)

            pieces = {1: turn, 3: project_conv, 5: project_res, 9: project_bc, 11: project_dt}

            def body(g, s, more):
                for n in range(states):
                    if n < states - 2:
                        spread_b(g, s, n + 2)
                    elif more:
                        spread_b(g + 1, 1 - s, n + 2 - states)
                    if n < states - 1:
                        spread_c(g, s, n + 1)
                    elif more:
                        spread_c(g + 1, 1 - s, 0)
                    if n:
                        sum_state(g, s, n - 1)
                    if more and n in pieces:
                        pieces[n](g + 1, 1 - s)
                sum_state(g, s, states - 1)
                project_out(g, s, more)

            def front(g, s):
                pieces_of(pieces)(g, s)
                spread_b(g, s, 0)
                spread_b(g, s, 1)
                spread_c(g, s, 0)

            over_groups(pe, front, body)


def phase_cross1(core):
    nc = core.nc
    x = core.x
    heads, dk, banks = 16, 64, 4
    per = heads // banks
    blocks = heads * dk // 128
    half = blocks // 2
    with ExitStack() as ctx:
        def sb(name, shape, dt=F32):
            return ctx.enter_context(nc.sbuf_tensor(name, shape, dt))

        def ps(name, shape, dt=F32):
            return ctx.enter_context(nc.psum_tensor(name, shape, dt))

        signals = []

        def sig(name, per_pass=1):
            signals.append(Signal(ctx.enter_context(nc.semaphore(name)), per_pass))
            return signals[-1]

        ctxT = sb("c_ctxT", [128, 2, S2])
        xs = sb("c_xs", [128, 2, 128])
        xs_bo = sb("c_xs_bo", [128, 2, 128])
        xs_beta = sb("c_xs_beta", [128, 2, 128])
        xT = sb("c_xT", [128, 2, 128])
        q = sb("c_q", [128, 2, blocks, 128])
        k = sb("c_k", [128, 2, blocks, S2])
        v = sb("c_v", [S2, 2, heads * dk])
        p = sb("c_p", [128, 2, heads, S2])
        pT = sb("c_pT", [S2, heads, 128])
        top = sb("c_top", [128, 2, heads])
        norm = sb("c_norm", [128, 2, heads])
        oT = sb("c_oT", [128, blocks, 128])
        inner = sb("c_inner", [128, 128])
        inner_stats = sb("c_inner_stats", [128, 6])
        inner_mv = sb("c_inner_mv", [128, 2])
        spare = sb("c_spare", [128, 1])
        total = sb("c_total", [128, 128])
        stats = sb("c_stats", [128, 2, 6])

        s_ps = ps("c_s_ps", [128, banks, 512])
        turn_ps = ps("c_turn_ps", [128, 2, 512])
        f0_ps = ps("c_f0_ps", [128, 512])
        f1_ps = ps("c_f1_ps", [128, 512])
        scores = s_ps[:, :, 0:per * S2].rearrange("p r (j s) -> p r j s", s=S2)

        loaded = sig("c_loaded", 16)
        x_normed = sig("c_x_normed")
        bo_added = sig("c_bo_added")
        x_turned = sig("c_x_turned")
        xT_ready = sig("c_xT_ready")
        qk_ps_ready = sig("c_qk_ps_ready", 4)
        qk_ready = sig("c_qk_ready", 4)
        v_ps_ready = sig("c_v_ps_ready", 2)
        v_ready = sig("c_v_ready", 2)
        scored = sig("c_scored")
        top_ready = sig("c_top_ready")
        lowered = sig("c_lowered")
        exped = sig("c_exped")
        norm_steps = sig("c_norm_steps", 2)
        divided = sig("c_divided")
        p_turned = sig("c_p_turned", banks)
        pT_ready = sig("c_pT_ready", banks)
        mixed = sig("c_mixed", 2)
        oT_ready = sig("c_oT_ready", 2)
        y_ready = sig("c_y_ready")
        inner_steps = sig("c_inner_steps", 4)
        inner_eps = sig("c_inner_eps")
        inner_rstd = sig("c_inner_rstd")
        scaled = sig("c_scaled")
        summed = sig("c_summed")
        left_steps = sig("c_left_steps", 3)

        def head_of(r, j):
            return 8 * (r // 2) + 2 * j + r % 2

        open_signals(nc, signals, [core.landed["c"]])
        block = ctx.enter_context(nc.Block())

        @block.sync
        def _(sp):
            def load(i, s):
                sp.wait_ge(loaded.sem, loaded.at(i, 0))
                if behind(i, 2):
                    sp.wait_ge(v_ps_ready.sem, v_ps_ready.at(i - 1, 0))
                sp.dma_start(ctxT[:, s, :], core.ins["ctxT"][:, ds(i, 1), :].rearrange("p a s -> p (a s)")
                             ).then_inc(loaded.sem, 16)

            load(0, 0)
            with sp.Fori(1, B - 2, 2) as i:
                load(i, 1)
                load(i + 1, 0)
            load(B - 1, 1)

        @block.gpsimd
        def _(pool):
            def inner_root(i, s):
                pool.wait_ge(inner_steps.sem, inner_steps.at(i, 3))
                nc.gpsimd.tensor_tensor(inner_mv[:, 1:2], inner_mv[:, 1:2], core.ln_eps[:, :],
                                        ALU.add).then_inc(inner_eps.sem, 1)
                pool.wait_ge(inner_eps.sem, inner_eps.at(i, 1))
                nc.gpsimd.tensor_tensor(inner_mv[:, 1:2], inner_mv[:, 1:2], core.minus_half[:, 0:1],
                                        ALU.pow).then_inc(inner_rstd.sem, 1)

            def gamma_beta(i, s):
                pool.wait_ge(inner_steps.sem, inner_steps.at(i, 4))
                if behind(i, 1):
                    pool.wait_ge(left_steps.sem, left_steps.at(i - 1, 3))
                nc.gpsimd.tensor_tensor(total[:, :], inner[:, :], core.w["c_gamma"][:, :],
                                        ALU.mult).then_inc(scaled.sem, 1)
                pool.wait_ge(scaled.sem, scaled.at(i, 1))
                nc.gpsimd.tensor_tensor(total[:, :], total[:, :], xs_beta[:, s, :],
                                        ALU.add).then_inc(summed.sem, 1)

            def add_biases(i, s):
                pool.wait_ge(x_normed.sem, x_normed.at(i, 1))
                if behind(i, 2):
                    pool.wait_ge(inner_steps.sem, inner_steps.at(i - 1, 0))
                if behind(i, 2):
                    pool.wait_ge(summed.sem, summed.at(i - 1, 0))
                nc.gpsimd.tensor_tensor(xs_bo[:, s, :], xs[:, s, :], core.w["c_bo"][:, :], ALU.add)
                nc.gpsimd.tensor_tensor(xs_beta[:, s, :], xs[:, s, :], core.w["c_beta"][:, :],
                                        ALU.add).then_inc(bo_added.sem, 1)

            def divide(i, s):
                pool.wait_ge(norm_steps.sem, norm_steps.at(i, 2))
                nc.gpsimd.tensor_tensor(p[:, s, :, :], p[:, s, :, :],
                                        norm[:, s, :].unsqueeze(2).broadcast_to([128, heads, S2]),
                                        ALU.mult).then_inc(divided.sem, 1)

            def step(i, s, stages):
                if "d" in stages:
                    inner_root(i - 1, 1 - s)
                    gamma_beta(i - 1, 1 - s)
                if "b" in stages:
                    add_biases(i + 1, 1 - s)
                    divide(i + 1, 1 - s)

            in_steps(pool, step)

        @block.scalar
        def _(act):
            def turn_x(i, s):
                act.wait_ge(x_turned.sem, x_turned.at(i, 1))
                if behind(i, 2):
                    act.wait_ge(qk_ps_ready.sem, qk_ps_ready.at(i - 1, 0))
                nc.scalar.activation(xT[:, s, :], f0_ps[:, 0:128], ACT.Copy).then_inc(xT_ready.sem, 1)

            def exp(i, s):
                act.wait_ge(lowered.sem, lowered.at(i, 1))
                nc.scalar.activation(p[:, s, :, :], p[:, s, :, :], ACT.Exp, scale=dk ** -0.5).then_inc(exped.sem, 1)

            def copy_p(i, s, r):
                act.wait_ge(p_turned.sem, p_turned.at(i, r + 1))
                if r == 0:
                    if behind(i, 1):
                        act.wait_ge(mixed.sem, mixed.at(i - 1, 2))
                nc.scalar.activation(pT[:, per * r:per * (r + 1), :],
                                     turn_ps[0:S2, r % 2, :].rearrange("p (j t) -> p j t", t=128),
                                     ACT.Copy).then_inc(pT_ready.sem, 1)

            def copy_o(i, s, m):
                act.wait_ge(mixed.sem, mixed.at(i, m + 1))
                if m == 0:
                    if behind(i, 1):
                        act.wait_ge(y_ready.sem, y_ready.at(i - 1, 1))
                nc.scalar.activation(oT[:, half * m:half * (m + 1), :],
                                     (f1_ps, f0_ps)[m][:, :].rearrange("p (b t) -> p b t", t=128),
                                     ACT.Copy).then_inc(oT_ready.sem, 1)

            def step(i, s, stages):
                if "c" in stages:
                    copy_p(i, s, 0)
                    copy_p(i, s, 1)
                if "a" in stages:
                    turn_x(i + 2, s)
                if "c" in stages:
                    copy_p(i, s, 2)
                    copy_p(i, s, 3)
                if "b" in stages:
                    exp(i + 1, 1 - s)
                if "c" in stages:
                    copy_o(i, s, 0)
                    copy_o(i, s, 1)

            in_steps(act, step)

        @block.vector
        def _(dve):
            def normalise(i, s):
                if behind(i, 2):
                    dve.wait_ge(bo_added.sem, bo_added.at(i - 1, 0))
                if behind(i, 2):
                    dve.wait_ge(x_turned.sem, x_turned.at(i - 1, 0))
                nc.vector.tensor_scalar(xs[:, s, :], x[:, i, :], core.mean[:, ds(i, 1)],
                                        core.rstd[:, ds(i, 1)], ALU.subtract,
                                        ALU.mult).then_inc(x_normed.sem, 1)

            def add_qk(i, s):
                if behind(i, 2):
                    dve.wait_ge(scored.sem, scored.at(i - 1, 0))
                for n, (dst, bias, width) in enumerate(((q, "c_bq", 128), (q, "c_bq", 128),
                                                        (k, "c_bk", S2), (k, "c_bk", S2))):
                    rows = slice(half * (n % 2), half * (n % 2 + 1))
                    dve.wait_ge(qk_ps_ready.sem, qk_ps_ready.at(i, n + 1))
                    nc.vector.tensor_tensor(
                        dst[:, s, rows, :],
                        (f1_ps, f0_ps)[n % 2][:, 0:half * width].rearrange("p (b t) -> p b t", t=width),
                        core.w[bias][:, rows].unsqueeze(2).broadcast_to([128, half, width]),
                        ALU.add).then_inc(qk_ready.sem, 1)

            def add_v(i, s):
                for n in range(2):
                    cols = slice(512 * n, 512 * (n + 1))
                    dve.wait_ge(v_ps_ready.sem, v_ps_ready.at(i, n + 1))
                    if n == 0:
                        if behind(i, 2):
                            dve.wait_ge(mixed.sem, mixed.at(i - 2, 2))
                    nc.vector.tensor_tensor(v[:, s, cols], (f1_ps, f0_ps)[n][0:S2, :], core.w["c_bv"][0:S2, cols],
                                            ALU.add).then_inc(v_ready.sem, 1)

            def lower(i, s):
                dve.wait_ge(scored.sem, scored.at(i, 1))
                nc.vector.tensor_reduce(top[:, s, :].rearrange("p (r j) -> p r j", r=banks), scores,
                                        AX.X, ALU.max).then_inc(top_ready.sem, 1)
                dve.wait_ge(top_ready.sem, top_ready.at(i, 1))
                if behind(i, 2):
                    dve.wait_ge(p_turned.sem, p_turned.at(i - 1, 0))
                nc.vector.tensor_tensor(
                    p[:, s, :, :].rearrange("p (r j) s -> p r j s", r=banks), scores,
                    top[:, s, :].rearrange("p (r j) -> p r j", r=banks).unsqueeze(3).broadcast_to(
                        [128, banks, per, S2]), ALU.subtract).then_inc(lowered.sem, 1)

            def sums(i, s):
                dve.wait_ge(exped.sem, exped.at(i, 1))
                nc.vector.tensor_reduce(norm[:, s, :], p[:, s, :, :], AX.X, ALU.add).then_inc(norm_steps.sem, 1)
                dve.wait_ge(norm_steps.sem, norm_steps.at(i, 1))
                nc.vector.reciprocal(norm[:, s, :], norm[:, s, :]).then_inc(norm_steps.sem, 1)

            def inner_sum(i, s):
                dve.wait_ge(y_ready.sem, y_ready.at(i, 1))
                dve.wait_ge(bo_added.sem, bo_added.at(i, 1))
                if behind(i, 1):
                    dve.wait_ge(summed.sem, summed.at(i - 1, 1))
                nc.vector.tensor_tensor(inner[:, :], f1_ps[:, 0:128], xs_bo[:, s, :],
                                        ALU.add).then_inc(inner_steps.sem, 1)
                dve.wait_ge(inner_steps.sem, inner_steps.at(i, 1))
                nc.vector.bn_stats(inner_stats[:, :], inner[:, :]).then_inc(inner_steps.sem, 1)
                dve.wait_ge(inner_steps.sem, inner_steps.at(i, 2))
                nc.vector.memset(spare[:, :], 0.0)
                nc.vector.bn_aggr(inner_mv[:, :], inner_stats[:, :]).then_inc(inner_steps.sem, 1)

            def inner_norm(i, s):
                dve.wait_ge(inner_rstd.sem, inner_rstd.at(i, 1))
                nc.vector.tensor_scalar(inner[:, :], inner[:, :], inner_mv[:, 0:1], inner_mv[:, 1:2],
                                        ALU.subtract, ALU.mult).then_inc(inner_steps.sem, 1)

            def leave_sum(i, s):
                dve.wait_ge(summed.sem, summed.at(i, 1))
                nc.vector.bn_stats(stats[:, s, :], total[:, :]).then_inc(left_steps.sem, 1)
                nc.vector.tensor_copy(core.x[:, i, :], total[:, :]).then_inc(left_steps.sem, 1)
                dve.wait_ge(left_steps.sem, left_steps.at(i, 2))
                nc.vector.tensor_copy(core.stats[:, i, :], stats[:, s, :]).then_inc(left_steps.sem, 1)

            def step(i, s, stages):
                if "d" in stages:
                    inner_sum(i - 1, 1 - s)
                if "a" in stages:
                    normalise(i + 2, s)
                if "b" in stages:
                    lower(i + 1, 1 - s)
                if "d" in stages:
                    inner_norm(i - 1, 1 - s)
                if "a" in stages:
                    add_qk(i + 2, s)
                if "b" in stages:
                    sums(i + 1, 1 - s)
                if "d" in stages:
                    leave_sum(i - 1, 1 - s)
                if "a" in stages:
                    add_v(i + 2, s)

            in_steps(dve, step)

        @block.tensor
        def _(pe):
            def turn_x(i, s):
                pe.wait_ge(x_normed.sem, x_normed.at(i, 1))
                if behind(i, 1):
                    pe.wait_ge(v_ready.sem, v_ready.at(i - 1, 2))
                nc.tensor.transpose(f0_ps[:, 0:128], xs[:, s, :], core.ident[:, :]).then_inc(x_turned.sem, 1)

            def project_qk(i, s):
                pe.wait_ge(xT_ready.sem, xT_ready.at(i, 1))
                pe.wait_ge(loaded.sem, loaded.at(i, 16))
                if behind(i, 3):
                    pe.wait_ge(inner_steps.sem, inner_steps.at(i - 3, 1))
                for n, (weights, rhs, width) in enumerate((("c_wq", xT, 128), ("c_wq", xT, 128),
                                                           ("c_wk", ctxT, S2), ("c_wk", ctxT, S2))):
                    if n >= 2:
                        pe.wait_ge(qk_ready.sem, qk_ready.at(i, n - 1))
                    for b in range(half):
                        cols = 128 * (half * (n % 2) + b)
                        last = nc.tensor.matmul((f1_ps, f0_ps)[n % 2][:, width * b:width * (b + 1)],
                                                core.w[weights][:, cols:cols + 128], rhs[:, s, :],
                                                start=True, stop=True)
                    last.then_inc(qk_ps_ready.sem, 1)

            def project_v(i, s):
                pe.wait_ge(qk_ready.sem, qk_ready.at(i, 4))
                if behind(i, 2):
                    pe.wait_ge(oT_ready.sem, oT_ready.at(i - 2, 2))
                for n in range(2):
                    nc.tensor.matmul((f1_ps, f0_ps)[n][0:S2, :], ctxT[:, s, :],
                                     core.w["c_wv"][:, 512 * n:512 * (n + 1)],
                                     start=True, stop=True).then_inc(v_ps_ready.sem, 1)

            def score(i, s):
                pe.wait_ge(qk_ready.sem, qk_ready.at(i, 4))
                if behind(i, 1):
                    pe.wait_ge(lowered.sem, lowered.at(i - 1, 1))
                for j in range(per):
                    for r in range(banks):
                        h = head_of(r, j)
                        rows = slice(dk * (h % 2), dk * (h % 2 + 1))
                        last = nc.tensor.matmul(s_ps[:, r, S2 * j:S2 * (j + 1)], q[rows, s, h // 2, :],
                                                k[rows, s, h // 2, :], start=True, stop=True)
                last.then_inc(scored.sem, 1)

            def turn_p(i, s, r):
                if r == 0:
                    pe.wait_ge(divided.sem, divided.at(i, 1))
                if r < 2:
                    if behind(i, 1):
                        pe.wait_ge(pT_ready.sem, pT_ready.at(i - 1, r + 3))
                else:
                    pe.wait_ge(pT_ready.sem, pT_ready.at(i, r - 1))
                for j in range(per):
                    last = nc.tensor.transpose(turn_ps[0:S2, r % 2, j * 128:(j + 1) * 128],
                                               p[:, s, per * r + j, :], core.ident[:, :])
                last.then_inc(p_turned.sem, 1)

            def mix(i, s, more):
                pe.wait_ge(v_ready.sem, v_ready.at(i, 2))
                if behind(i, 1):
                    pe.wait_ge(inner_steps.sem, inner_steps.at(i - 1, 1))
                if behind(i, 1):
                    pe.wait_ge(oT_ready.sem, oT_ready.at(i - 1, 2))
                if more:
                    pe.wait_ge(qk_ready.sem, qk_ready.at(i + 2, 4))
                for m in range(2):
                    pe.wait_ge(pT_ready.sem, pT_ready.at(i, 2 * m + 2))
                    for j in range(per):
                        for r in (2 * m, 2 * m + 1):
                            h = head_of(r, j)
                            rows = slice(dk * (h % 2), dk * (h % 2 + 1))
                            last = nc.tensor.matmul((f1_ps, f0_ps)[m][rows, 128 * j:128 * (j + 1)],
                                                    v[:, s, dk * h:dk * (h + 1)], pT[:, per * r + j, :],
                                                    start=True, stop=True)
                    last.then_inc(mixed.sem, 1)

            def project_out(i, s, more):
                pe.wait_ge(oT_ready.sem, oT_ready.at(i, 2))
                if more:
                    pe.wait_ge(v_ready.sem, v_ready.at(i + 2, 1))
                for b in range(blocks):
                    last = nc.tensor.matmul(f1_ps[:, 0:128], oT[:, b, :], core.w["c_wo"][:, b, :],
                                            start=(b == 0), stop=(b == blocks - 1))
                last.then_inc(y_ready.sem, 1)

            def step(i, s, stages):
                if "b" in stages:
                    score(i + 1, 1 - s)
                if "c" in stages:
                    turn_p(i, s, 0)
                    turn_p(i, s, 1)
                if "a" in stages:
                    turn_x(i + 2, s)
                if "c" in stages:
                    turn_p(i, s, 2)
                    turn_p(i, s, 3)
                if "a" in stages:
                    project_qk(i + 2, s)
                if "c" in stages:
                    mix(i, s, "a" in stages)
                if "a" in stages:
                    project_v(i + 2, s)
                if "c" in stages:
                    project_out(i, s, "a" in stages)

            in_steps(pe, step)


def phase_quantised(core):
    nc = core.nc
    x = core.x
    inner_blocks = 4
    inner = inner_blocks * 128
    to_whole = 1.5 * 2.0 ** 23
    names = ("q_wg", "q_wu", "q_wd")
    with ExitStack() as ctx:
        def sb(name, shape, dt=F32):
            return ctx.enter_context(nc.sbuf_tensor(name, shape, dt))

        def ps(name, shape, dt=F32):
            return ctx.enter_context(nc.psum_tensor(name, shape, dt))

        signals = []

        def sig(name, per_pass=1):
            signals.append(Signal(ctx.enter_context(nc.semaphore(name)), per_pass))
            return signals[-1]

        ones = sb("q_ones", [128, 128])
        ident16 = sb("q_ident16", [128, 128], BF16)
        w_sum = sb("q_w_sum", [128, 3])
        w_mean = sb("q_w_mean", [128, 3])
        w_scale = sb("q_w_scale", [128, 3])
        w_scaled = sb("q_w_scaled", [128, 3, inner])
        ternary = sb("q_ternary", [128, 3, inner], BF16)
        xs = sb("q_xs", [128, 2, 128])
        x_top = sb("q_x_top", [128, 2])
        x_scale = sb("q_x_scale", [128, 2])
        x_back = sb("q_x_back", [128, 2, 2])
        x_scaled = sb("q_x_scaled", [128, 2, 128])
        xq = sb("q_xq", [128, 2, 128], BF16)
        xqT = sb("q_xqT", [128, 2, 128], BF16)
        silu = sb("q_silu", [128, 2, inner])
        h = sb("q_h", [128, 2, inner])
        h_top = sb("q_h_top", [128, 2])
        h_scale = sb("q_h_scale", [128, 2])
        h_back = sb("q_h_back", [128, 2])
        hq = sb("q_hq", [128, 2, inner], BF16)
        hqT = sb("q_hqT", [128, 2, inner], BF16)
        total = sb("q_total", [128, 2, 128])
        stats = sb("q_stats", [128, 2, 6])

        sum_ps = ps("q_sum_ps", [128, 3])
        xT_ps = ps("q_xT_ps", [128, 128], BF16)
        g_ps = ps("q_g_ps", [128, inner])
        u_ps = ps("q_u_ps", [128, inner])
        hT_ps = ps("q_hT_ps", [128, inner], BF16)
        o_ps = ps("q_o_ps", [128, 128])

        ones_ready = sig("q_ones_ready")
        prep_steps = sig("q_prep_steps", 6)
        sum_ready = sig("q_sum_ready")
        x_steps = sig("q_x_steps", 8)
        x_turned = sig("q_x_turned")
        xT_ready = sig("q_xT_ready")
        gu_ready = sig("q_gu_ready")
        silu_ready = sig("q_silu_ready")
        h_steps = sig("q_h_steps", 7)
        h_turned = sig("q_h_turned")
        hT_ready = sig("q_hT_ready")
        o_ready = sig("q_o_ready")
        left_steps = sig("q_left_steps", 3)

        open_signals(nc, signals, [core.landed["q"]])
        block = ctx.enter_context(nc.Block())

        @block.gpsimd
        def _(pool):
            nc.gpsimd.memset(ones[:, :], 1.0).then_inc(ones_ready.sem, 1)

        @block.scalar
        def _(act):
            def copy_x(i, s):
                act.wait_ge(x_turned.sem, x_turned.at(i, 1))
                if behind(i, 2):
                    act.wait_ge(gu_ready.sem, gu_ready.at(i - 1, 0))
                nc.scalar.activation(xqT[:, s, :], xT_ps[:, :], ACT.Copy).then_inc(xT_ready.sem, 1)

            def gate(i, s):
                act.wait_ge(gu_ready.sem, gu_ready.at(i, 1))
                if behind(i, 2):
                    act.wait_ge(h_steps.sem, h_steps.at(i - 1, 0))
                nc.scalar.activation(silu[:, s, :], g_ps[:, :], ACT.Silu,
                                     scale=x_back[:, s, 0:1]).then_inc(silu_ready.sem, 1)

            def copy_h(i, s):
                act.wait_ge(h_turned.sem, h_turned.at(i, 1))
                if behind(i, 2):
                    act.wait_ge(o_ready.sem, o_ready.at(i - 1, 0))
                nc.scalar.activation(hqT[:, s, :], hT_ps[:, :], ACT.Copy).then_inc(hT_ready.sem, 1)

            def step(i, s, stages):
                if "b" in stages:
                    gate(i + 1, 1 - s)
                if "c" in stages:
                    copy_h(i, s)
                if "a" in stages:
                    copy_x(i + 2, s)

            in_steps(act, step)

        @block.vector
        def _(dve):
            for n, name in enumerate(names):
                last = nc.vector.tensor_reduce(w_sum[:, n:n + 1], core.w[name][:, :], AX.X, ALU.add,
                                               apply_absolute_value=True)
            last.then_inc(prep_steps.sem, 1)
            nc.vector.tensor_copy(ident16[:, :], core.ident[:, :])
            dve.wait_ge(sum_ready.sem, sum_ready.at(0, 1))
            nc.vector.tensor_scalar(w_mean[:, :], sum_ps[:, :], 1.0 / (D * inner), 1e-5, ALU.mult,
                                    ALU.max).then_inc(prep_steps.sem, 1)
            dve.wait_ge(prep_steps.sem, prep_steps.at(0, 2))
            nc.vector.reciprocal(w_scale[:, :], w_mean[:, :]).then_inc(prep_steps.sem, 1)
            dve.wait_ge(prep_steps.sem, prep_steps.at(0, 3))
            for n, name in enumerate(names):
                last = nc.vector.tensor_scalar(w_scaled[:, n, :], core.w[name][:, :], w_scale[:, n:n + 1], to_whole,
                                               ALU.mult, ALU.add)
            last.then_inc(prep_steps.sem, 1)
            dve.wait_ge(prep_steps.sem, prep_steps.at(0, 4))
            nc.vector.tensor_scalar(w_scaled[:, :, :], w_scaled[:, :, :], to_whole, 1.0, ALU.subtract,
                                    ALU.min).then_inc(prep_steps.sem, 1)
            dve.wait_ge(prep_steps.sem, prep_steps.at(0, 5))
            nc.vector.tensor_scalar(ternary[:, :, :], w_scaled[:, :, :], -1.0, None,
                                    ALU.max).then_inc(prep_steps.sem, 1)

            def quantise_x(i, s):
                if behind(i, 2):
                    dve.wait_ge(left_steps.sem, left_steps.at(i - 1, 0))
                nc.vector.tensor_scalar(xs[:, s, :], x[:, i, :], core.mean[:, ds(i, 1)],
                                        core.rstd[:, ds(i, 1)], ALU.subtract, ALU.mult).then_inc(x_steps.sem, 1)
                dve.wait_ge(x_steps.sem, x_steps.at(i, 1))
                nc.vector.tensor_reduce(x_top[:, s:s + 1], xs[:, s, :], AX.X, ALU.max,
                                        apply_absolute_value=True).then_inc(x_steps.sem, 1)
                dve.wait_ge(x_steps.sem, x_steps.at(i, 2))
                nc.vector.tensor_scalar(x_top[:, s:s + 1], x_top[:, s:s + 1], 1e-5, 1.0 / 127.0, ALU.max,
                                        ALU.mult).then_inc(x_steps.sem, 1)
                dve.wait_ge(x_steps.sem, x_steps.at(i, 3))
                nc.vector.reciprocal(x_scale[:, s:s + 1], x_top[:, s:s + 1]).then_inc(x_steps.sem, 1)
                if behind(i, 2):
                    dve.wait_ge(silu_ready.sem, silu_ready.at(i - 1, 0))
                nc.vector.tensor_tensor(x_back[:, s, :], w_mean[:, 0:2],
                                        x_top[:, s:s + 1].broadcast_to([128, 2]), ALU.mult).then_inc(x_steps.sem, 1)
                dve.wait_ge(x_steps.sem, x_steps.at(i, 5))
                nc.vector.tensor_scalar(x_scaled[:, s, :], xs[:, s, :], x_scale[:, s:s + 1], to_whole,
                                        ALU.mult, ALU.add).then_inc(x_steps.sem, 1)
                dve.wait_ge(x_steps.sem, x_steps.at(i, 6))
                if behind(i, 2):
                    dve.wait_ge(x_turned.sem, x_turned.at(i - 1, 0))
                nc.vector.tensor_scalar(xq[:, s, :], x_scaled[:, s, :], to_whole, 127.0, ALU.subtract,
                                        ALU.min).then_inc(x_steps.sem, 2)

            def hidden(i, s):
                dve.wait_ge(silu_ready.sem, silu_ready.at(i, 1))
                nc.vector.scalar_tensor_tensor(h[:, s, :], u_ps[:, :], x_back[:, s, 1:2], silu[:, s, :],
                                               ALU.mult, ALU.mult).then_inc(h_steps.sem, 1)
                dve.wait_ge(h_steps.sem, h_steps.at(i, 1))
                nc.vector.tensor_reduce(h_top[:, s:s + 1], h[:, s, :], AX.X, ALU.max,
                                        apply_absolute_value=True).then_inc(h_steps.sem, 1)
                dve.wait_ge(h_steps.sem, h_steps.at(i, 2))
                nc.vector.tensor_scalar(h_top[:, s:s + 1], h_top[:, s:s + 1], 1e-5, 1.0 / 127.0, ALU.max,
                                        ALU.mult).then_inc(h_steps.sem, 1)
                dve.wait_ge(h_steps.sem, h_steps.at(i, 3))
                nc.vector.reciprocal(h_scale[:, s:s + 1], h_top[:, s:s + 1]).then_inc(h_steps.sem, 1)
                if behind(i, 2):
                    dve.wait_ge(left_steps.sem, left_steps.at(i - 1, 0))
                nc.vector.tensor_tensor(h_back[:, s:s + 1], w_mean[:, 2:3], h_top[:, s:s + 1],
                                        ALU.mult).then_inc(h_steps.sem, 1)
                dve.wait_ge(h_steps.sem, h_steps.at(i, 5))
                nc.vector.tensor_scalar(h[:, s, :], h[:, s, :], h_scale[:, s:s + 1], to_whole,
                                        ALU.mult, ALU.add).then_inc(h_steps.sem, 1)
                dve.wait_ge(h_steps.sem, h_steps.at(i, 6))
                if behind(i, 2):
                    dve.wait_ge(h_turned.sem, h_turned.at(i - 1, 0))
                nc.vector.tensor_scalar(hq[:, s, :], h[:, s, :], to_whole, 127.0, ALU.subtract,
                                        ALU.min).then_inc(h_steps.sem, 1)

            def add_up(i, s):
                dve.wait_ge(o_ready.sem, o_ready.at(i, 1))
                nc.vector.scalar_tensor_tensor(total[:, s, :], o_ps[:, :], h_back[:, s:s + 1], xs[:, s, :],
                                               ALU.mult, ALU.add).then_inc(left_steps.sem, 1)
                leave_one(dve, nc, core, i, left_steps, total[:, s, :], stats[:, s, :])

            def step(i, s, stages):
                if "b" in stages:
                    hidden(i + 1, 1 - s)
                if "c" in stages:
                    add_up(i, s)
                if "a" in stages:
                    quantise_x(i + 2, s)

            in_steps(dve, step)

        @block.tensor
        def _(pe):
            pe.wait_ge(ones_ready.sem, ones_ready.at(0, 1))
            pe.wait_ge(prep_steps.sem, prep_steps.at(0, 1))
            nc.tensor.matmul(sum_ps[:, :], ones[:, :], w_sum[:, :], start=True, stop=True).then_inc(sum_ready.sem, 1)
            pe.wait_ge(prep_steps.sem, prep_steps.at(0, 6))

            def turn_x(i, s):
                pe.wait_ge(x_steps.sem, x_steps.at(i, 8))
                if behind(i, 1):
                    pe.wait_ge(xT_ready.sem, xT_ready.at(i - 1, 1))
                nc.tensor.transpose(xT_ps[:, :], xq[:, s, :], ident16[:, :]).then_inc(x_turned.sem, 1)

            def up(i, s):
                pe.wait_ge(xT_ready.sem, xT_ready.at(i, 1))
                if behind(i, 1):
                    pe.wait_ge(silu_ready.sem, silu_ready.at(i - 1, 1))
                if behind(i, 1):
                    pe.wait_ge(h_steps.sem, h_steps.at(i - 1, 1))
                nc.tensor.matmul(g_ps[:, :], xqT[:, s, :], ternary[:, 0, :], start=True, stop=True)
                nc.tensor.matmul(u_ps[:, :], xqT[:, s, :], ternary[:, 1, :],
                                 start=True, stop=True).then_inc(gu_ready.sem, 1)

            def turn_h(i, s):
                pe.wait_ge(h_steps.sem, h_steps.at(i, 7))
                if behind(i, 1):
                    pe.wait_ge(hT_ready.sem, hT_ready.at(i - 1, 1))
                for b in range(inner_blocks):
                    cols = slice(128 * b, 128 * (b + 1))
                    last = nc.tensor.transpose(hT_ps[:, cols], hq[:, s, cols], ident16[:, :])
                last.then_inc(h_turned.sem, 1)

            def down(i, s):
                pe.wait_ge(hT_ready.sem, hT_ready.at(i, 1))
                if behind(i, 1):
                    pe.wait_ge(left_steps.sem, left_steps.at(i - 1, 1))
                for b in range(inner_blocks):
                    cols = slice(128 * b, 128 * (b + 1))
                    last = nc.tensor.matmul(o_ps[:, :], hqT[:, s, cols], ternary[:, 2, cols],
                                            start=(b == 0), stop=(b == inner_blocks - 1))
                last.then_inc(o_ready.sem, 1)

            def step(i, s, stages):
                if "b" in stages:
                    up(i + 1, 1 - s)
                if "c" in stages:
                    turn_h(i, s)
                    down(i, s)
                if "a" in stages:
                    turn_x(i + 2, s)

            in_steps(pe, step)


def phase_out(core):
    nc = core.nc
    x = core.x
    with ExitStack() as ctx:
        normed = ctx.enter_context(nc.semaphore("z_normed"))
        stored = ctx.enter_context(nc.semaphore("z_stored"))
        block = ctx.enter_context(nc.Block())

        @block.vector
        def _(dve):
            with dve.Fori(0, NG) as g:
                for j in range(GB):
                    last = nc.vector.tensor_scalar(x[:, g * GB + j, :], x[:, g * GB + j, :],
                                                   core.mean[:, ds(g * GB + j, 1)],
                                                   core.rstd[:, ds(g * GB + j, 1)],
                                                   ALU.subtract, ALU.mult)
                last.then_inc(normed, 1)

        @block.sync
        def _(sp):
            with sp.Fori(0, NG) as g:
                sp.wait_ge(normed, g + 1)
                sp.dma_start(core.out[ds(g * GB, GB), :, :].rearrange("b t d -> t b d"),
                             x[:, ds(g * GB, GB), :]).then_inc(stored, 16)
            sp.wait_ge(stored, 16 * NG)


def build(nc, ins, out):
    with ExitStack() as ctx:
        core = Core(nc, ctx, ins, out)
        core.x = core.sb("x", [128, B, 128])
        core.stats = core.sb("stats", [128, B, 6])
        core.mean = core.sb("mean", [128, B])
        core.rstd = core.sb("rstd", [128, B])
        core.minus_half = core.sb("minus_half", [128, B])
        core.euler = core.sb("euler", [128, 32])
        core.ln_eps = core.sb("ln_eps", [128, 1])
        core.neg_rate = core.sb("neg_rate", [128, 2, 16])
        core.rms_eps = core.sb("rms_eps", [128, 2 * GB])
        core.w = {}
        core.landed = {phase: Landed(ctx.enter_context(nc.semaphore(f"weights_{phase}")), len(names))
                       for phase, names in WEIGHTS.items()}

        def place(phases, within):
            for phase in phases:
                for name in WEIGHTS[phase]:
                    core.w[name] = within.enter_context(nc.sbuf_tensor(f"w_{name}", list(ins[name].shape), F32))

        place("scq", ctx)
        with ExitStack() as layer0:
            place("abm", layer0)
            core.ident, core.upper = core.w["ident"], core.w["upper"]
            setup(core)
            run_phase(core, "a", phase_aft)
            run_phase(core, "b", phase_cross0)
            run_phase(core, "m", phase_moe)
        run_phase(core, "s", phase_scan)
        run_phase(core, "c", phase_cross1)
        run_phase(core, "q", phase_quantised)
        phase_out(core)


def run_phase(core, name, phase):
    if PHASES.index(name) < LAST_PHASE:
        phase(core)
        finish_statistics(core, name)


class Landed:

    def __init__(self, sem, count):
        self.sem = sem
        self.value = 16 * count


PHASES = "abmscq"
WEIGHTS = {
    "a": ["a_wqkvT", "a_wuvT", "a_woutT", "upper"],
    "b": ["b_wq", "b_wk", "b_wv", "b_wo", "b_bq", "b_bk", "b_bv", "b_bo", "head_mask"],
    "m": ["m_router", "m_bias", "m_earlier", "m_w1", "m_w3", "m_w2"],
    "s": ["ident", "s_bo", "s_b_in", "s_dt_bias", "s_A_log", "s_pick", "s_conv_w", "s_conv_b", "s_D", "s_w_in",
          "s_x_proj", "s_dt_proj", "s_w_out"],
    "c": ["c_bo", "c_beta", "c_gamma", "c_bq", "c_bk", "c_bv", "c_wq", "c_wk", "c_wv", "c_wo"],
    "q": ["q_wg", "q_wu", "q_wd"],
}


def layout(inputs):
    def c(a):
        return np.ascontiguousarray(a)

    i = {k: np.asarray(v) for k, v in inputs.items()}

    def up(name):
        both = np.concatenate([i["L0_ffn_s" + name], i["L0_ffn_" + name]])
        return c(both.reshape(20, 128, 128).transpose(2, 0, 1))

    head_mask = np.tile(np.kron(np.eye(4), np.ones((8, 1))) * 8 ** -0.5, (4, 1)).astype(np.float32)
    return {
        "x": c(i["x"]),
        "ident": np.eye(128, dtype=np.float32),
        "upper": np.triu(np.ones((128, 128), np.float32)),
        "a_wqkvT": c(i["L0_attn_w_qkv"].T),
        "a_wuvT": c(i["L0_attn_w_swiglu"].T),
        "a_woutT": c(i["L0_attn_w_out"].T),
        "ctxT": c(i["ctx_1024"].transpose(2, 0, 1)),
        "fside": c(i["fside_BxSxS2_0"]),
        "mask": c(i["mask_BxSxS2_ff0"]),
        "b_wq": c(i["L0_xattn_Wq"]),
        "b_wk": c(i["L0_xattn_Wk"]),
        "b_wv": c(i["L0_xattn_Wv"]),
        "b_wo": c(i["L0_xattn_Wo"]),
        "b_bq": c(i["L0_xattn_bq"].reshape(128, 1)),
        "b_bk": c(i["L0_xattn_bk"].reshape(128, 1)),
        "b_bv": c(np.tile(i["L0_xattn_bv"], (128, 1))),
        "b_bo": c(np.tile(i["L0_xattn_bo"], (128, 1))),
        "head_mask": head_mask,
        "s_bo": c(np.tile(i["L1_attn_b_out"], (128, 1))),
        "s_b_in": c(i["L1_attn_b_in"].reshape(4, 128).T),
        "s_dt_bias": c(i["L1_attn_dt_bias"].reshape(2, 128).T),
        "s_A_log": c(i["L1_attn_A_log"].reshape(2, 128, 16).transpose(1, 0, 2)),
        "s_pick": c(np.tile(np.eye(32, dtype=np.float32), (3, 1))),
        "s_conv_w": c(i["L1_attn_conv_w"].reshape(2, 128, 4).transpose(1, 0, 2)),
        "s_conv_b": c(i["L1_attn_conv_b"].reshape(2, 128).T),
        "s_D": c(i["L1_attn_D_param"].reshape(2, 128).T),
        "s_w_in": c(i["L1_attn_W_in"]),
        "s_x_proj": c(i["L1_attn_x_proj_w"].reshape(2, 128, 48).transpose(1, 0, 2)),
        "s_dt_proj": c(i["L1_attn_dt_proj_w"]),
        "s_w_out": c(i["L1_attn_W_out"].reshape(2, 128, 128).transpose(1, 0, 2)),
        "c_bo": c(np.tile(i["L1_xattn_bo"], (128, 1))),
        "c_beta": c(np.tile(i["L1_xattn_ln_beta"], (128, 1))),
        "c_gamma": c(np.tile(i["L1_xattn_ln_gamma"], (128, 1))),
        "c_bq": c(i["L1_xattn_bq"].reshape(8, 128).T),
        "c_bk": c(i["L1_xattn_bk"].reshape(8, 128).T),
        "c_bv": c(np.tile(i["L1_xattn_bv"], (128, 1))),
        "c_wq": c(i["L1_xattn_Wq"]),
        "c_wk": c(i["L1_xattn_Wk"]),
        "c_wv": c(i["L1_xattn_Wv"]),
        "c_wo": c(i["L1_xattn_Wo"].reshape(8, 128, 128).transpose(1, 0, 2)),
        "q_wg": c(i["L1_ffn_w_gate"].T),
        "q_wu": c(i["L1_ffn_w_up"].T),
        "q_wd": c(i["L1_ffn_w_down"].reshape(128, 4, 128).transpose(2, 1, 0).reshape(128, 512)),
        "m_router": c(i["L0_ffn_router_w"].T),
        "m_bias": c(np.tile(i["L0_ffn_expert_bias"], (128, 1))),
        "m_earlier": c(np.tile(np.tril(np.ones((8, 8), np.float32), -1).reshape(1, 64), (128, 1))),
        "m_w1": up("w1"),
        "m_w3": up("w3"),
        "m_w2": c(np.concatenate([i["L0_ffn_sw2"], i["L0_ffn_w2"]]).transpose(0, 2, 1).reshape(20, 128, 128)
                  .transpose(1, 0, 2)),
    }


def kernel(**inputs):
    import concourse.bacc as _bacc
    from concourse.bass_utils import run_bass_kernel_spmd as _run

    nc = _bacc.Bacc("TRN2", target_bir_lowering=False, num_devices=1)
    arrays = layout(inputs)
    ins = {name: nc.dram_tensor(f"in_{name}_dram", a.shape, mybir.dt.from_np(a.dtype), kind="ExternalInput").ap()
           for name, a in arrays.items()}
    out = nc.dram_tensor("out_0_dram", (B, T, D), F32, kind="ExternalOutput").ap()
    build(nc, ins, out)
    r = _run(nc, [{f"in_{name}_dram": a for name, a in arrays.items()}], core_ids=[0])
    return r.results[0]["out_0_dram"]
```

```python
from contextlib import ExitStack

import numpy as np

import concourse.bass as bass
from concourse import mybir

F32 = mybir.dt.float32
BF16 = mybir.dt.bfloat16
ALU = mybir.AluOpType
ACT = mybir.ActivationFunctionType
AX = mybir.AxisListType
ds = bass.ds

B, T, D = 64, 128, 128
S2 = 77
GB = 4
NG = B // GB
GT = GB * T
LN_EPS = 1e-5
RMS_EPS = 1.1920929e-07


class Signal:

    def __init__(self, sem, per_pass=1):
        self.sem = sem
        self.per_pass = per_pass

    def at(self, done, k):
        return done * self.per_pass + k + 1


def behind(i, n):
    return not isinstance(i, int) or i >= n


def open_signals(nc, signals, landed):
    with nc.Block() as block:

        @block.sync
        def _(sp):
            for weights in landed:
                sp.wait_ge(weights.sem, weights.value)
            for signal in signals:
                sp.sem_inc(signal.sem, 1)


class Core:

    def __init__(self, nc, ctx, ins, out):
        self.nc, self.ctx, self.ins, self.out = nc, ctx, ins, out

    def sb(self, name, shape, dt=F32):
        return self.ctx.enter_context(self.nc.sbuf_tensor(name, shape, dt))


def setup(core):
    nc = core.nc
    with nc.Block() as block:

        @block.sync
        def _(sp):
            for phase in "a":
                for name in WEIGHTS[phase]:
                    sp.dma_start(core.w[name][:], core.ins[name]).then_inc(core.landed[phase].sem, 16)

        @block.scalar
        def _(act):
            for phase in "sbmcq":
                for name in WEIGHTS[phase]:
                    act.dma_start(core.w[name][:], core.ins[name]).then_inc(core.landed[phase].sem, 16)

        @block.gpsimd
        def _(pool):
            nc.gpsimd.memset(core.minus_half[:, :], -0.5)
            nc.gpsimd.memset(core.euler[:, :], float(np.e))
            nc.gpsimd.memset(core.ln_eps[:, :], LN_EPS)
            nc.gpsimd.memset(core.rms_eps[:, 0:GB], 4 * RMS_EPS)
            nc.gpsimd.memset(core.rms_eps[:, GB:2 * GB], RMS_EPS)


def finish_statistics(core, name):
    nc = core.nc
    half_n = D // 2
    with nc.sbuf_tensor(f"{name}_gap", [128, B], F32) as gap, nc.semaphore(f"{name}_folded") as folded, \
            nc.semaphore(f"{name}_rstd") as rstd_ready, nc.Block() as block:
        mean_even, spread_even = core.stats[:, :, 1], core.stats[:, :, 2]
        mean_odd, spread_odd = core.stats[:, :, 4], core.stats[:, :, 5]

        @block.vector
        def _(dve):
            nc.vector.tensor_tensor(gap[:, :], mean_even, mean_odd, ALU.subtract)
            nc.vector.tensor_tensor(core.mean[:, :], mean_even, mean_odd, ALU.add)
            nc.vector.tensor_tensor(core.rstd[:, :], spread_even, spread_odd, ALU.add).then_inc(folded, 1)
            dve.wait_ge(folded, 1)
            nc.vector.tensor_scalar(core.mean[:, :], core.mean[:, :], 0.5, None, ALU.mult)
            nc.vector.scalar_tensor_tensor(gap[:, :], gap[:, :], half_n / 2.0, gap[:, :],
                                           ALU.mult, ALU.mult).then_inc(folded, 1)
            dve.wait_ge(folded, 2)
            nc.vector.tensor_tensor(core.rstd[:, :], core.rstd[:, :], gap[:, :], ALU.add).then_inc(folded, 1)
            dve.wait_ge(folded, 3)
            nc.vector.tensor_scalar(core.rstd[:, :], core.rstd[:, :], 1.0 / D, LN_EPS,
                                    ALU.mult, ALU.add).then_inc(folded, 1)

        @block.gpsimd
        def _(pool):
            pool.wait_ge(folded, 4)
            nc.gpsimd.tensor_tensor(core.rstd[:, :], core.rstd[:, :], core.minus_half[:, 0:B],
                                    ALU.pow).then_inc(rstd_ready, 1)
            pool.wait_ge(rstd_ready, 1)


def leave(dve, nc, core, g, steps, total, stats):
    dve.wait_ge(steps.sem, steps.at(g, 1))
    for j in range(GB):
        last = nc.vector.bn_stats(stats[:, j, :], total[:, j, :])
    last.then_inc(steps.sem, 1)
    nc.vector.tensor_copy(core.x[:, ds(g * GB, GB), :], total[:, :, :])
    dve.wait_ge(steps.sem, steps.at(g, 2))
    nc.vector.tensor_copy(core.stats[:, ds(g * GB, GB), :], stats[:, :, :]).then_inc(steps.sem, 1)


def leave_one(dve, nc, core, i, steps, total, stats):
    dve.wait_ge(steps.sem, steps.at(i, 1))
    nc.vector.bn_stats(stats, total).then_inc(steps.sem, 1)
    nc.vector.tensor_copy(core.x[:, i, :], total)
    dve.wait_ge(steps.sem, steps.at(i, 2))
    nc.vector.tensor_copy(core.stats[:, i, :], stats).then_inc(steps.sem, 1)


def in_group_steps(eng, step):
    step(-2, "a")
    step(-1, "ab")
    step(0, "abc")
    with eng.Fori(1, NG - 2) as g:
        step(g, "abcd")
    step(NG - 2, "bcd")
    step(NG - 1, "cd")
    step(NG, "d")


def phase_aft(core):
    nc = core.nc
    x = core.x
    with ExitStack() as ctx:
        def sb(name, shape, dt=F32):
            return ctx.enter_context(nc.sbuf_tensor(name, shape, dt))

        def ps(name, shape, dt=F32):
            return ctx.enter_context(nc.psum_tensor(name, shape, dt))

        signals = []

        def sig(name, per_pass=1):
            signals.append(Signal(ctx.enter_context(nc.semaphore(name)), per_pass))
            return signals[-1]

        square = sb("a_square", [128, 3, GB, 128])
        x_ms = sb("a_x_ms", [128, GB])
        qk_ms = sb("a_qk_ms", [128, 2, GB])
        xn = sb("a_xn", [128, GB, 128])
        xnT = sb("a_xnT", [128, GT])
        th_q = sb("a_th_q", [128, GB, 128])
        w_kv = sb("a_w_kv", [128, 2, GB, 128])
        den = sb("a_den", [128, GT])
        gate = sb("a_gate", [128, GT])
        y = sb("a_y", [128, GT])
        yT = sb("a_yT", [128, GT])
        th_g = sb("a_th_g", [128, GT])
        h = sb("a_h", [128, GT])
        total = sb("a_total", [128, GB, 128])
        stats = sb("a_stats", [128, GB, 6])

        turn_ps = ps("a_turn_ps", [128, GT])
        q_ps = ps("a_q_ps", [128, GB, 128])
        k_ps = ps("a_k_ps", [128, GB, 128])
        v_ps = ps("a_v_ps", [128, GB, 128])
        wsum_ps = ps("a_wsum_ps", [128, GT])
        kvsum_ps = ps("a_kvsum_ps", [128, GT])
        u_ps = ps("a_u_ps", [128, GT])
        g_ps = ps("a_g_ps", [128, GT])
        o_ps = u_ps.rearrange("p (b d) -> p b d", b=GB)

        x_in = sig("a_x_in", 16)
        x_squared = sig("a_x_squared")
        x_eps = sig("a_x_eps")
        x_rms = sig("a_x_rms")
        x_normed = sig("a_x_normed")
        x_turned = sig("a_x_turned")
        xnT_ready = sig("a_xnT_ready")
        qkv_ready = sig("a_qkv_ready")
        qk_squared = sig("a_qk_squared")
        qk_eps = sig("a_qk_eps")
        qk_rms = sig("a_qk_rms")
        w_ready = sig("a_w_ready")
        th_q_ready = sig("a_th_q_ready")
        kv_ready = sig("a_kv_ready")
        sums_ready = sig("a_sums_ready")
        y_steps = sig("a_y_steps", 4)
        y_turned = sig("a_y_turned")
        yT_ready = sig("a_yT_ready")
        ug_ready = sig("a_ug_ready")
        th_g_ready = sig("a_th_g_ready")
        h_steps = sig("a_h_steps", 2)
        o_ready = sig("a_o_ready")
        x_steps = sig("a_x_steps", 3)

        open_signals(nc, signals, [core.landed["a"], core.landed["s"]])
        block = ctx.enter_context(nc.Block())

        @block.sync
        def _(sp):
            with sp.Fori(0, NG) as g:
                sp.wait_ge(x_in.sem, x_in.at(g, 0))
                sp.dma_start(x[:, ds(g * GB, GB), :],
                             core.ins["x"][ds(g * GB, GB), :, :].rearrange("b t d -> t b d")
                             ).then_inc(x_in.sem, 16)

        @block.gpsimd
        def _(pool):
            def x_rms_of(g):
                pool.wait_ge(x_squared.sem, x_squared.at(g, 1))
                nc.gpsimd.tensor_tensor(x_ms[:, :], x_ms[:, :], core.rms_eps[:, GB:2 * GB],
                                        ALU.add).then_inc(x_eps.sem, 1)
                pool.wait_ge(x_eps.sem, x_eps.at(g, 1))
                nc.gpsimd.tensor_tensor(x_ms[:, :], x_ms[:, :], core.minus_half[:, 0:GB],
                                        ALU.pow).then_inc(x_rms.sem, 1)

            def qk_rms_of(g):
                pool.wait_ge(qk_squared.sem, qk_squared.at(g, 1))
                nc.gpsimd.tensor_tensor(qk_ms[:, :, :].rearrange("p a b -> p (a b)"),
                                        qk_ms[:, :, :].rearrange("p a b -> p (a b)"),
                                        core.rms_eps[:, :], ALU.add).then_inc(qk_eps.sem, 1)
                pool.wait_ge(qk_eps.sem, qk_eps.at(g, 1))
                nc.gpsimd.tensor_tensor(qk_ms[:, :, :].rearrange("p a b -> p (a b)"),
                                        qk_ms[:, :, :].rearrange("p a b -> p (a b)"),
                                        core.minus_half[:, 0:2 * GB], ALU.pow).then_inc(qk_rms.sem, 1)

            def step(g, stages):
                if "a" in stages:
                    x_rms_of(g + 2)
                if "b" in stages:
                    qk_rms_of(g + 1)

            in_group_steps(pool, step)

        @block.scalar
        def _(act):
            def square_x(g):
                act.wait_ge(x_in.sem, x_in.at(g, 16))
                act.wait_ge(x_normed.sem, x_normed.at(g, 0))
                for j in range(GB):
                    last = nc.scalar.activation(square[:, 0, j, :], x[:, g * GB + j, :], ACT.Square,
                                                scale=D ** -0.5, accum_out=x_ms[:, j:j + 1])
                last.then_inc(x_squared.sem, 1)

            def copy_xnT(g):
                act.wait_ge(x_turned.sem, x_turned.at(g, 1))
                act.wait_ge(qkv_ready.sem, qkv_ready.at(g, 0))
                nc.scalar.activation(xnT[:, :], turn_ps[:, :], ACT.Copy).then_inc(xnT_ready.sem, 1)

            def square_qk(g):
                act.wait_ge(qkv_ready.sem, qkv_ready.at(g, 1))
                for j in range(GB):
                    nc.scalar.activation(square[:, 1, j, :], q_ps[:, j, :], ACT.Square,
                                         scale=2 * D ** -0.5, accum_out=qk_ms[:, 0, j:j + 1])
                for j in range(GB):
                    last = nc.scalar.activation(square[:, 2, j, :], k_ps[:, j, :], ACT.Square,
                                                scale=D ** -0.5, accum_out=qk_ms[:, 1, j:j + 1])
                last.then_inc(qk_squared.sem, 1)

            def exp_tanh(g):
                act.wait_ge(qk_rms.sem, qk_rms.at(g, 1))
                act.wait_ge(sums_ready.sem, sums_ready.at(g, 0))
                for j in range(GB):
                    last = nc.scalar.activation(w_kv[:, 0, j, :], k_ps[:, j, :], ACT.Exp,
                                                scale=qk_ms[:, 1, j:j + 1])
                last.then_inc(w_ready.sem, 1)
                act.wait_ge(y_steps.sem, y_steps.at(g, 0))
                for j in range(GB):
                    last = nc.scalar.activation(th_q[:, j, :], q_ps[:, j, :], ACT.Tanh,
                                                scale=qk_ms[:, 0, j:j + 1])
                last.then_inc(th_q_ready.sem, 1)

            def copy_yT(g):
                act.wait_ge(y_turned.sem, y_turned.at(g, 1))
                act.wait_ge(ug_ready.sem, ug_ready.at(g, 0))
                nc.scalar.activation(yT[:, :], wsum_ps[:, :], ACT.Copy).then_inc(yT_ready.sem, 1)

            def tanh_g(g):
                act.wait_ge(ug_ready.sem, ug_ready.at(g, 1))
                act.wait_ge(h_steps.sem, h_steps.at(g, 0))
                nc.scalar.activation(th_g[:, :], g_ps[:, :], ACT.Tanh, scale=0.5).then_inc(th_g_ready.sem, 1)

            def step(g, stages):
                if "a" in stages:
                    square_x(g + 2)
                if "b" in stages:
                    square_qk(g + 1)
                if "c" in stages:
                    copy_yT(g)
                if "b" in stages:
                    exp_tanh(g + 1)
                if "a" in stages:
                    copy_xnT(g + 2)
                if "c" in stages:
                    tanh_g(g)

            in_group_steps(act, step)

        @block.vector
        def _(dve):
            def normalise(g):
                dve.wait_ge(x_rms.sem, x_rms.at(g, 1))
                dve.wait_ge(x_turned.sem, x_turned.at(g, 0))
                for j in range(GB):
                    last = nc.vector.tensor_scalar(xn[:, j, :], x[:, g * GB + j, :], x_ms[:, j:j + 1],
                                                   None, ALU.mult)
                last.then_inc(x_normed.sem, 1)

            def weigh(g):
                dve.wait_ge(w_ready.sem, w_ready.at(g, 1))
                nc.vector.tensor_tensor(w_kv[:, 1, :, :], w_kv[:, 0, :, :], v_ps[:, :, :],
                                        ALU.mult).then_inc(kv_ready.sem, 1)

            def mean_y(g):
                dve.wait_ge(sums_ready.sem, sums_ready.at(g, 1))
                nc.vector.tensor_scalar(den[:, :], wsum_ps[:, :], 1e-6, None,
                                        ALU.add).then_inc(y_steps.sem, 1)
                dve.wait_ge(y_steps.sem, y_steps.at(g, 1))
                nc.vector.reciprocal(den[:, :], den[:, :]).then_inc(y_steps.sem, 1)
                dve.wait_ge(th_q_ready.sem, th_q_ready.at(g, 1))
                dve.wait_ge(y_steps.sem, y_steps.at(g, 2))
                nc.vector.scalar_tensor_tensor(gate[:, :], th_q[:, :, :].rearrange("p a b -> p (a b)"),
                                               1.0, den[:, :], ALU.add, ALU.mult).then_inc(y_steps.sem, 1)
                dve.wait_ge(y_steps.sem, y_steps.at(g, 3))
                dve.wait_ge(y_turned.sem, y_turned.at(g, 0))
                nc.vector.scalar_tensor_tensor(y[:, :], kvsum_ps[:, :], 0.5, gate[:, :],
                                               ALU.mult, ALU.mult).then_inc(y_steps.sem, 1)

            def hidden(g):
                dve.wait_ge(th_g_ready.sem, th_g_ready.at(g, 1))
                dve.wait_ge(o_ready.sem, o_ready.at(g, 0))
                nc.vector.scalar_tensor_tensor(th_g[:, :], th_g[:, :], 1.0, g_ps[:, :],
                                               ALU.add, ALU.mult).then_inc(h_steps.sem, 1)
                dve.wait_ge(h_steps.sem, h_steps.at(g, 1))
                nc.vector.scalar_tensor_tensor(h[:, :], th_g[:, :], 0.5, u_ps[:, :],
                                               ALU.mult, ALU.mult).then_inc(h_steps.sem, 1)

            def add_up(g):
                dve.wait_ge(o_ready.sem, o_ready.at(g, 1))
                nc.vector.scalar_tensor_tensor(total[:, :, :], x[:, ds(g * GB, GB), :], 2.0,
                                               o_ps[:, :, :], ALU.mult, ALU.add).then_inc(x_steps.sem, 1)
                leave(dve, nc, core, g, x_steps, total, stats)

            def step(g, stages):
                if "c" in stages:
                    mean_y(g)
                if "a" in stages:
                    normalise(g + 2)
                if "d" in stages:
                    add_up(g - 1)
                if "b" in stages:
                    weigh(g + 1)
                if "c" in stages:
                    hidden(g)

            in_group_steps(dve, step)

        @block.tensor
        def _(pe):
            def turn_x(g):
                pe.wait_ge(x_normed.sem, x_normed.at(g, 1))
                pe.wait_ge(xnT_ready.sem, xnT_ready.at(g, 0))
                for j in range(GB):
                    last = nc.tensor.transpose(turn_ps[:, j * 128:(j + 1) * 128], xn[:, j, :], core.ident[:, :])
                last.then_inc(x_turned.sem, 1)

            def project(g):
                pe.wait_ge(xnT_ready.sem, xnT_ready.at(g, 1))
                pe.wait_ge(th_q_ready.sem, th_q_ready.at(g, 0))
                pe.wait_ge(kv_ready.sem, kv_ready.at(g, 0))
                for which, bank in enumerate((q_ps, k_ps, v_ps)):
                    for j in range(GB):
                        last = nc.tensor.matmul(bank[:, j, :], xnT[:, j * 128:(j + 1) * 128],
                                                core.w["a_wqkvT"][:, which * 128:(which + 1) * 128],
                                                start=True, stop=True)
                last.then_inc(qkv_ready.sem, 1)

            def sum_up(g):
                pe.wait_ge(w_ready.sem, w_ready.at(g, 1))
                pe.wait_ge(y_steps.sem, y_steps.at(g, 0))
                pe.wait_ge(yT_ready.sem, yT_ready.at(g, 0))
                nc.tensor.matmul(wsum_ps[:, :], core.upper[:, :],
                                 w_kv[:, 0, :, :].rearrange("p a b -> p (a b)"), start=True, stop=True)
                pe.wait_ge(kv_ready.sem, kv_ready.at(g, 1))
                nc.tensor.matmul(kvsum_ps[:, :], core.upper[:, :],
                                 w_kv[:, 1, :, :].rearrange("p a b -> p (a b)"),
                                 start=True, stop=True).then_inc(sums_ready.sem, 1)

            def turn_y(g):
                pe.wait_ge(y_steps.sem, y_steps.at(g, 4))
                for j in range(GB):
                    last = nc.tensor.transpose(wsum_ps[:, j * 128:(j + 1) * 128],
                                               y[:, j * 128:(j + 1) * 128], core.ident[:, :])
                last.then_inc(y_turned.sem, 1)

            def up(g):
                pe.wait_ge(yT_ready.sem, yT_ready.at(g, 1))
                pe.wait_ge(h_steps.sem, h_steps.at(g, 0))
                nc.tensor.matmul(g_ps[:, :], core.w["a_wuvT"][:, 128:256], yT[:, :], start=True, stop=True)
                if behind(g, 1):
                    pe.wait_ge(x_steps.sem, x_steps.at(g - 1, 1))
                nc.tensor.matmul(u_ps[:, :], core.w["a_wuvT"][:, 0:128], yT[:, :],
                                 start=True, stop=True).then_inc(ug_ready.sem, 1)

            def down(g):
                pe.wait_ge(h_steps.sem, h_steps.at(g, 2))
                for j in range(GB):
                    last = nc.tensor.matmul(o_ps[:, j, :], h[:, j * 128:(j + 1) * 128],
                                            core.w["a_woutT"][:, :], start=True, stop=True)
                last.then_inc(o_ready.sem, 1)

            def step(g, stages):
                if "b" in stages:
                    project(g + 1)
                if "c" in stages:
                    turn_y(g)
                if "a" in stages:
                    turn_x(g + 2)
                if "c" in stages:
                    up(g)
                if "b" in stages:
                    sum_up(g + 1)
                if "c" in stages:
                    down(g)

            in_group_steps(pe, step)


def in_steps(eng, step):
    step(-2, 0, "a")
    step(-1, 1, "ab")
    step(0, 0, "abc")
    with eng.Fori(1, B - 4, 2) as i:
        step(i, 1, "abcd")
        step(i + 1, 0, "abcd")
    step(B - 3, 1, "abcd")
    step(B - 2, 0, "bcd")
    step(B - 1, 1, "cd")
    step(B, 0, "d")


def phase_cross0(core):
    nc = core.nc
    x = core.x
    heads, dk, quads = 16, 8, 4
    per = heads // quads
    with ExitStack() as ctx:
        def sb(name, shape, dt=F32):
            return ctx.enter_context(nc.sbuf_tensor(name, shape, dt))

        def ps(name, shape, dt=F32):
            return ctx.enter_context(nc.psum_tensor(name, shape, dt))

        signals = []

        def sig(name, per_pass=1):
            signals.append(Signal(ctx.enter_context(nc.semaphore(name)), per_pass))
            return signals[-1]

        ctxT = sb("b_ctxT", [128, 2, S2])
        side = sb("b_side", [128, 2, 2, S2])
        side_sum = sb("b_side_sum", [128, 2, S2])
        xs = sb("b_xs", [128, 2, 128])
        xs_bo = sb("b_xs_bo", [128, 2, 128])
        xT = sb("b_xT", [128, 2, 128])
        qT = sb("b_qT", [128, 2, 128])
        k_own = sb("b_k_own", [128, 2, per, S2])
        v = sb("b_v", [S2, 2, 128])
        p = sb("b_p", [128, 2, heads, S2])
        pT = sb("b_pT", [S2, 2, heads, 128])
        top = sb("b_top", [128, 2, heads])
        norm = sb("b_norm", [128, 2, heads])
        c = sb("b_c", [128, 2, 128])
        cT = sb("b_cT", [128, 2, 128])
        total = sb("b_total", [128, 2, 128])
        stats = sb("b_stats", [128, 2, 6])

        s_ps = ps("b_s_ps", [128, quads, 512])
        turn_ps = ps("b_turn_ps", [128, 2, 512])
        in_ps = ps("b_in_ps", [128, 512])
        out_ps = ps("b_out_ps", [128, 512])
        xT_ps, q_ps, k_ps = in_ps[:, 384:512], in_ps[:, 0:128], in_ps[:, 128:128 + S2]
        v_ps = in_ps[0:S2, 256:384]
        c_ps, cT_ps, y_ps = out_ps[:, 0:128], out_ps[:, 128:256], out_ps[:, 256:384]
        scores = s_ps[:, :, 0:per * S2].rearrange("p r (j s) -> p r j s", s=S2)

        loaded = sig("b_loaded", 48)
        side_ready = sig("b_side_ready")
        x_normed = sig("b_x_normed")
        bo_added = sig("b_bo_added")
        x_turned = sig("b_x_turned")
        xT_ready = sig("b_xT_ready")
        projected = sig("b_projected")
        k_ready = sig("b_k_ready")
        v_ready = sig("b_v_ready")
        scored = sig("b_scored")
        biased = sig("b_biased")
        top_ready = sig("b_top_ready")
        lowered = sig("b_lowered")
        exped = sig("b_exped")
        norm_steps = sig("b_norm_steps", 2)
        p_turned = sig("b_p_turned", quads)
        pT_ready = sig("b_pT_ready", quads)
        mixed = sig("b_mixed")
        c_ready = sig("b_c_ready")
        c_turned = sig("b_c_turned")
        cT_ready = sig("b_cT_ready")
        y_ready = sig("b_y_ready")
        x_steps = sig("b_x_steps", 3)

        open_signals(nc, signals, [core.landed["b"]])
        block = ctx.enter_context(nc.Block())

        @block.sync
        def _(sp):
            def load(i, s):
                sp.wait_ge(loaded.sem, loaded.at(i, 0))
                if behind(i, 2):
                    sp.wait_ge(projected.sem, projected.at(i - 1, 0))
                sp.dma_start(ctxT[:, s, :], core.ins["ctxT"][:, ds(i, 1), :].rearrange("p a s -> p (a s)")
                             ).then_inc(loaded.sem, 16)
                if behind(i, 2):
                    sp.wait_ge(side_ready.sem, side_ready.at(i - 1, 0))
                for n, name in enumerate(("fside", "mask")):
                    sp.dma_start(side[:, s, n, :], core.ins[name][ds(i, 1), :, :].rearrange("a t s -> (a t) s")
                                 ).then_inc(loaded.sem, 16)

            load(0, 0)
            with sp.Fori(1, B - 2, 2) as i:
                load(i, 1)
                load(i + 1, 0)
            load(B - 1, 1)

        @block.gpsimd
        def _(pool):
            def front(i, s):
                pool.wait_ge(loaded.sem, loaded.at(i, 48))
                if behind(i, 2):
                    pool.wait_ge(biased.sem, biased.at(i - 1, 0))
                nc.gpsimd.tensor_tensor(side_sum[:, s, :], side[:, s, 0, :], side[:, s, 1, :],
                                        ALU.add).then_inc(side_ready.sem, 1)
                pool.wait_ge(top_ready.sem, top_ready.at(i, 1))
                nc.gpsimd.tensor_tensor(p[:, s, :, :], p[:, s, :, :],
                                        top[:, s, :].unsqueeze(2).broadcast_to([128, heads, S2]),
                                        ALU.subtract).then_inc(lowered.sem, 1)
                pool.wait_ge(x_normed.sem, x_normed.at(i, 1))
                if behind(i, 2):
                    pool.wait_ge(x_steps.sem, x_steps.at(i - 1, 0))
                nc.gpsimd.tensor_tensor(xs_bo[:, s, :], xs[:, s, :], core.w["b_bo"][:, :],
                                        ALU.add).then_inc(bo_added.sem, 1)

            def step(i, s, stages):
                if "b" in stages:
                    front(i + 1, 1 - s)

            in_steps(pool, step)

        @block.scalar
        def _(act):
            def turn_x(i, s):
                act.wait_ge(x_turned.sem, x_turned.at(i, 1))
                if behind(i, 2):
                    act.wait_ge(projected.sem, projected.at(i - 1, 0))
                nc.scalar.activation(xT[:, s, :], xT_ps, ACT.Copy).then_inc(xT_ready.sem, 1)

            def exp(i, s):
                act.wait_ge(lowered.sem, lowered.at(i, 1))
                nc.scalar.activation(p[:, s, :, :], p[:, s, :, :], ACT.Exp).then_inc(exped.sem, 1)

            def copy_p(i, s, r):
                act.wait_ge(p_turned.sem, p_turned.at(i, r + 1))
                if r == 0:
                    if behind(i, 2):
                        act.wait_ge(mixed.sem, mixed.at(i - 1, 0))
                nc.scalar.activation(pT[:, s, per * r:per * (r + 1), :],
                                     turn_ps[0:S2, r % 2, :].rearrange("p (j t) -> p j t", t=128),
                                     ACT.Copy).then_inc(pT_ready.sem, 1)

            def copy_c(i, s):
                act.wait_ge(c_turned.sem, c_turned.at(i, 1))
                if behind(i, 2):
                    act.wait_ge(y_ready.sem, y_ready.at(i - 1, 0))
                nc.scalar.activation(cT[:, s, :], cT_ps, ACT.Copy).then_inc(cT_ready.sem, 1)

            def step(i, s, stages):
                if "d" in stages:
                    copy_c(i - 1, 1 - s)
                if "a" in stages:
                    turn_x(i + 2, s)
                if "c" in stages:
                    for r in range(quads):
                        copy_p(i, s, r)
                if "b" in stages:
                    exp(i + 1, 1 - s)

            in_steps(act, step)

        @block.vector
        def _(dve):
            def normalise(i, s):
                if behind(i, 2):
                    dve.wait_ge(bo_added.sem, bo_added.at(i - 1, 0))
                if behind(i, 2):
                    dve.wait_ge(x_turned.sem, x_turned.at(i - 1, 0))
                nc.vector.tensor_scalar(xs[:, s, :], x[:, i, :], core.mean[:, ds(i, 1)],
                                        core.rstd[:, ds(i, 1)], ALU.subtract,
                                        ALU.mult).then_inc(x_normed.sem, 1)

            def keys(i, s):
                dve.wait_ge(projected.sem, projected.at(i, 1))
                if behind(i, 2):
                    dve.wait_ge(scored.sem, scored.at(i - 1, 0))
                nc.vector.tensor_scalar(qT[:, s, :], q_ps, core.w["b_bq"][:, :], None, ALU.add)
                nc.vector.scalar_tensor_tensor(
                    k_own[:, s, :, :], k_ps.unsqueeze(1).broadcast_to([128, per, S2]),
                    core.w["b_bk"][:, :], core.w["head_mask"][:, :].unsqueeze(2).broadcast_to([128, per, S2]),
                    ALU.add, ALU.mult).then_inc(k_ready.sem, 1)

            def values(i, s):
                if behind(i, 2):
                    dve.wait_ge(mixed.sem, mixed.at(i - 1, 0))
                nc.vector.tensor_tensor(v[:, s, :], v_ps, core.w["b_bv"][0:S2, :],
                                        ALU.add).then_inc(v_ready.sem, 1)

            def bias_max(i, s):
                dve.wait_ge(scored.sem, scored.at(i, 1))
                dve.wait_ge(side_ready.sem, side_ready.at(i, 1))
                if behind(i, 2):
                    dve.wait_ge(p_turned.sem, p_turned.at(i - 1, 0))
                nc.vector.tensor_tensor(
                    p[:, s, :, :].rearrange("p (r j) s -> p r j s", r=quads), scores,
                    side_sum[:, s, :].unsqueeze(1).unsqueeze(1).broadcast_to([128, quads, per, S2]),
                    ALU.add).then_inc(biased.sem, 1)
                dve.wait_ge(biased.sem, biased.at(i, 1))
                nc.vector.tensor_reduce(top[:, s, :], p[:, s, :, :], AX.X, ALU.max).then_inc(top_ready.sem, 1)

            def sums(i, s):
                dve.wait_ge(exped.sem, exped.at(i, 1))
                if behind(i, 2):
                    dve.wait_ge(c_ready.sem, c_ready.at(i - 1, 0))
                nc.vector.tensor_reduce(norm[:, s, :], p[:, s, :, :], AX.X, ALU.add).then_inc(norm_steps.sem, 1)
                dve.wait_ge(norm_steps.sem, norm_steps.at(i, 1))
                nc.vector.reciprocal(norm[:, s, :], norm[:, s, :]).then_inc(norm_steps.sem, 1)

            def divide(i, s):
                dve.wait_ge(norm_steps.sem, norm_steps.at(i, 2))
                dve.wait_ge(mixed.sem, mixed.at(i, 1))
                nc.vector.tensor_tensor(
                    c[:, s, :].rearrange("p (h d) -> p h d", d=dk), c_ps.rearrange("p (h d) -> p h d", d=dk),
                    norm[:, s, :].unsqueeze(2).broadcast_to([128, heads, dk]), ALU.mult).then_inc(c_ready.sem, 1)

            def add_up(i, s):
                dve.wait_ge(y_ready.sem, y_ready.at(i, 1))
                dve.wait_ge(bo_added.sem, bo_added.at(i, 1))
                nc.vector.tensor_tensor(total[:, s, :], y_ps, xs_bo[:, s, :], ALU.add).then_inc(x_steps.sem, 1)
                leave_one(dve, nc, core, i, x_steps, total[:, s, :], stats[:, s, :])

            def step(i, s, stages):
                if "d" in stages:
                    divide(i - 1, 1 - s)
                if "a" in stages:
                    normalise(i + 2, s)
                if "b" in stages:
                    values(i + 1, 1 - s)
                if "c" in stages:
                    sums(i, s)
                if "b" in stages:
                    bias_max(i + 1, 1 - s)
                if "d" in stages:
                    add_up(i - 1, 1 - s)
                if "a" in stages:
                    keys(i + 2, s)

            in_steps(dve, step)

        @block.tensor
        def _(pe):
            def turn_x(i, s):
                pe.wait_ge(x_normed.sem, x_normed.at(i, 1))
                if behind(i, 1):
                    pe.wait_ge(k_ready.sem, k_ready.at(i, 0))
                    pe.wait_ge(v_ready.sem, v_ready.at(i, 0))
                nc.tensor.transpose(xT_ps, xs[:, s, :], core.ident[:, :]).then_inc(x_turned.sem, 1)

            def project(i, s):
                pe.wait_ge(xT_ready.sem, xT_ready.at(i, 1))
                pe.wait_ge(loaded.sem, loaded.at(i, 48))
                nc.tensor.matmul(q_ps, core.w["b_wq"][:, :], xT[:, s, :], start=True, stop=True)
                nc.tensor.matmul(k_ps, core.w["b_wk"][:, :], ctxT[:, s, :], start=True, stop=True)
                nc.tensor.matmul(v_ps, ctxT[:, s, :], core.w["b_wv"][:, :],
                                 start=True, stop=True).then_inc(projected.sem, 1)

            def score(i, s):
                pe.wait_ge(k_ready.sem, k_ready.at(i, 1))
                if behind(i, 1):
                    pe.wait_ge(biased.sem, biased.at(i, 0))
                for r in range(quads):
                    rows = slice(32 * r, 32 * r + 32)
                    last = nc.tensor.matmul(s_ps[:, r, 0:per * S2], qT[rows, s, :],
                                            k_own[rows, s, :, :].rearrange("p j s -> p (j s)"),
                                            start=True, stop=True)
                last.then_inc(scored.sem, 1)

            def turn_p(i, s, r):
                if r == 0:
                    pe.wait_ge(exped.sem, exped.at(i, 1))
                if r < 2:
                    if behind(i, 1):
                        pe.wait_ge(pT_ready.sem, pT_ready.at(i - 1, r + 3))
                else:
                    pe.wait_ge(pT_ready.sem, pT_ready.at(i, r - 1))
                for j in range(per):
                    last = nc.tensor.transpose(turn_ps[0:S2, r % 2, j * 128:(j + 1) * 128],
                                               p[:, s, per * r + j, :], core.ident[:, :])
                last.then_inc(p_turned.sem, 1)

            def mix(i, s):
                pe.wait_ge(v_ready.sem, v_ready.at(i, 1))
                if behind(i, 1):
                    pe.wait_ge(x_steps.sem, x_steps.at(i - 1, 1))
                for h in range(heads):
                    if h % per == 0:
                        pe.wait_ge(pT_ready.sem, pT_ready.at(i, h // per + 1))
                    last = nc.tensor.matmul(c_ps[:, dk * h:dk * (h + 1)], pT[:, s, h, :],
                                            v[:, s, dk * h:dk * (h + 1)], start=True, stop=True)
                last.then_inc(mixed.sem, 1)

            def turn_c(i, s):
                pe.wait_ge(c_ready.sem, c_ready.at(i, 1))
                nc.tensor.transpose(cT_ps, c[:, s, :], core.ident[:, :]).then_inc(c_turned.sem, 1)

            def project_out(i, s):
                pe.wait_ge(cT_ready.sem, cT_ready.at(i, 1))
                nc.tensor.matmul(y_ps, cT[:, s, :], core.w["b_wo"][:, :],
                                 start=True, stop=True).then_inc(y_ready.sem, 1)

            def step(i, s, stages):
                if "b" in stages:
                    score(i + 1, 1 - s)
                if "d" in stages:
                    turn_c(i - 1, 1 - s)
                if "a" in stages:
                    turn_x(i + 2, s)
                if "c" in stages:
                    turn_p(i, s, 0)
                    turn_p(i, s, 1)
                if "d" in stages:
                    project_out(i - 1, 1 - s)
                if "a" in stages:
                    project(i + 2, s)
                if "c" in stages:
                    turn_p(i, s, 2)
                    turn_p(i, s, 3)
                    mix(i, s)

            in_steps(pe, step)


def phase_moe(core):
    nc = core.nc
    x = core.x
    shared, routed, halves, top_k = 2, 8, 2, 2
    units = (shared + routed) * halves
    h_slots = 6
    with ExitStack() as ctx:
        def sb(name, shape, dt=F32):
            return ctx.enter_context(nc.sbuf_tensor(name, shape, dt))

        def ps(name, shape, dt=F32):
            return ctx.enter_context(nc.psum_tensor(name, shape, dt))

        signals = []

        def sig(name, per_pass=1):
            signals.append(Signal(ctx.enter_context(nc.semaphore(name)), per_pass))
            return signals[-1]

        xs = sb("m_xs", [128, GB, 128])
        xT = sb("m_xT", [128, GT])
        logits = sb("m_logits", [128, GB, routed])
        above = sb("m_above", [128, GB, routed, routed])
        tied = sb("m_tied", [128, GB, routed, routed])
        rank = sb("m_rank", [128, GB, routed])
        top = sb("m_top", [128, GB])
        share = sb("m_share", [128, GB, routed])
        share_sum = sb("m_share_sum", [128, GB])
        weight = sb("m_weight", [128, GB, routed])
        silu = sb("m_silu", [128, 2, GT])
        h = sb("m_h", [128, h_slots, GT])
        acc = sb("m_acc", [128, GB, 128])
        stats = sb("m_stats", [128, GB, 6])

        g_ps = ps("m_g_ps", [128, 2, GT])
        u_ps = ps("m_u_ps", [128, 2, GT])
        o_ps = ps("m_o_ps", [128, 2, GT])
        turn_ps = ps("m_turn_ps", [128, GT])
        r_ps = ps("m_r_ps", [128, GB, routed])

        x_normed = sig("m_x_normed")
        x_turned = sig("m_x_turned")
        xT_ready = sig("m_xT_ready")
        routed_ready = sig("m_routed_ready")
        route_steps = sig("m_route_steps", 8)
        powered = sig("m_powered")
        divided = sig("m_divided", 3)
        up_ready = sig("m_up_ready", units)
        silu_ready = sig("m_silu_ready", units)
        h_ready = sig("m_h_ready", units)
        down_ready = sig("m_down_ready", 1 + routed)
        acc_steps = sig("m_acc_steps", 1 + routed)
        left_steps = sig("m_left_steps", 3)

        def over_groups(eng, body):
            with eng.Fori(0, NG - 1) as g:
                body(g, True)
            body(NG - 1, False)

        open_signals(nc, signals, [core.landed["m"]])
        block = ctx.enter_context(nc.Block())

        @block.gpsimd
        def _(pool):
            def body(g, more):
                pool.wait_ge(route_steps.sem, route_steps.at(g, 3))
                nc.gpsimd.tensor_tensor(share[:, :, :], core.euler[:, :].rearrange("p (a b) -> p a b", a=GB),
                                        share[:, :, :], ALU.pow).then_inc(powered.sem, 1)

            over_groups(pool, body)

        @block.scalar
        def _(act):
            def copy_xT(g):
                act.wait_ge(x_turned.sem, x_turned.at(g, 1))
                if behind(g, 1):
                    act.wait_ge(up_ready.sem, up_ready.at(g - 1, units))
                nc.scalar.activation(xT[:, :], turn_ps[:, :], ACT.Copy).then_inc(xT_ready.sem, 1)

            def body(g):
                copy_xT(g)
                for n in range(units):
                    act.wait_ge(up_ready.sem, up_ready.at(g, n + 1))
                    if n < 2:
                        act.wait_ge(h_ready.sem, h_ready.at(g, 0))
                    else:
                        act.wait_ge(h_ready.sem, h_ready.at(g, n - 1))
                    nc.scalar.activation(silu[:, n % 2, :], g_ps[:, n % 2, :],
                                         ACT.Silu).then_inc(silu_ready.sem, 1)

            body(0)
            with act.Fori(1, NG) as g:
                body(g)

        @block.vector
        def _(dve):
            def normalise(g):
                if behind(g, 1):
                    dve.wait_ge(acc_steps.sem, acc_steps.at(g - 1, 1))
                for j in range(GB):
                    last = nc.vector.tensor_scalar(xs[:, j, :], x[:, g * GB + j, :],
                                                   core.mean[:, ds(g * GB + j, 1)],
                                                   core.rstd[:, ds(g * GB + j, 1)], ALU.subtract, ALU.mult)
                last.then_inc(x_normed.sem, 1)

            def compare(g):
                grid = [128, GB, routed, routed]
                dve.wait_ge(routed_ready.sem, routed_ready.at(g, 1))
                nc.vector.tensor_tensor(logits[:, :, :], r_ps[:, :, :],
                                        core.w["m_bias"][:, :].unsqueeze(1).broadcast_to([128, GB, routed]),
                                        ALU.add).then_inc(route_steps.sem, 1)
                dve.wait_ge(route_steps.sem, route_steps.at(g, 1))
                nc.vector.tensor_reduce(top[:, :], logits[:, :, :], AX.X, ALU.max).then_inc(route_steps.sem, 1)
                other = logits[:, :, :].unsqueeze(2).broadcast_to(grid)
                own = logits[:, :, :].unsqueeze(3).broadcast_to(grid)
                nc.vector.tensor_tensor(above[:, :, :, :], other, own, ALU.is_gt)
                dve.wait_ge(route_steps.sem, route_steps.at(g, 2))
                nc.vector.tensor_tensor(share[:, :, :], logits[:, :, :],
                                        top[:, :].unsqueeze(2).broadcast_to([128, GB, routed]),
                                        ALU.subtract).then_inc(route_steps.sem, 1)
                nc.vector.tensor_tensor(tied[:, :, :, :], other, own, ALU.is_equal).then_inc(route_steps.sem, 1)

            def rank_experts(g):
                dve.wait_ge(route_steps.sem, route_steps.at(g, 4))
                nc.vector.tensor_tensor(tied[:, :, :, :].rearrange("p b e f -> p b (e f)"),
                                        tied[:, :, :, :].rearrange("p b e f -> p b (e f)"),
                                        core.w["m_earlier"][:, :].unsqueeze(1).broadcast_to(
                                            [128, GB, routed * routed]), ALU.mult).then_inc(route_steps.sem, 1)
                dve.wait_ge(route_steps.sem, route_steps.at(g, 5))
                nc.vector.tensor_tensor(above[:, :, :, :], above[:, :, :, :], tied[:, :, :, :],
                                        ALU.add).then_inc(route_steps.sem, 1)
                dve.wait_ge(route_steps.sem, route_steps.at(g, 6))
                nc.vector.tensor_reduce(rank[:, :, :], above[:, :, :, :], AX.X, ALU.add).then_inc(route_steps.sem, 1)

            def weigh(g):
                dve.wait_ge(route_steps.sem, route_steps.at(g, 7))
                dve.wait_ge(powered.sem, powered.at(g, 1))
                nc.vector.scalar_tensor_tensor(weight[:, :, :], rank[:, :, :], float(top_k), share[:, :, :],
                                               ALU.is_lt, ALU.mult).then_inc(route_steps.sem, 1)
                dve.wait_ge(route_steps.sem, route_steps.at(g, 8))
                nc.vector.tensor_reduce(share_sum[:, :], weight[:, :, :], AX.X, ALU.add).then_inc(divided.sem, 1)
                dve.wait_ge(divided.sem, divided.at(g, 1))
                nc.vector.reciprocal(share_sum[:, :], share_sum[:, :]).then_inc(divided.sem, 1)
                dve.wait_ge(divided.sem, divided.at(g, 2))
                nc.vector.tensor_tensor(weight[:, :, :], weight[:, :, :],
                                        share_sum[:, :].unsqueeze(2).broadcast_to([128, GB, routed]),
                                        ALU.mult).then_inc(divided.sem, 1)
                dve.wait_ge(divided.sem, divided.at(g, 3))

            def hidden(g, n):
                dve.wait_ge(silu_ready.sem, silu_ready.at(g, n + 1))
                if n < h_slots:
                    dve.wait_ge(down_ready.sem, down_ready.at(g, 0))
                else:
                    dve.wait_ge(down_ready.sem, down_ready.at(g, max(0, (n - h_slots) // 2 - 1) + 1))
                nc.vector.tensor_tensor(h[:, n % h_slots, :], silu[:, n % 2, :], u_ps[:, n % 2, :],
                                        ALU.mult).then_inc(h_ready.sem, 1)

            def gather(g, d):
                dve.wait_ge(down_ready.sem, down_ready.at(g, d + 1))
                if d == 0:
                    dve.wait_ge(left_steps.sem, left_steps.at(g, 0))
                    nc.vector.tensor_tensor(acc[:, :, :].rearrange("p b d -> p (b d)"),
                                            xs[:, :, :].rearrange("p b d -> p (b d)"), o_ps[:, 0, :],
                                            ALU.add).then_inc(acc_steps.sem, 1)
                    return
                dve.wait_ge(acc_steps.sem, acc_steps.at(g, d))
                for j in range(GB):
                    last = nc.vector.scalar_tensor_tensor(
                        acc[:, j, :], o_ps[:, d % 2, j * 128:(j + 1) * 128], weight[:, j, d - 1:d],
                        acc[:, j, :], ALU.mult, ALU.add)
                last.then_inc(acc_steps.sem, 1)

            def body(g, more):
                compare(g)
                hidden(g, 2)
                rank_experts(g)
                hidden(g, 3)
                for d in range(1 + routed):
                    if d < routed:
                        hidden(g, 2 * d + 4)
                        hidden(g, 2 * d + 5)
                    gather(g, d)
                    if d == 0:
                        weigh(g)
                    if d == 4 and more:
                        normalise(g + 1)
                if more:
                    hidden(g + 1, 0)
                    hidden(g + 1, 1)
                dve.wait_ge(acc_steps.sem, acc_steps.at(g, 1 + routed))
                for j in range(GB):
                    last = nc.vector.bn_stats(stats[:, j, :], acc[:, j, :])
                last.then_inc(left_steps.sem, 1)
                nc.vector.tensor_copy(core.x[:, ds(g * GB, GB), :], acc[:, :, :]).then_inc(left_steps.sem, 1)
                dve.wait_ge(left_steps.sem, left_steps.at(g, 2))
                nc.vector.tensor_copy(core.stats[:, ds(g * GB, GB), :], stats[:, :, :]).then_inc(left_steps.sem, 1)

            normalise(0)
            hidden(0, 0)
            hidden(0, 1)
            over_groups(dve, body)

        @block.tensor
        def _(pe):
            def turn(g):
                pe.wait_ge(x_normed.sem, x_normed.at(g, 1))
                if behind(g, 1):
                    pe.wait_ge(xT_ready.sem, xT_ready.at(g - 1, 1))
                for j in range(GB):
                    last = nc.tensor.transpose(turn_ps[:, j * 128:(j + 1) * 128], xs[:, j, :], core.ident[:, :])
                last.then_inc(x_turned.sem, 1)

            def router(g):
                pe.wait_ge(xT_ready.sem, xT_ready.at(g, 1))
                pe.wait_ge(route_steps.sem, route_steps.at(g, 0))
                for j in range(GB):
                    last = nc.tensor.matmul(r_ps[:, j, :], xT[:, j * 128:(j + 1) * 128], core.w["m_router"][:, :],
                                            start=True, stop=True)
                last.then_inc(routed_ready.sem, 1)

            def up(g, n):
                if n < 2:
                    pe.wait_ge(h_ready.sem, h_ready.at(g, 0))
                else:
                    pe.wait_ge(h_ready.sem, h_ready.at(g, n - 1))
                nc.tensor.matmul(g_ps[:, n % 2, :], core.w["m_w1"][:, n, :], xT[:, :], start=True, stop=True)
                nc.tensor.matmul(u_ps[:, n % 2, :], core.w["m_w3"][:, n, :], xT[:, :],
                                 start=True, stop=True).then_inc(up_ready.sem, 1)

            def down(g, d):
                mine = range(0, shared * halves) if d == 0 else range(2 * d + 2, 2 * d + 4)
                pe.wait_ge(h_ready.sem, h_ready.at(g, mine[-1] + 1))
                pe.wait_ge(acc_steps.sem, acc_steps.at(g, max(0, d - 1)))
                for j in range(GB):
                    for n in mine:
                        last = nc.tensor.matmul(o_ps[:, d % 2, j * 128:(j + 1) * 128],
                                                h[:, n % h_slots, j * 128:(j + 1) * 128],
                                                core.w["m_w2"][:, n, :], start=(n == mine[0]), stop=(n == mine[-1]))
                last.then_inc(down_ready.sem, 1)

            def body(g, more):
                router(g)
                for n in range(4):
                    up(g, n)
                for d in range(1 + routed):
                    if d < routed:
                        up(g, 2 * d + 4)
                        up(g, 2 * d + 5)
                    elif more:
                        turn(g + 1)
                    down(g, d)

            turn(0)
            over_groups(pe, body)


def phase_scan(core):
    nc = core.nc
    x = core.x
    halves, states, rank, taps = 2, 16, 16, 4
    deep = 4
    parts = 3
    with ExitStack() as ctx:
        def sb(name, shape, dt=F32):
            return ctx.enter_context(nc.sbuf_tensor(name, shape, dt))

        def ps(name, shape, dt=F32):
            return ctx.enter_context(nc.psum_tensor(name, shape, dt))

        signals = []

        def sig(name, per_pass=1):
            signals.append(Signal(ctx.enter_context(nc.semaphore(name)), per_pass))
            return signals[-1]

        decay_rate = sb("s_decay_rate", [128, halves, states])
        pick = sb("s_pick", [parts * 32, 2 * states, 128], BF16)
        xs = sb("s_xs", [128, GB, 128])
        xs_bo = sb("s_xs_bo", [128, 2, GB, 128])
        xT = sb("s_xT", [128, GT])
        padded = sb("s_padded", [128, halves, GB, taps - 1 + T])
        conv = sb("s_conv", [128, halves, GB, T])
        conv_sig = sb("s_conv_sig", [128, halves, GT])
        u = sb("s_u", [128, 2, halves, GT])
        res = sb("s_res", [128, halves, GT])
        res_th = sb("s_res_th", [128, halves, GT])
        res_gate = sb("s_res_gate", [128, 2, halves, GT])
        dtT = sb("s_dtT", [rank, GT])
        rest1 = sb("s_rest1", [32, GT])
        middle = sb("s_middle", [32, GT], BF16)
        bc_parts = sb("s_bc_parts", [parts * 32, 2, GT], BF16)
        raw = res
        soft = conv_sig
        delta = sb("s_delta", [128, 2, halves, GT])
        du = sb("s_du", [128, 2, halves, GT])
        decay = sb("s_decay", [128, 2, halves, GB, T])
        b_sb = sb("s_b_sb", [128, deep, GT])
        drive = sb("s_drive", [128, 2, halves, GT])
        state = sb("s_state", [128, 2, halves, GT])
        read = sb("s_read", [128, deep, halves, GT])
        y = conv[:, :, :, :].rearrange("p h b t -> p h (b t)")
        total = sb("s_total", [128, GB, 128])
        stats = sb("s_stats", [128, GB, 6])

        b_ps = ps("s_b_ps", [128, 2, GT])
        c_ps = ps("s_c_ps", [128, 2, GT])
        y_ps = ps("s_y_ps", [128, halves, GT])
        f0_ps = ps("s_f0_ps", [128, GT])
        f1_ps = ps("s_f1_ps", [128, GT])

        prepared = sig("s_prepared", 4)
        x_normed = sig("s_x_normed")
        bo_added = sig("s_bo_added")
        x_turned = sig("s_x_turned")
        xT_ready = sig("s_xT_ready")
        z_ready = sig("s_z_ready", 4)
        z_copied = sig("s_z_copied", 4)
        conv_steps = sig("s_conv_steps", halves * taps)
        res_tanh = sig("s_res_tanh")
        res_ready = sig("s_res_ready")
        conv_th = sig("s_conv_th")
        conv_gate = sig("s_conv_gate")
        u_ready = sig("s_u_ready")
        bc_ready = sig("s_bc_ready")
        dt_ready = sig("s_dt_ready")
        dt_copied = sig("s_dt_copied")
        split_steps = sig("s_split_steps", 5)
        raw_ps_ready = sig("s_raw_ps_ready", halves)
        raw_ready = sig("s_raw_ready", halves)
        soft_steps = sig("s_soft_steps", 3)
        delta_ready = sig("s_delta_ready")
        du_ready = sig("s_du_ready")
        b_spread = sig("s_b_spread", states)
        c_spread = sig("s_c_spread", states)
        decay_ready = sig("s_decay_ready", states)
        b_copied = sig("s_b_copied", states)
        driven = sig("s_driven", states)
        scanned = sig("s_scanned", states)
        read_out = sig("s_read_out", states)
        summed = sig("s_summed", states)
        y_steps = sig("s_y_steps", 3)
        o_ready = sig("s_o_ready")
        x_steps = sig("s_x_steps", 3)

        def over_groups(eng, front, body):
            front(0, 0)
            body(0, 0, True)
            with eng.Fori(1, NG - 2, 2) as g:
                body(g, 1, True)
                body(g + 1, 0, True)
            body(NG - 1, 1, False)

        def pieces_of(pieces):
            def front(g, s):
                for piece in pieces.values():
                    piece(g, s)
            return front

        open_signals(nc, signals, [core.landed["s"]])
        block = ctx.enter_context(nc.Block())

        @block.gpsimd
        def _(pool):
            nc.gpsimd.memset(padded[:, :, :, 0:taps - 1], 0.0).then_inc(prepared.sem, 1)
            nc.gpsimd.memset(decay[:, :, :, :, 0:1], 0.0).then_inc(prepared.sem, 1)

            def add_bo(g, s):
                pool.wait_ge(x_normed.sem, x_normed.at(g, 1))
                if behind(g, 2):
                    pool.wait_ge(x_steps.sem, x_steps.at(g - 1, 0))
                nc.gpsimd.tensor_tensor(xs_bo[:, s, :, :], xs[:, :, :],
                                        core.w["s_bo"][:, :].unsqueeze(1).broadcast_to([128, GB, 128]),
                                        ALU.add).then_inc(bo_added.sem, 1)

            def gate_u(g, s):
                pool.wait_ge(conv_gate.sem, conv_gate.at(g, 1))
                if behind(g, 2):
                    pool.wait_ge(y_steps.sem, y_steps.at(g - 1, 0))
                nc.gpsimd.tensor_tensor(u[:, s, :, :], conv_sig[:, :, :],
                                        conv[:, :, :, :].rearrange("p h b t -> p h (b t)"),
                                        ALU.mult).then_inc(u_ready.sem, 1)

            def mult_du(g, s):
                pool.wait_ge(delta_ready.sem, delta_ready.at(g, 1))
                nc.gpsimd.tensor_tensor(du[:, s, :, :], delta[:, s, :, :], u[:, s, :, :],
                                        ALU.mult).then_inc(du_ready.sem, 1)

            def drive_state(g, s, n):
                if n == 0:
                    pool.wait_ge(du_ready.sem, du_ready.at(g, 1))
                pool.wait_ge(b_copied.sem, b_copied.at(g, n + 1))
                if n:
                    pool.wait_ge(scanned.sem, scanned.at(g, n - 1))
                elif behind(g, 1):
                    pool.wait_ge(scanned.sem, scanned.at(g - 1, states - 1))
                nc.gpsimd.tensor_tensor(drive[:, n % 2, :, :], du[:, s, :, :],
                                        b_sb[:, n % deep, :].unsqueeze(1).broadcast_to([128, halves, GT]),
                                        ALU.mult).then_inc(driven.sem, 1)

            pieces = {4: add_bo, 9: gate_u, 15: mult_du}

            def body(g, s, more):
                for n in range(states):
                    drive_state(g, s, n)
                    if more and n in pieces:
                        pieces[n](g + 1, 1 - s)

            over_groups(pool, pieces_of(pieces), body)

        @block.scalar
        def _(act):
            nc.scalar.activation(decay_rate[:, :, :], core.w["s_A_log"][:, :, :], ACT.Exp).then_inc(prepared.sem, 1)

            def copy_xT(g, s):
                act.wait_ge(x_turned.sem, x_turned.at(g, 1))
                nc.scalar.activation(xT[:, :], f0_ps[:, :], ACT.Copy).then_inc(xT_ready.sem, 1)

            def copy_z(g, s, m):
                act.wait_ge(z_ready.sem, z_ready.at(g, m + 1))
                bank = (f0_ps, f1_ps)[m % 2]
                bias = core.w["s_b_in"][:, m:m + 1]
                if m < 2:
                    if behind(g, 1):
                        act.wait_ge(conv_steps.sem, conv_steps.at(g - 1, halves * taps))
                    out = padded[:, m, :, taps - 1:]
                    nc.scalar.activation(out, bank[:, :].rearrange("p (b t) -> p b t", t=T), ACT.Identity,
                                         bias=bias).then_inc(z_copied.sem, 1)
                else:
                    if behind(g, 1):
                        act.wait_ge(delta_ready.sem, delta_ready.at(g - 1, 1))
                    nc.scalar.activation(res[:, m - 2, :], bank[:, :], ACT.Identity,
                                         bias=bias).then_inc(z_copied.sem, 1)

            def tanh_res(g, s):
                act.wait_ge(z_copied.sem, z_copied.at(g, 4))
                if behind(g, 1):
                    act.wait_ge(res_ready.sem, res_ready.at(g - 1, 1))
                nc.scalar.activation(res_th[:, :, :], res[:, :, :], ACT.Tanh, scale=0.5).then_inc(res_tanh.sem, 1)

            def sigmoid_conv(g, s):
                act.wait_ge(conv_steps.sem, conv_steps.at(g, halves * taps))
                if behind(g, 1):
                    act.wait_ge(delta_ready.sem, delta_ready.at(g - 1, 1))
                nc.scalar.activation(conv_sig[:, :, :], conv[:, :, :, :].rearrange("p h b t -> p h (b t)"),
                                     ACT.Tanh, scale=0.5).then_inc(conv_th.sem, 1)
                act.wait_ge(conv_th.sem, conv_th.at(g, 1))
                nc.scalar.activation(conv_sig[:, :, :], conv_sig[:, :, :], ACT.Copy, scale=0.5,
                                     bias=0.5).then_inc(conv_gate.sem, 1)

            def copy_raw(g, s):
                for m in range(halves):
                    act.wait_ge(raw_ps_ready.sem, raw_ps_ready.at(g, m + 1))
                    if m == 0:
                        act.wait_ge(res_ready.sem, res_ready.at(g, 1))
                    nc.scalar.activation(raw[:, m, :], (f1_ps, f0_ps)[m][:, :], ACT.Identity,
                                         bias=core.w["s_dt_bias"][:, m:m + 1]).then_inc(raw_ready.sem, 1)

            def softplus_exp(g, s):
                act.wait_ge(raw_ready.sem, raw_ready.at(g, halves))
                act.wait_ge(u_ready.sem, u_ready.at(g, 1))
                nc.scalar.activation(soft[:, :, :], raw[:, :, :], ACT.Abs).then_inc(soft_steps.sem, 1)
                act.wait_ge(soft_steps.sem, soft_steps.at(g, 1))
                nc.scalar.activation(soft[:, :, :], soft[:, :, :], ACT.Exp, scale=-1.0).then_inc(soft_steps.sem, 1)

            def softplus_ln(g, s):
                act.wait_ge(soft_steps.sem, soft_steps.at(g, 2))
                nc.scalar.activation(soft[:, :, :], soft[:, :, :], ACT.Ln, bias=1.0).then_inc(soft_steps.sem, 1)

            def copy_b(g, s, n):
                act.wait_ge(b_spread.sem, b_spread.at(g, n + 1))
                if n >= deep:
                    act.wait_ge(driven.sem, driven.at(g, n - deep + 1))
                elif behind(g, 1):
                    act.wait_ge(driven.sem, driven.at(g - 1, states + n - deep + 1))
                nc.scalar.activation(b_sb[:, n % deep, :], b_ps[:, n % 2, :], ACT.Copy).then_inc(b_copied.sem, 1)

            def decay_state(g, s, n):
                if n == 0:
                    act.wait_ge(delta_ready.sem, delta_ready.at(g, 1))
                    if isinstance(g, int) and g == 0:
                        act.wait_ge(prepared.sem, 1 + 4)
                if n >= 2:
                    act.wait_ge(scanned.sem, scanned.at(g, n - 1))
                elif behind(g, 1):
                    act.wait_ge(scanned.sem, scanned.at(g - 1, states + n - 1))
                for m in range(halves):
                    last = nc.scalar.activation(
                        decay[:, n % 2, m, :, 1:], delta[:, s, m, :].rearrange("p (b t) -> p b t", t=T)[:, :, 1:],
                        ACT.Exp, scale=core.neg_rate[:, m, n:n + 1])
                last.then_inc(decay_ready.sem, 1)

            def copy_conv(g, s):
                copy_z(g, s, 0)
                copy_z(g, s, 1)

            def copy_res(g, s):
                copy_z(g, s, 2)
                copy_z(g, s, 3)

            pieces = {1: copy_xT, 4: copy_conv, 5: copy_res, 6: tanh_res, 8: sigmoid_conv, 12: copy_raw,
                      13: softplus_exp, 14: softplus_ln}

            def body(g, s, more):
                for n in range(states):
                    decay_state(g, s, n)
                    if n < states - 1:
                        copy_b(g, s, n + 1)
                    elif more:
                        copy_b(g + 1, 1 - s, 0)
                    if more and n in pieces:
                        pieces[n](g + 1, 1 - s)

            def front(g, s):
                pieces_of(pieces)(g, s)
                copy_b(g, s, 0)

            over_groups(act, front, body)

        @block.vector
        def _(dve):
            dve.wait_ge(prepared.sem, 1 + 3)
            nc.vector.tensor_scalar(core.neg_rate[:, :, :], decay_rate[:, :, :], -1.0, None, ALU.mult)
            nc.vector.tensor_copy(pick[:, :, :], core.w["s_pick"][:, :].unsqueeze(2).broadcast_to(
                [parts * 32, 2 * states, 128])).then_inc(prepared.sem, 1)

            def normalise(g, s):
                if behind(g, 1):
                    dve.wait_ge(bo_added.sem, bo_added.at(g - 1, 1))
                if behind(g, 1):
                    dve.wait_ge(x_turned.sem, x_turned.at(g - 1, 1))
                for j in range(GB):
                    last = nc.vector.tensor_scalar(xs[:, j, :], x[:, g * GB + j, :],
                                                   core.mean[:, ds(g * GB + j, 1)],
                                                   core.rstd[:, ds(g * GB + j, 1)], ALU.subtract, ALU.mult)
                last.then_inc(x_normed.sem, 1)

            def convolve(g, s, k):
                if k == 0:
                    dve.wait_ge(z_copied.sem, z_copied.at(g, halves))
                    if behind(g, 1):
                        dve.wait_ge(u_ready.sem, u_ready.at(g - 1, 1))
                    if behind(g, 2):
                        dve.wait_ge(o_ready.sem, o_ready.at(g - 2, 1))
                for m in range(halves):
                    tap = core.w["s_conv_w"][:, m, k:k + 1]
                    shifted = padded[:, m, :, k:k + T]
                    if k == 0:
                        nc.vector.tensor_scalar(conv[:, m, :, :], shifted, tap, core.w["s_conv_b"][:, m:m + 1],
                                                ALU.mult, ALU.add).then_inc(conv_steps.sem, 1)
                    else:
                        dve.wait_ge(conv_steps.sem, conv_steps.at(g, halves * (k - 1) + m + 1))
                        nc.vector.scalar_tensor_tensor(conv[:, m, :, :], shifted, tap, conv[:, m, :, :],
                                                       ALU.mult, ALU.add).then_inc(conv_steps.sem, 1)

            def gate_res(g, s):
                dve.wait_ge(res_tanh.sem, res_tanh.at(g, 1))
                if behind(g, 2):
                    dve.wait_ge(y_steps.sem, y_steps.at(g - 1, 0))
                nc.vector.scalar_tensor_tensor(res_gate[:, s, :, :], res_th[:, :, :], 1.0, res[:, :, :],
                                               ALU.add, ALU.mult).then_inc(res_ready.sem, 1)

            def split_bc(g, s):
                dve.wait_ge(dt_ready.sem, dt_ready.at(g, 1))
                if behind(g, 1):
                    dve.wait_ge(raw_ps_ready.sem, raw_ps_ready.at(g - 1, halves))
                nc.vector.tensor_copy(dtT[:, :], f0_ps[0:rank, :]).then_inc(dt_copied.sem, 1)
                dve.wait_ge(bc_ready.sem, bc_ready.at(g, 1))
                if behind(g, 2):
                    dve.wait_ge(c_spread.sem, c_spread.at(g - 1, 0))
                nc.vector.tensor_copy(bc_parts[0:32, s, :], f1_ps[0:32, :]).then_inc(split_steps.sem, 1)
                dve.wait_ge(split_steps.sem, split_steps.at(g, 1))
                nc.vector.tensor_tensor(rest1[:, :], f1_ps[0:32, :], bc_parts[0:32, s, :],
                                        ALU.subtract).then_inc(split_steps.sem, 1)

            def split_rest(g, s):
                dve.wait_ge(split_steps.sem, split_steps.at(g, 2))
                nc.vector.tensor_copy(middle[:, :], rest1[:, :]).then_inc(split_steps.sem, 1)
                dve.wait_ge(split_steps.sem, split_steps.at(g, 3))
                nc.vector.tensor_copy(bc_parts[32:64, s, :], middle[:, :]).then_inc(split_steps.sem, 1)
                nc.vector.tensor_tensor(bc_parts[64:96, s, :], rest1[:, :], middle[:, :],
                                        ALU.subtract).then_inc(split_steps.sem, 1)

            def make_delta(g, s):
                dve.wait_ge(soft_steps.sem, soft_steps.at(g, 3))
                if behind(g, 2):
                    dve.wait_ge(decay_ready.sem, decay_ready.at(g - 1, 0))
                if behind(g, 2):
                    dve.wait_ge(du_ready.sem, du_ready.at(g - 1, 0))
                nc.vector.scalar_tensor_tensor(delta[:, s, :, :], raw[:, :, :], 0.0, soft[:, :, :],
                                               ALU.max, ALU.add).then_inc(delta_ready.sem, 1)

            def scan_state(g, s, n):
                dve.wait_ge(decay_ready.sem, decay_ready.at(g, n + 1))
                dve.wait_ge(driven.sem, driven.at(g, n + 1))
                if n >= 2:
                    dve.wait_ge(read_out.sem, read_out.at(g, n - 1))
                elif behind(g, 1):
                    dve.wait_ge(read_out.sem, read_out.at(g - 1, states + n - 1))
                nc.vector.tensor_tensor_scan(state[:, n % 2, :, :].rearrange("p h t -> p (h t)"),
                                             decay[:, n % 2, :, :, :].rearrange("p h b t -> p (h b t)"),
                                             drive[:, n % 2, :, :].rearrange("p h t -> p (h t)"),
                                             0.0, ALU.mult, ALU.add).then_inc(scanned.sem, 1)

            def read_state(g, s, n):
                dve.wait_ge(scanned.sem, scanned.at(g, n + 1))
                if n >= deep:
                    dve.wait_ge(summed.sem, summed.at(g, n - deep + 1))
                elif behind(g, 1):
                    dve.wait_ge(summed.sem, summed.at(g - 1, states + n - deep + 1))
                dve.wait_ge(c_spread.sem, c_spread.at(g, n + 1))
                nc.vector.tensor_tensor(read[:, n % deep, :, :], state[:, n % 2, :, :],
                                        c_ps[:, n % 2, :].unsqueeze(1).broadcast_to([128, halves, GT]),
                                        ALU.mult).then_inc(read_out.sem, 1)

            def gate_y(g, s, more):
                dve.wait_ge(summed.sem, summed.at(g, states))
                if more:
                    dve.wait_ge(u_ready.sem, u_ready.at(g + 1, 1))
                else:
                    dve.wait_ge(u_ready.sem, u_ready.at(g, 1))
                for m in range(halves):
                    nc.vector.scalar_tensor_tensor(y[:, m, :], u[:, s, m, :], core.w["s_D"][:, m:m + 1],
                                                   y_ps[:, m, :], ALU.mult, ALU.add).then_inc(y_steps.sem, 1)
                dve.wait_ge(y_steps.sem, y_steps.at(g, 2))
                nc.vector.scalar_tensor_tensor(y[:, :, :], y[:, :, :], 0.5, res_gate[:, s, :, :],
                                               ALU.mult, ALU.mult).then_inc(y_steps.sem, 1)

            def add_up(g, s):
                dve.wait_ge(o_ready.sem, o_ready.at(g, 1))
                dve.wait_ge(bo_added.sem, bo_added.at(g, 1))
                nc.vector.tensor_tensor(total[:, :, :].rearrange("p b d -> p (b d)"), f1_ps[:, :],
                                        xs_bo[:, s, :, :].rearrange("p b d -> p (b d)"),
                                        ALU.add).then_inc(x_steps.sem, 1)
                leave(dve, nc, core, g, x_steps, total, stats)

            pieces = {0: normalise, 4: lambda g, s: convolve(g, s, 0), 5: lambda g, s: convolve(g, s, 1),
                      6: lambda g, s: convolve(g, s, 2), 7: lambda g, s: convolve(g, s, 3),
                      8: gate_res, 11: split_bc, 12: split_rest, 14: make_delta}

            def body(g, s, more):
                for n in range(states):
                    scan_state(g, s, n)
                    if n == 0 and behind(g, 1):
                        gate_y(g - 1, 1 - s, True)
                    if n:
                        read_state(g, s, n - 1)
                    if n == 2 and behind(g, 1):
                        add_up(g - 1, 1 - s)
                    if more and n in pieces:
                        pieces[n](g + 1, 1 - s)
                read_state(g, s, states - 1)

            over_groups(dve, pieces_of(pieces), body)
            gate_y(NG - 1, 1, False)
            add_up(NG - 1, 1)

        @block.tensor
        def _(pe):
            def turn(g, s):
                pe.wait_ge(x_normed.sem, x_normed.at(g, 1))
                if behind(g, 1):
                    pe.wait_ge(raw_ready.sem, raw_ready.at(g - 1, halves))
                for j in range(GB):
                    last = nc.tensor.transpose(f0_ps[:, j * 128:(j + 1) * 128], xs[:, j, :], core.ident[:, :])
                last.then_inc(x_turned.sem, 1)

            def project_z(g, s, m):
                if m == 0:
                    pe.wait_ge(xT_ready.sem, xT_ready.at(g, 1))
                elif m == 1:
                    if behind(g, 2):
                        pe.wait_ge(x_steps.sem, x_steps.at(g - 2, 1))
                    if behind(g, 1):
                        pe.wait_ge(raw_ready.sem, raw_ready.at(g - 1, 1))
                else:
                    pe.wait_ge(z_copied.sem, z_copied.at(g, m - 1))
                nc.tensor.matmul((f0_ps, f1_ps)[m % 2][:, :], core.w["s_w_in"][:, m * 128:(m + 1) * 128],
                                 xT[:, :], start=True, stop=True).then_inc(z_ready.sem, 1)

            def project_bc(g, s):
                pe.wait_ge(u_ready.sem, u_ready.at(g, 1))
                pe.wait_ge(z_copied.sem, z_copied.at(g, 4))
                for cols, bank, rows, signal in ((slice(rank, rank + 2 * states), f1_ps, 2 * states, bc_ready),
                                                 (slice(0, rank), f0_ps, rank, dt_ready)):
                    for m in range(halves):
                        last = nc.tensor.matmul(bank[0:rows, :], core.w["s_x_proj"][:, m, cols], u[:, s, m, :],
                                                start=(m == 0), stop=(m == halves - 1))
                    last.then_inc(signal.sem, 1)

            def project_dt(g, s):
                pe.wait_ge(dt_copied.sem, dt_copied.at(g, 1))
                pe.wait_ge(split_steps.sem, split_steps.at(g, 2))
                for m in range(halves):
                    nc.tensor.matmul((f1_ps, f0_ps)[m][:, :], core.w["s_dt_proj"][:, m * 128:(m + 1) * 128],
                                     dtT[:, :], start=True, stop=True).then_inc(raw_ps_ready.sem, 1)

            def spread_b(g, s, n):
                if n == 0:
                    if isinstance(g, int) and g == 0:
                        pe.wait_ge(prepared.sem, 1 + 4)
                    pe.wait_ge(split_steps.sem, split_steps.at(g, 5))
                if n >= 2:
                    pe.wait_ge(b_copied.sem, b_copied.at(g, n - 1))
                elif behind(g, 1):
                    pe.wait_ge(b_copied.sem, b_copied.at(g - 1, states + n - 1))
                nc.tensor.matmul(b_ps[:, n % 2, :], pick[:, n, :], bc_parts[:, s, :],
                                 start=True, stop=True).then_inc(b_spread.sem, 1)

            def spread_c(g, s, n):
                if n >= 2:
                    pe.wait_ge(read_out.sem, read_out.at(g, n - 1))
                elif behind(g, 1):
                    pe.wait_ge(read_out.sem, read_out.at(g - 1, states + n - 1))
                nc.tensor.matmul(c_ps[:, n % 2, :], pick[:, states + n, :], bc_parts[:, s, :],
                                 start=True, stop=True).then_inc(c_spread.sem, 1)

            def sum_state(g, s, n):
                pe.wait_ge(read_out.sem, read_out.at(g, n + 1))
                if n == 0:
                    if behind(g, 1):
                        pe.wait_ge(y_steps.sem, y_steps.at(g - 1, 2))
                for m in range(halves):
                    last = nc.tensor.matmul(y_ps[:, m, :], core.ident[:, :], read[:, n % deep, m, :],
                                            start=(n == 0), stop=(n == states - 1))
                last.then_inc(summed.sem, 1)

            def project_out(g, s, more):
                pe.wait_ge(y_steps.sem, y_steps.at(g, 3))
                if more:
                    pe.wait_ge(raw_ready.sem, raw_ready.at(g + 1, 1))
                else:
                    pe.wait_ge(raw_ready.sem, raw_ready.at(g, 1))
                for j in range(GB):
                    for m in range(halves):
                        last = nc.tensor.matmul(f1_ps[:, j * 128:(j + 1) * 128], y[:, m, j * 128:(j + 1) * 128],
                                                core.w["s_w_out"][:, m, :], start=(m == 0), stop=(m == halves - 1))
                last.then_inc(o_ready.sem, 1)

            def project_conv(g, s):
                project_z(g, s, 0)
                project_z(g, s, 1)

            def project_res(g, s):
                project_z(g, s, 2)
                project_z(g, s, 3)

            pieces = {0: turn, 2: project_conv, 4: project_res, 10: project_bc, 11: project_dt}

            def body(g, s, more):
                for n in range(states):
                    if n < states - 2:
                        spread_b(g, s, n + 2)
                    elif more:
                        spread_b(g + 1, 1 - s, n + 2 - states)
                    if n < states - 1:
                        spread_c(g, s, n + 1)
                    elif more:
                        spread_c(g + 1, 1 - s, 0)
                    if n:
                        sum_state(g, s, n - 1)
                    if more and n in pieces:
                        pieces[n](g + 1, 1 - s)
                    if n == 0 and behind(g, 1):
                        project_out(g - 1, 1 - s, True)
                sum_state(g, s, states - 1)

            def front(g, s):
                pieces_of(pieces)(g, s)
                spread_b(g, s, 0)
                spread_b(g, s, 1)
                spread_c(g, s, 0)

            over_groups(pe, front, body)
            project_out(NG - 1, 1, False)


def phase_cross1(core):
    nc = core.nc
    x = core.x
    heads, dk, banks = 16, 64, 4
    per = heads // banks
    blocks = heads * dk // 128
    half = blocks // 2
    with ExitStack() as ctx:
        def sb(name, shape, dt=F32):
            return ctx.enter_context(nc.sbuf_tensor(name, shape, dt))

        def ps(name, shape, dt=F32):
            return ctx.enter_context(nc.psum_tensor(name, shape, dt))

        signals = []

        def sig(name, per_pass=1):
            signals.append(Signal(ctx.enter_context(nc.semaphore(name)), per_pass))
            return signals[-1]

        ctxT = sb("c_ctxT", [128, 2, S2])
        xs = sb("c_xs", [128, 2, 128])
        xs_bo = sb("c_xs_bo", [128, 2, 128])
        xs_beta = sb("c_xs_beta", [128, 2, 128])
        xT = sb("c_xT", [128, 2, 128])
        q = sb("c_q", [128, 2, blocks, 128])
        k = sb("c_k", [128, 2, blocks, S2])
        v = sb("c_v", [S2, 2, heads * dk])
        p = sb("c_p", [128, 2, heads, S2])
        pT = sb("c_pT", [S2, heads, 128])
        top = sb("c_top", [128, 2, heads])
        norm = sb("c_norm", [128, 2, heads])
        oT = sb("c_oT", [128, blocks, 128])
        inner = sb("c_inner", [128, 128])
        inner_stats = sb("c_inner_stats", [128, 6])
        inner_mv = sb("c_inner_mv", [128, 2])
        spare = sb("c_spare", [128, 1])
        total = sb("c_total", [128, 128])
        stats = sb("c_stats", [128, 2, 6])

        s_ps = ps("c_s_ps", [128, banks, 512])
        turn_ps = ps("c_turn_ps", [128, 2, 512])
        f0_ps = ps("c_f0_ps", [128, 512])
        f1_ps = ps("c_f1_ps", [128, 512])
        y_ps = turn_ps[:, 0, 0:128]
        scores = s_ps[:, :, 0:per * S2].rearrange("p r (j s) -> p r j s", s=S2)

        loaded = sig("c_loaded", 16)
        x_normed = sig("c_x_normed")
        bo_added = sig("c_bo_added")
        x_turned = sig("c_x_turned")
        xT_ready = sig("c_xT_ready")
        qk_ps_ready = sig("c_qk_ps_ready", 4)
        qk_ready = sig("c_qk_ready", 4)
        v_ps_ready = sig("c_v_ps_ready", 2)
        v_ready = sig("c_v_ready", 2)
        scored = sig("c_scored")
        top_ready = sig("c_top_ready")
        lowered = sig("c_lowered")
        exped = sig("c_exped")
        norm_steps = sig("c_norm_steps", 2)
        divided = sig("c_divided")
        p_turned = sig("c_p_turned", banks)
        pT_ready = sig("c_pT_ready", banks)
        mixed = sig("c_mixed", 2)
        oT_ready = sig("c_oT_ready", 2)
        y_ready = sig("c_y_ready")
        inner_steps = sig("c_inner_steps", 4)
        inner_eps = sig("c_inner_eps")
        inner_rstd = sig("c_inner_rstd")
        scaled = sig("c_scaled")
        summed = sig("c_summed")
        left_steps = sig("c_left_steps", 3)

        def head_of(r, j):
            return 8 * (r // 2) + 2 * j + r % 2

        open_signals(nc, signals, [core.landed["c"]])
        block = ctx.enter_context(nc.Block())

        @block.sync
        def _(sp):
            def load(i, s):
                sp.wait_ge(loaded.sem, loaded.at(i, 0))
                if behind(i, 2):
                    sp.wait_ge(v_ps_ready.sem, v_ps_ready.at(i - 1, 0))
                sp.dma_start(ctxT[:, s, :], core.ins["ctxT"][:, ds(i, 1), :].rearrange("p a s -> p (a s)")
                             ).then_inc(loaded.sem, 16)

            load(0, 0)
            with sp.Fori(1, B - 2, 2) as i:
                load(i, 1)
                load(i + 1, 0)
            load(B - 1, 1)

        @block.gpsimd
        def _(pool):
            def inner_root(i, s):
                pool.wait_ge(inner_steps.sem, inner_steps.at(i, 3))
                nc.gpsimd.tensor_tensor(inner_mv[:, 1:2], inner_mv[:, 1:2], core.ln_eps[:, :],
                                        ALU.add).then_inc(inner_eps.sem, 1)
                pool.wait_ge(inner_eps.sem, inner_eps.at(i, 1))
                nc.gpsimd.tensor_tensor(inner_mv[:, 1:2], inner_mv[:, 1:2], core.minus_half[:, 0:1],
                                        ALU.pow).then_inc(inner_rstd.sem, 1)

            def gamma_beta(i, s):
                pool.wait_ge(inner_steps.sem, inner_steps.at(i, 4))
                if behind(i, 1):
                    pool.wait_ge(left_steps.sem, left_steps.at(i - 1, 3))
                nc.gpsimd.tensor_tensor(total[:, :], inner[:, :], core.w["c_gamma"][:, :],
                                        ALU.mult).then_inc(scaled.sem, 1)
                pool.wait_ge(scaled.sem, scaled.at(i, 1))
                nc.gpsimd.tensor_tensor(total[:, :], total[:, :], xs_beta[:, s, :],
                                        ALU.add).then_inc(summed.sem, 1)

            def add_biases(i, s):
                pool.wait_ge(x_normed.sem, x_normed.at(i, 1))
                if behind(i, 2):
                    pool.wait_ge(inner_steps.sem, inner_steps.at(i - 1, 0))
                if behind(i, 2):
                    pool.wait_ge(summed.sem, summed.at(i - 1, 0))
                nc.gpsimd.tensor_tensor(xs_bo[:, s, :], xs[:, s, :], core.w["c_bo"][:, :], ALU.add)
                nc.gpsimd.tensor_tensor(xs_beta[:, s, :], xs[:, s, :], core.w["c_beta"][:, :],
                                        ALU.add).then_inc(bo_added.sem, 1)

            def divide(i, s):
                pool.wait_ge(norm_steps.sem, norm_steps.at(i, 2))
                nc.gpsimd.tensor_tensor(p[:, s, :, :], p[:, s, :, :],
                                        norm[:, s, :].unsqueeze(2).broadcast_to([128, heads, S2]),
                                        ALU.mult).then_inc(divided.sem, 1)

            def step(i, s, stages):
                if "d" in stages:
                    inner_root(i - 1, 1 - s)
                    gamma_beta(i - 1, 1 - s)
                if "b" in stages:
                    add_biases(i + 1, 1 - s)
                    divide(i + 1, 1 - s)

            in_steps(pool, step)

        @block.scalar
        def _(act):
            def turn_x(i, s):
                act.wait_ge(x_turned.sem, x_turned.at(i, 1))
                if behind(i, 2):
                    act.wait_ge(qk_ps_ready.sem, qk_ps_ready.at(i - 1, 0))
                nc.scalar.activation(xT[:, s, :], f0_ps[:, 0:128], ACT.Copy).then_inc(xT_ready.sem, 1)

            def exp(i, s):
                act.wait_ge(lowered.sem, lowered.at(i, 1))
                nc.scalar.activation(p[:, s, :, :], p[:, s, :, :], ACT.Exp, scale=dk ** -0.5).then_inc(exped.sem, 1)

            def copy_p(i, s, r):
                act.wait_ge(p_turned.sem, p_turned.at(i, r + 1))
                if r == 0:
                    if behind(i, 1):
                        act.wait_ge(mixed.sem, mixed.at(i - 1, 2))
                nc.scalar.activation(pT[:, per * r:per * (r + 1), :],
                                     turn_ps[0:S2, r % 2, :].rearrange("p (j t) -> p j t", t=128),
                                     ACT.Copy).then_inc(pT_ready.sem, 1)

            def copy_o(i, s, m):
                act.wait_ge(mixed.sem, mixed.at(i, m + 1))
                if m == 0:
                    if behind(i, 1):
                        act.wait_ge(y_ready.sem, y_ready.at(i - 1, 1))
                nc.scalar.activation(oT[:, half * m:half * (m + 1), :],
                                     (f1_ps, f0_ps)[m][:, :].rearrange("p (b t) -> p b t", t=128),
                                     ACT.Copy).then_inc(oT_ready.sem, 1)

            def step(i, s, stages):
                if "c" in stages:
                    copy_p(i, s, 0)
                if "a" in stages:
                    turn_x(i + 2, s)
                if "c" in stages:
                    copy_p(i, s, 1)
                    copy_p(i, s, 2)
                    copy_p(i, s, 3)
                if "b" in stages:
                    exp(i + 1, 1 - s)
                if "c" in stages:
                    copy_o(i, s, 0)
                    copy_o(i, s, 1)

            in_steps(act, step)

        @block.vector
        def _(dve):
            def normalise(i, s):
                if behind(i, 2):
                    dve.wait_ge(bo_added.sem, bo_added.at(i - 1, 0))
                if behind(i, 2):
                    dve.wait_ge(x_turned.sem, x_turned.at(i - 1, 0))
                nc.vector.tensor_scalar(xs[:, s, :], x[:, i, :], core.mean[:, ds(i, 1)],
                                        core.rstd[:, ds(i, 1)], ALU.subtract,
                                        ALU.mult).then_inc(x_normed.sem, 1)

            def add_qk(i, s, n):
                if n == 0 and behind(i, 2):
                    dve.wait_ge(scored.sem, scored.at(i - 1, 0))
                dst, bias, width = ((q, "c_bq", 128), (k, "c_bk", S2))[n // 2]
                rows = slice(half * (n % 2), half * (n % 2 + 1))
                dve.wait_ge(qk_ps_ready.sem, qk_ps_ready.at(i, n + 1))
                nc.vector.tensor_tensor(
                    dst[:, s, rows, :],
                    (f1_ps, f0_ps)[n % 2][:, 0:half * width].rearrange("p (b t) -> p b t", t=width),
                    core.w[bias][:, rows].unsqueeze(2).broadcast_to([128, half, width]),
                    ALU.add).then_inc(qk_ready.sem, 1)

            def add_v(i, s):
                for n in range(2):
                    cols = slice(512 * n, 512 * (n + 1))
                    dve.wait_ge(v_ps_ready.sem, v_ps_ready.at(i, n + 1))
                    if n == 0:
                        if behind(i, 2):
                            dve.wait_ge(mixed.sem, mixed.at(i - 2, 2))
                    nc.vector.tensor_tensor(v[:, s, cols], (f1_ps, f0_ps)[n][0:S2, :], core.w["c_bv"][0:S2, cols],
                                            ALU.add).then_inc(v_ready.sem, 1)

            def peak(i, s):
                dve.wait_ge(scored.sem, scored.at(i, 1))
                nc.vector.tensor_reduce(top[:, s, :].rearrange("p (r j) -> p r j", r=banks), scores,
                                        AX.X, ALU.max).then_inc(top_ready.sem, 1)

            def lower(i, s):
                dve.wait_ge(top_ready.sem, top_ready.at(i, 1))
                if behind(i, 2):
                    dve.wait_ge(p_turned.sem, p_turned.at(i - 1, 0))
                nc.vector.tensor_tensor(
                    p[:, s, :, :].rearrange("p (r j) s -> p r j s", r=banks), scores,
                    top[:, s, :].rearrange("p (r j) -> p r j", r=banks).unsqueeze(3).broadcast_to(
                        [128, banks, per, S2]), ALU.subtract).then_inc(lowered.sem, 1)

            def sums(i, s):
                dve.wait_ge(exped.sem, exped.at(i, 1))
                nc.vector.tensor_reduce(norm[:, s, :], p[:, s, :, :], AX.X, ALU.add).then_inc(norm_steps.sem, 1)
                dve.wait_ge(norm_steps.sem, norm_steps.at(i, 1))
                nc.vector.reciprocal(norm[:, s, :], norm[:, s, :]).then_inc(norm_steps.sem, 1)

            def inner_sum(i, s):
                dve.wait_ge(y_ready.sem, y_ready.at(i, 1))
                dve.wait_ge(bo_added.sem, bo_added.at(i, 1))
                if behind(i, 1):
                    dve.wait_ge(summed.sem, summed.at(i - 1, 1))
                nc.vector.tensor_tensor(inner[:, :], y_ps, xs_bo[:, s, :],
                                        ALU.add).then_inc(inner_steps.sem, 1)
                dve.wait_ge(inner_steps.sem, inner_steps.at(i, 1))
                nc.vector.bn_stats(inner_stats[:, :], inner[:, :]).then_inc(inner_steps.sem, 1)
                dve.wait_ge(inner_steps.sem, inner_steps.at(i, 2))
                nc.vector.memset(spare[:, :], 0.0)
                nc.vector.bn_aggr(inner_mv[:, :], inner_stats[:, :]).then_inc(inner_steps.sem, 1)

            def inner_norm(i, s):
                dve.wait_ge(inner_rstd.sem, inner_rstd.at(i, 1))
                nc.vector.tensor_scalar(inner[:, :], inner[:, :], inner_mv[:, 0:1], inner_mv[:, 1:2],
                                        ALU.subtract, ALU.mult).then_inc(inner_steps.sem, 1)

            def leave_sum(i, s):
                dve.wait_ge(summed.sem, summed.at(i, 1))
                nc.vector.bn_stats(stats[:, s, :], total[:, :]).then_inc(left_steps.sem, 1)
                nc.vector.tensor_copy(core.x[:, i, :], total[:, :]).then_inc(left_steps.sem, 1)
                dve.wait_ge(left_steps.sem, left_steps.at(i, 2))
                nc.vector.tensor_copy(core.stats[:, i, :], stats[:, s, :]).then_inc(left_steps.sem, 1)

            def step(i, s, stages):
                if "d" in stages:
                    inner_sum(i - 1, 1 - s)
                if "a" in stages:
                    normalise(i + 2, s)
                if "b" in stages:
                    peak(i + 1, 1 - s)
                if "d" in stages:
                    inner_norm(i - 1, 1 - s)
                if "a" in stages:
                    add_qk(i + 2, s, 0)
                if "b" in stages:
                    lower(i + 1, 1 - s)
                if "a" in stages:
                    add_qk(i + 2, s, 1)
                    add_qk(i + 2, s, 2)
                    add_qk(i + 2, s, 3)
                if "b" in stages:
                    sums(i + 1, 1 - s)
                if "d" in stages:
                    leave_sum(i - 1, 1 - s)
                if "a" in stages:
                    add_v(i + 2, s)

            in_steps(dve, step)

        @block.tensor
        def _(pe):
            def turn_x(i, s):
                pe.wait_ge(x_normed.sem, x_normed.at(i, 1))
                if behind(i, 1):
                    pe.wait_ge(v_ready.sem, v_ready.at(i - 1, 2))
                nc.tensor.transpose(f0_ps[:, 0:128], xs[:, s, :], core.ident[:, :]).then_inc(x_turned.sem, 1)

            def project_qk(i, s, n):
                if n == 0:
                    pe.wait_ge(xT_ready.sem, xT_ready.at(i, 1))
                    pe.wait_ge(loaded.sem, loaded.at(i, 16))
                if n >= 2:
                    pe.wait_ge(qk_ready.sem, qk_ready.at(i, n - 1))
                weights, rhs, width = (("c_wq", xT, 128), ("c_wk", ctxT, S2))[n // 2]
                for b in range(half):
                    cols = 128 * (half * (n % 2) + b)
                    last = nc.tensor.matmul((f1_ps, f0_ps)[n % 2][:, width * b:width * (b + 1)],
                                            core.w[weights][:, cols:cols + 128], rhs[:, s, :],
                                            start=True, stop=True)
                last.then_inc(qk_ps_ready.sem, 1)

            def project_v(i, s):
                for n in range(2):
                    pe.wait_ge(qk_ready.sem, qk_ready.at(i, 3 + n))
                    if behind(i, 2):
                        pe.wait_ge(oT_ready.sem, oT_ready.at(i - 2, 1 + n))
                    nc.tensor.matmul((f1_ps, f0_ps)[n][0:S2, :], ctxT[:, s, :],
                                     core.w["c_wv"][:, 512 * n:512 * (n + 1)],
                                     start=True, stop=True).then_inc(v_ps_ready.sem, 1)

            def score(i, s):
                pe.wait_ge(qk_ready.sem, qk_ready.at(i, 4))
                if behind(i, 1):
                    pe.wait_ge(lowered.sem, lowered.at(i - 1, 1))
                for j in range(per):
                    for r in range(banks):
                        h = head_of(r, j)
                        rows = slice(dk * (h % 2), dk * (h % 2 + 1))
                        last = nc.tensor.matmul(s_ps[:, r, S2 * j:S2 * (j + 1)], q[rows, s, h // 2, :],
                                                k[rows, s, h // 2, :], start=True, stop=True)
                last.then_inc(scored.sem, 1)

            def turn_p(i, s, r):
                if r == 0:
                    pe.wait_ge(divided.sem, divided.at(i, 1))
                    if behind(i, 1):
                        pe.wait_ge(inner_steps.sem, inner_steps.at(i - 1, 1))
                elif r == 1:
                    if behind(i, 1):
                        pe.wait_ge(pT_ready.sem, pT_ready.at(i - 1, 4))
                else:
                    pe.wait_ge(pT_ready.sem, pT_ready.at(i, r - 1))
                for j in range(per):
                    last = nc.tensor.transpose(turn_ps[0:S2, r % 2, j * 128:(j + 1) * 128],
                                               p[:, s, per * r + j, :], core.ident[:, :])
                last.then_inc(p_turned.sem, 1)

            def mix(i, s, more):
                pe.wait_ge(v_ready.sem, v_ready.at(i, 2))
                if behind(i, 1):
                    pe.wait_ge(oT_ready.sem, oT_ready.at(i - 1, 2))
                for m in range(2):
                    if more:
                        pe.wait_ge(qk_ready.sem, qk_ready.at(i + 2, 3 + m))
                    pe.wait_ge(pT_ready.sem, pT_ready.at(i, 2 * m + 2))
                    for j in range(per):
                        for r in (2 * m, 2 * m + 1):
                            h = head_of(r, j)
                            rows = slice(dk * (h % 2), dk * (h % 2 + 1))
                            last = nc.tensor.matmul((f1_ps, f0_ps)[m][rows, 128 * j:128 * (j + 1)],
                                                    v[:, s, dk * h:dk * (h + 1)], pT[:, per * r + j, :],
                                                    start=True, stop=True)
                    last.then_inc(mixed.sem, 1)

            def project_out(i, s):
                pe.wait_ge(oT_ready.sem, oT_ready.at(i, 2))
                for b in range(blocks):
                    last = nc.tensor.matmul(y_ps, oT[:, b, :], core.w["c_wo"][:, b, :],
                                            start=(b == 0), stop=(b == blocks - 1))
                last.then_inc(y_ready.sem, 1)

            def step(i, s, stages):
                if "b" in stages:
                    score(i + 1, 1 - s)
                if "c" in stages:
                    turn_p(i, s, 0)
                if "a" in stages:
                    turn_x(i + 2, s)
                if "c" in stages:
                    turn_p(i, s, 1)
                if "a" in stages:
                    project_qk(i + 2, s, 0)
                if "c" in stages:
                    turn_p(i, s, 2)
                if "a" in stages:
                    project_qk(i + 2, s, 1)
                if "c" in stages:
                    turn_p(i, s, 3)
                if "a" in stages:
                    project_qk(i + 2, s, 2)
                    project_qk(i + 2, s, 3)
                if "c" in stages:
                    mix(i, s, "a" in stages)
                if "a" in stages:
                    project_v(i + 2, s)
                if "c" in stages:
                    project_out(i, s)

            in_steps(pe, step)


def phase_quantised(core):
    nc = core.nc
    x = core.x
    inner_blocks = 4
    inner = inner_blocks * 128
    to_whole = 1.5 * 2.0 ** 23
    names = ("q_wg", "q_wu", "q_wd")
    with ExitStack() as ctx:
        def sb(name, shape, dt=F32):
            return ctx.enter_context(nc.sbuf_tensor(name, shape, dt))

        def ps(name, shape, dt=F32):
            return ctx.enter_context(nc.psum_tensor(name, shape, dt))

        signals = []

        def sig(name, per_pass=1):
            signals.append(Signal(ctx.enter_context(nc.semaphore(name)), per_pass))
            return signals[-1]

        ones = sb("q_ones", [128, 128])
        ident16 = sb("q_ident16", [128, 128], BF16)
        w_sum = sb("q_w_sum", [128, 3])
        w_mean = sb("q_w_mean", [128, 3])
        w_scale = sb("q_w_scale", [128, 3])
        w_scaled = sb("q_w_scaled", [128, 3, inner])
        ternary = sb("q_ternary", [128, 3, inner], BF16)
        xs = sb("q_xs", [128, 2, 128])
        kept = sb("q_kept", [128, 2, 128])
        x_top = sb("q_x_top", [128, 2])
        x_scale = sb("q_x_scale", [128, 2])
        x_back = sb("q_x_back", [128, 2, 2])
        x_scaled = sb("q_x_scaled", [128, 2, 128])
        xq = sb("q_xq", [128, 2, 128], BF16)
        xqT = sb("q_xqT", [128, 2, 128], BF16)
        silu = sb("q_silu", [128, 2, inner])
        h = sb("q_h", [128, 2, inner])
        h_top = sb("q_h_top", [128, 2])
        h_scale = sb("q_h_scale", [128, 2])
        h_back = sb("q_h_back", [128, 2])
        hq = sb("q_hq", [128, 2, inner], BF16)
        hqT = sb("q_hqT", [128, 2, inner], BF16)
        total = sb("q_total", [128, 2, 128])
        stats = sb("q_stats", [128, 2, 6])

        xT_ps = ps("q_xT_ps", [128, 128], BF16)
        g_ps = ps("q_g_ps", [128, 2, inner])
        u_ps = ps("q_u_ps", [128, 2, inner])
        hT_ps = ps("q_hT_ps", [128, inner], BF16)
        o_ps = ps("q_o_ps", [128, 128])
        sum_ps = ps("q_sum_ps", [128, 3])

        ones_ready = sig("q_ones_ready")
        prep_steps = sig("q_prep_steps", 6)
        sum_ready = sig("q_sum_ready")
        x_steps = sig("q_x_steps", 7)
        kept_ready = sig("q_kept_ready")
        x_turned = sig("q_x_turned")
        xT_ready = sig("q_xT_ready")
        gu_ready = sig("q_gu_ready")
        silu_ready = sig("q_silu_ready")
        h_steps = sig("q_h_steps", 7)
        h_turned = sig("q_h_turned")
        hT_ready = sig("q_hT_ready")
        o_ready = sig("q_o_ready")
        left_steps = sig("q_left_steps", 3)

        open_signals(nc, signals, [core.landed["q"]])
        block = ctx.enter_context(nc.Block())

        @block.gpsimd
        def _(pool):
            nc.gpsimd.memset(ones[:, :], 1.0).then_inc(ones_ready.sem, 1)
            pool.wait_ge(ones_ready.sem, ones_ready.at(0, 1))

            def keep_x(i, s):
                pool.wait_ge(x_steps.sem, x_steps.at(i, 1))
                if behind(i, 2):
                    pool.wait_ge(left_steps.sem, left_steps.at(i - 2, 1))
                nc.gpsimd.tensor_tensor(kept[:, s, :], xs[:, s, :], ones[:, :], ALU.mult).then_inc(kept_ready.sem, 1)

            def step(i, s, stages):
                if "a" in stages:
                    keep_x(i + 2, s)

            in_steps(pool, step)

        @block.scalar
        def _(act):
            def copy_x(i, s):
                act.wait_ge(x_turned.sem, x_turned.at(i, 1))
                if behind(i, 2):
                    act.wait_ge(gu_ready.sem, gu_ready.at(i - 1, 0))
                nc.scalar.activation(xqT[:, s, :], xT_ps[:, :], ACT.Copy).then_inc(xT_ready.sem, 1)

            def gate(i, s):
                act.wait_ge(gu_ready.sem, gu_ready.at(i, 1))
                if behind(i, 2):
                    act.wait_ge(h_steps.sem, h_steps.at(i - 1, 0))
                nc.scalar.activation(silu[:, s, :], g_ps[:, s, :], ACT.Silu,
                                     scale=x_back[:, s, 0:1]).then_inc(silu_ready.sem, 1)

            def copy_h(i, s):
                act.wait_ge(h_turned.sem, h_turned.at(i, 1))
                if behind(i, 2):
                    act.wait_ge(o_ready.sem, o_ready.at(i - 1, 0))
                nc.scalar.activation(hqT[:, s, :], hT_ps[:, :], ACT.Copy).then_inc(hT_ready.sem, 1)

            def step(i, s, stages):
                if "c" in stages:
                    copy_h(i, s)
                if "a" in stages:
                    copy_x(i + 2, s)
                    gate(i + 2, s)

            in_steps(act, step)

        @block.vector
        def _(dve):
            for n, name in enumerate(names):
                last = nc.vector.tensor_reduce(w_sum[:, n:n + 1], core.w[name][:, :], AX.X, ALU.add,
                                               apply_absolute_value=True)
            last.then_inc(prep_steps.sem, 1)
            nc.vector.tensor_copy(ident16[:, :], core.ident[:, :])
            dve.wait_ge(sum_ready.sem, sum_ready.at(0, 1))
            nc.vector.tensor_scalar(w_mean[:, :], sum_ps[:, :], 1.0 / (D * inner), 1e-5, ALU.mult,
                                    ALU.max).then_inc(prep_steps.sem, 1)
            dve.wait_ge(prep_steps.sem, prep_steps.at(0, 2))
            nc.vector.reciprocal(w_scale[:, :], w_mean[:, :]).then_inc(prep_steps.sem, 1)
            dve.wait_ge(prep_steps.sem, prep_steps.at(0, 3))
            for n, name in enumerate(names):
                last = nc.vector.tensor_scalar(w_scaled[:, n, :], core.w[name][:, :], w_scale[:, n:n + 1], to_whole,
                                               ALU.mult, ALU.add)
            last.then_inc(prep_steps.sem, 1)
            dve.wait_ge(prep_steps.sem, prep_steps.at(0, 4))
            nc.vector.tensor_scalar(w_scaled[:, :, :], w_scaled[:, :, :], to_whole, 1.0, ALU.subtract,
                                    ALU.min).then_inc(prep_steps.sem, 1)
            dve.wait_ge(prep_steps.sem, prep_steps.at(0, 5))
            nc.vector.tensor_scalar(ternary[:, :, :], w_scaled[:, :, :], -1.0, None,
                                    ALU.max).then_inc(prep_steps.sem, 1)

            def x_norm(i, s):
                if behind(i, 2):
                    dve.wait_ge(kept_ready.sem, kept_ready.at(i - 1, 0))
                nc.vector.tensor_scalar(xs[:, s, :], x[:, i, :], core.mean[:, ds(i, 1)],
                                        core.rstd[:, ds(i, 1)], ALU.subtract, ALU.mult).then_inc(x_steps.sem, 1)

            def x_peak(i, s):
                dve.wait_ge(x_steps.sem, x_steps.at(i, 1))
                nc.vector.tensor_reduce(x_top[:, s:s + 1], xs[:, s, :], AX.X, ALU.max,
                                        apply_absolute_value=True).then_inc(x_steps.sem, 1)

            def x_unit(i, s):
                dve.wait_ge(x_steps.sem, x_steps.at(i, 2))
                nc.vector.tensor_scalar(x_top[:, s:s + 1], x_top[:, s:s + 1], 1e-5, 1.0 / 127.0, ALU.max,
                                        ALU.mult).then_inc(x_steps.sem, 1)

            def x_scales(i, s):
                dve.wait_ge(x_steps.sem, x_steps.at(i, 3))
                nc.vector.reciprocal(x_scale[:, s:s + 1], x_top[:, s:s + 1]).then_inc(x_steps.sem, 1)
                if behind(i, 2):
                    dve.wait_ge(silu_ready.sem, silu_ready.at(i - 1, 0))
                nc.vector.tensor_tensor(x_back[:, s, :], w_mean[:, 0:2],
                                        x_top[:, s:s + 1].broadcast_to([128, 2]), ALU.mult).then_inc(x_steps.sem, 1)

            def x_rescale(i, s):
                dve.wait_ge(x_steps.sem, x_steps.at(i, 5))
                nc.vector.tensor_scalar(x_scaled[:, s, :], xs[:, s, :], x_scale[:, s:s + 1], to_whole,
                                        ALU.mult, ALU.add).then_inc(x_steps.sem, 1)

            def x_whole(i, s):
                dve.wait_ge(x_steps.sem, x_steps.at(i, 6))
                if behind(i, 2):
                    dve.wait_ge(x_turned.sem, x_turned.at(i - 1, 0))
                nc.vector.tensor_scalar(xq[:, s, :], x_scaled[:, s, :], to_whole, 127.0, ALU.subtract,
                                        ALU.min).then_inc(x_steps.sem, 1)

            def h_product(i, s):
                dve.wait_ge(silu_ready.sem, silu_ready.at(i, 1))
                nc.vector.scalar_tensor_tensor(h[:, s, :], u_ps[:, s, :], x_back[:, s, 1:2], silu[:, s, :],
                                               ALU.mult, ALU.mult).then_inc(h_steps.sem, 1)

            def h_peak(i, s):
                dve.wait_ge(h_steps.sem, h_steps.at(i, 1))
                nc.vector.tensor_reduce(h_top[:, s:s + 1], h[:, s, :], AX.X, ALU.max,
                                        apply_absolute_value=True).then_inc(h_steps.sem, 1)

            def h_unit(i, s):
                dve.wait_ge(h_steps.sem, h_steps.at(i, 2))
                nc.vector.tensor_scalar(h_top[:, s:s + 1], h_top[:, s:s + 1], 1e-5, 1.0 / 127.0, ALU.max,
                                        ALU.mult).then_inc(h_steps.sem, 1)

            def h_scales(i, s):
                dve.wait_ge(h_steps.sem, h_steps.at(i, 3))
                nc.vector.reciprocal(h_scale[:, s:s + 1], h_top[:, s:s + 1]).then_inc(h_steps.sem, 1)
                if behind(i, 2):
                    dve.wait_ge(left_steps.sem, left_steps.at(i - 1, 0))
                nc.vector.tensor_tensor(h_back[:, s:s + 1], w_mean[:, 2:3], h_top[:, s:s + 1],
                                        ALU.mult).then_inc(h_steps.sem, 1)

            def h_rescale(i, s):
                dve.wait_ge(h_steps.sem, h_steps.at(i, 5))
                nc.vector.tensor_scalar(h[:, s, :], h[:, s, :], h_scale[:, s:s + 1], to_whole,
                                        ALU.mult, ALU.add).then_inc(h_steps.sem, 1)

            def h_whole(i, s):
                dve.wait_ge(h_steps.sem, h_steps.at(i, 6))
                if behind(i, 2):
                    dve.wait_ge(h_turned.sem, h_turned.at(i - 1, 0))
                nc.vector.tensor_scalar(hq[:, s, :], h[:, s, :], to_whole, 127.0, ALU.subtract,
                                        ALU.min).then_inc(h_steps.sem, 1)

            def add_up(i, s):
                dve.wait_ge(o_ready.sem, o_ready.at(i, 1))
                dve.wait_ge(kept_ready.sem, kept_ready.at(i, 1))
                nc.vector.scalar_tensor_tensor(total[:, s, :], o_ps[:, :], h_back[:, s:s + 1], kept[:, s, :],
                                               ALU.mult, ALU.add).then_inc(left_steps.sem, 1)

            def step(i, s, stages):
                if "a" in stages:
                    x_norm(i + 2, s)
                    x_peak(i + 2, s)
                if "b" in stages:
                    h_product(i + 1, 1 - s)
                if "a" in stages:
                    x_unit(i + 2, s)
                if "b" in stages:
                    h_peak(i + 1, 1 - s)
                if "a" in stages:
                    x_scales(i + 2, s)
                if "b" in stages:
                    h_unit(i + 1, 1 - s)
                if "a" in stages:
                    x_rescale(i + 2, s)
                if "b" in stages:
                    h_scales(i + 1, 1 - s)
                if "a" in stages:
                    x_whole(i + 2, s)
                if "c" in stages:
                    add_up(i, s)
                if "b" in stages:
                    h_rescale(i + 1, 1 - s)
                    h_whole(i + 1, 1 - s)
                if "c" in stages:
                    leave_one(dve, nc, core, i, left_steps, total[:, s, :], stats[:, s, :])

            in_steps(dve, step)

        @block.tensor
        def _(pe):
            pe.wait_ge(ones_ready.sem, ones_ready.at(0, 1))
            pe.wait_ge(prep_steps.sem, prep_steps.at(0, 1))
            nc.tensor.matmul(sum_ps[:, :], ones[:, :], w_sum[:, :], start=True, stop=True).then_inc(sum_ready.sem, 1)
            pe.wait_ge(prep_steps.sem, prep_steps.at(0, 6))

            def turn_x(i, s):
                pe.wait_ge(x_steps.sem, x_steps.at(i, 7))
                if behind(i, 1):
                    pe.wait_ge(xT_ready.sem, xT_ready.at(i - 1, 1))
                nc.tensor.transpose(xT_ps[:, :], xq[:, s, :], ident16[:, :]).then_inc(x_turned.sem, 1)

            def up(i, s):
                pe.wait_ge(xT_ready.sem, xT_ready.at(i, 1))
                if behind(i, 2):
                    pe.wait_ge(silu_ready.sem, silu_ready.at(i - 2, 1))
                    pe.wait_ge(h_steps.sem, h_steps.at(i - 2, 1))
                nc.tensor.matmul(g_ps[:, s, :], xqT[:, s, :], ternary[:, 0, :], start=True, stop=True)
                nc.tensor.matmul(u_ps[:, s, :], xqT[:, s, :], ternary[:, 1, :],
                                 start=True, stop=True).then_inc(gu_ready.sem, 1)

            def turn_h(i, s):
                pe.wait_ge(h_steps.sem, h_steps.at(i, 7))
                if behind(i, 1):
                    pe.wait_ge(hT_ready.sem, hT_ready.at(i - 1, 1))
                for b in range(inner_blocks):
                    cols = slice(128 * b, 128 * (b + 1))
                    last = nc.tensor.transpose(hT_ps[:, cols], hq[:, s, cols], ident16[:, :])
                last.then_inc(h_turned.sem, 1)

            def down(i, s):
                pe.wait_ge(hT_ready.sem, hT_ready.at(i, 1))
                if behind(i, 1):
                    pe.wait_ge(left_steps.sem, left_steps.at(i - 1, 1))
                for b in range(inner_blocks):
                    cols = slice(128 * b, 128 * (b + 1))
                    last = nc.tensor.matmul(o_ps[:, :], hqT[:, s, cols], ternary[:, 2, cols],
                                            start=(b == 0), stop=(b == inner_blocks - 1))
                last.then_inc(o_ready.sem, 1)

            def step(i, s, stages):
                if "c" in stages:
                    turn_h(i, s)
                    down(i, s)
                if "a" in stages:
                    turn_x(i + 2, s)
                    up(i + 2, s)

            in_steps(pe, step)


def phase_out(core):
    nc = core.nc
    x = core.x
    with ExitStack() as ctx:
        normed = ctx.enter_context(nc.semaphore("z_normed"))
        stored = ctx.enter_context(nc.semaphore("z_stored"))
        block = ctx.enter_context(nc.Block())

        @block.vector
        def _(dve):
            with dve.Fori(0, NG) as g:
                for j in range(GB):
                    last = nc.vector.tensor_scalar(x[:, g * GB + j, :], x[:, g * GB + j, :],
                                                   core.mean[:, ds(g * GB + j, 1)],
                                                   core.rstd[:, ds(g * GB + j, 1)],
                                                   ALU.subtract, ALU.mult)
                last.then_inc(normed, 1)

        @block.sync
        def _(sp):
            with sp.Fori(0, NG) as g:
                sp.wait_ge(normed, g + 1)
                sp.dma_start(core.out[ds(g * GB, GB), :, :].rearrange("b t d -> t b d"),
                             x[:, ds(g * GB, GB), :]).then_inc(stored, 16)
            sp.wait_ge(stored, 16 * NG)


def build(nc, ins, out):
    with ExitStack() as ctx:
        core = Core(nc, ctx, ins, out)
        core.x = core.sb("x", [128, B, 128])
        core.stats = core.sb("stats", [128, B, 6])
        core.mean = core.sb("mean", [128, B])
        core.rstd = core.sb("rstd", [128, B])
        core.minus_half = core.sb("minus_half", [128, B])
        core.euler = core.sb("euler", [128, 32])
        core.ln_eps = core.sb("ln_eps", [128, 1])
        core.neg_rate = core.sb("neg_rate", [128, 2, 16])
        core.rms_eps = core.sb("rms_eps", [128, 2 * GB])
        core.w = {}
        core.landed = {phase: Landed(ctx.enter_context(nc.semaphore(f"weights_{phase}")), len(names))
                       for phase, names in WEIGHTS.items()}

        def place(phases, within):
            for phase in phases:
                for name in WEIGHTS[phase]:
                    core.w[name] = within.enter_context(nc.sbuf_tensor(f"w_{name}", list(ins[name].shape), F32))

        place("scq", ctx)
        with ExitStack() as layer0:
            place("abm", layer0)
            core.ident, core.upper = core.w["ident"], core.w["upper"]
            setup(core)
            run_phase(core, "a", phase_aft)
            run_phase(core, "b", phase_cross0)
            run_phase(core, "m", phase_moe)
        run_phase(core, "s", phase_scan)
        run_phase(core, "c", phase_cross1)
        run_phase(core, "q", phase_quantised)
        phase_out(core)


def run_phase(core, name, phase):
    phase(core)
    finish_statistics(core, name)


class Landed:

    def __init__(self, sem, count):
        self.sem = sem
        self.value = 16 * count


WEIGHTS = {
    "a": ["a_wqkvT", "a_wuvT", "a_woutT", "upper"],
    "b": ["b_wq", "b_wk", "b_wv", "b_wo", "b_bq", "b_bk", "b_bv", "b_bo", "head_mask"],
    "m": ["m_router", "m_bias", "m_earlier", "m_w1", "m_w3", "m_w2"],
    "s": ["ident", "s_bo", "s_b_in", "s_dt_bias", "s_A_log", "s_pick", "s_conv_w", "s_conv_b", "s_D", "s_w_in",
          "s_x_proj", "s_dt_proj", "s_w_out"],
    "c": ["c_bo", "c_beta", "c_gamma", "c_bq", "c_bk", "c_bv", "c_wq", "c_wk", "c_wv", "c_wo"],
    "q": ["q_wg", "q_wu", "q_wd"],
}


def layout(inputs):
    def c(a):
        return np.ascontiguousarray(a)

    i = {k: np.asarray(v) for k, v in inputs.items()}

    def up(name):
        both = np.concatenate([i["L0_ffn_s" + name], i["L0_ffn_" + name]])
        return c(both.reshape(20, 128, 128).transpose(2, 0, 1))

    head_mask = np.tile(np.kron(np.eye(4), np.ones((8, 1))) * 8 ** -0.5, (4, 1)).astype(np.float32)
    return {
        "x": c(i["x"]),
        "ident": np.eye(128, dtype=np.float32),
        "upper": np.triu(np.ones((128, 128), np.float32)),
        "a_wqkvT": c(i["L0_attn_w_qkv"].T),
        "a_wuvT": c(i["L0_attn_w_swiglu"].T),
        "a_woutT": c(i["L0_attn_w_out"].T),
        "ctxT": c(i["ctx_1024"].transpose(2, 0, 1)),
        "fside": c(i["fside_BxSxS2_0"]),
        "mask": c(i["mask_BxSxS2_ff0"]),
        "b_wq": c(i["L0_xattn_Wq"]),
        "b_wk": c(i["L0_xattn_Wk"]),
        "b_wv": c(i["L0_xattn_Wv"]),
        "b_wo": c(i["L0_xattn_Wo"]),
        "b_bq": c(i["L0_xattn_bq"].reshape(128, 1)),
        "b_bk": c(i["L0_xattn_bk"].reshape(128, 1)),
        "b_bv": c(np.tile(i["L0_xattn_bv"], (128, 1))),
        "b_bo": c(np.tile(i["L0_xattn_bo"], (128, 1))),
        "head_mask": head_mask,
        "s_bo": c(np.tile(i["L1_attn_b_out"], (128, 1))),
        "s_b_in": c(i["L1_attn_b_in"].reshape(4, 128).T),
        "s_dt_bias": c(i["L1_attn_dt_bias"].reshape(2, 128).T),
        "s_A_log": c(i["L1_attn_A_log"].reshape(2, 128, 16).transpose(1, 0, 2)),
        "s_pick": c(np.tile(np.eye(32, dtype=np.float32), (3, 1))),
        "s_conv_w": c(i["L1_attn_conv_w"].reshape(2, 128, 4).transpose(1, 0, 2)),
        "s_conv_b": c(i["L1_attn_conv_b"].reshape(2, 128).T),
        "s_D": c(i["L1_attn_D_param"].reshape(2, 128).T),
        "s_w_in": c(i["L1_attn_W_in"]),
        "s_x_proj": c(i["L1_attn_x_proj_w"].reshape(2, 128, 48).transpose(1, 0, 2)),
        "s_dt_proj": c(i["L1_attn_dt_proj_w"]),
        "s_w_out": c(i["L1_attn_W_out"].reshape(2, 128, 128).transpose(1, 0, 2)),
        "c_bo": c(np.tile(i["L1_xattn_bo"], (128, 1))),
        "c_beta": c(np.tile(i["L1_xattn_ln_beta"], (128, 1))),
        "c_gamma": c(np.tile(i["L1_xattn_ln_gamma"], (128, 1))),
        "c_bq": c(i["L1_xattn_bq"].reshape(8, 128).T),
        "c_bk": c(i["L1_xattn_bk"].reshape(8, 128).T),
        "c_bv": c(np.tile(i["L1_xattn_bv"], (128, 1))),
        "c_wq": c(i["L1_xattn_Wq"]),
        "c_wk": c(i["L1_xattn_Wk"]),
        "c_wv": c(i["L1_xattn_Wv"]),
        "c_wo": c(i["L1_xattn_Wo"].reshape(8, 128, 128).transpose(1, 0, 2)),
        "q_wg": c(i["L1_ffn_w_gate"].T),
        "q_wu": c(i["L1_ffn_w_up"].T),
        "q_wd": c(i["L1_ffn_w_down"].reshape(128, 4, 128).transpose(2, 1, 0).reshape(128, 512)),
        "m_router": c(i["L0_ffn_router_w"].T),
        "m_bias": c(np.tile(i["L0_ffn_expert_bias"], (128, 1))),
        "m_earlier": c(np.tile(np.tril(np.ones((8, 8), np.float32), -1).reshape(1, 64), (128, 1))),
        "m_w1": up("w1"),
        "m_w3": up("w3"),
        "m_w2": c(np.concatenate([i["L0_ffn_sw2"], i["L0_ffn_w2"]]).transpose(0, 2, 1).reshape(20, 128, 128)
                  .transpose(1, 0, 2)),
    }


def kernel(**inputs):
    import concourse.bacc as _bacc
    from concourse.bass_utils import run_bass_kernel_spmd as _run

    nc = _bacc.Bacc("TRN2", target_bir_lowering=False, num_devices=1)
    arrays = layout(inputs)
    ins = {name: nc.dram_tensor(f"in_{name}_dram", a.shape, mybir.dt.from_np(a.dtype), kind="ExternalInput").ap()
           for name, a in arrays.items()}
    out = nc.dram_tensor("out_0_dram", (B, T, D), F32, kind="ExternalOutput").ap()
    build(nc, ins, out)
    r = _run(nc, [{f"in_{name}_dram": a for name, a in arrays.items()}], core_ids=[0])
    return r.results[0]["out_0_dram"]
```
